# Optimizing a Trainium2 kernel written in Bass

```python
import numpy as np
import jax
import jax.numpy as jnp

def _softmax(x, axis=-1):
    return jax.nn.softmax(x, axis=axis)

def _gelu(x):
    return jax.nn.gelu(x, approximate=True)

def _silu(x):
    return jax.nn.silu(x)

def _sigmoid(x):
    return jax.nn.sigmoid(x)

def _layernorm(x, axis=-1, eps=1e-05):
    m = jnp.mean(x, axis=axis, keepdims=True)
    v = jnp.var(x, axis=axis, keepdims=True)
    return (x - m) / jnp.sqrt(v + eps)

def _scatter_add(tgt, idx, src, axis=0):
    return tgt.at[idx].add(src)

def _segment_sum(src, seg, n):
    return jax.ops.segment_sum(src, seg, n)
kernel_name = 'mk_gnn_ffn_d1_gnn_r8_5feb72'

def setup_inputs(seed: int=0):
    np.random.seed(seed)
    _w = jnp.asarray

    def _rec_inputs():
        import jax
        import jax.numpy as jnp
        _gk = jax.random.key(seed)
        x = -0.0005963 + 1.001 * jax.random.normal(jax.random.fold_in(_gk, 1), (384, 1024), jnp.float32)
        src = jax.random.randint(jax.random.fold_in(_gk, 2), (6144,), 0, 384, jnp.int32)
        dst = jnp.minimum((384 * jax.random.uniform(jax.random.fold_in(_gk, 3), (6144,)) ** 2.0).astype(jnp.int32), 3071)
        _o = jnp.argsort(dst, stable=True)
        src = src[_o]
        dst = dst[_o]
        edge_type_5 = jax.random.randint(jax.random.fold_in(_gk, 12), (6144,), 0, 5, jnp.int32)
        return (x, src, dst, edge_type_5)
    x, src, dst, edge_type_5 = _rec_inputs()

    def _L0_gnn_setup():
        import jax, jax.numpy as jnp
        import numpy as np
        N = 384
        E = 12288
        IN_F = 1024
        OUT_F = 1024
        H = 16
        D = OUT_F // H
        NUM_ETYPES = 4

        def _build_mask(edge_index, edge_type, edge_type_weights, dtype):
            src, dst = (edge_index[0], edge_index[1])
            w = jax.nn.softplus(edge_type_weights)
            mask = jnp.full((N, N), -jnp.inf, dtype=dtype)
            mask = mask.at[src, dst].set(w[edge_type - 1])
            diag = jnp.diagonal(mask)
            idx = jnp.arange(N)
            mask = mask.at[idx, idx].set(jnp.where(jnp.isneginf(diag), w[3], diag))
            return mask
        key = jax.random.key(seed)
        ks = jax.random.split(key, 20)
        p = lambda k, shape: jax.random.normal(k, shape, dtype=jnp.float32) * 0.02
        return {'x': jax.random.normal(ks[0], (N, IN_F), dtype=jnp.float32), 'edge_index': jax.random.randint(ks[1], (2, E), 0, N), 'edge_type': jax.random.randint(ks[2], (E,), 1, NUM_ETYPES + 1), 'edge_type_weights': jnp.ones((NUM_ETYPES,), jnp.float32) + 0.1 * jax.random.normal(ks[3], (NUM_ETYPES,), dtype=jnp.float32), 'wq': p(ks[4], (OUT_F, IN_F)), 'bq': p(ks[5], (OUT_F,)), 'wk': p(ks[6], (OUT_F, IN_F)), 'bk': p(ks[7], (OUT_F,)), 'wv': p(ks[8], (OUT_F, IN_F)), 'bv': p(ks[9], (OUT_F,)), 'wiq': p(ks[10], (OUT_F, OUT_F)), 'biq': p(ks[11], (OUT_F,)), 'wik': p(ks[12], (OUT_F, OUT_F)), 'bik': p(ks[13], (OUT_F,)), 'wiv': p(ks[14], (OUT_F, OUT_F)), 'biv': p(ks[15], (OUT_F,)), 'wo': p(ks[16], (OUT_F, OUT_F)), 'bo': p(ks[17], (OUT_F,))}
    _L0_gnn_all = _L0_gnn_setup()
    _L0_gnn_in = {k: v for k, v in _L0_gnn_all.items() if k in ('edge_type_weights', 'wq', 'bq', 'wk', 'bk', 'wv', 'bv', 'wiq', 'biq', 'wik', 'bik', 'wiv', 'biv', 'wo', 'bo')}
    del _L0_gnn_all

    def _L0_ffn_setup():
        import jax, jax.numpy as jnp
        import numpy as np
        E = 16
        K = 4
        NG = 4
        TG = 2
        SCALE = 2.5
        NORM_TOPK = True
        H = 1024
        I = 512
        SH_I = I * 2
        B, S = (2, 256)
        key = jax.random.key(seed)
        ks = jax.random.split(key, 9)

        def w(k, shape, fan_in):
            return jax.random.normal(k, shape, jnp.float32) * (1.0 / np.sqrt(fan_in))
        return {'hidden_states': jax.random.normal(ks[0], (B, S, H), jnp.float32), 'gate_w': w(ks[1], (E, H), H), 'gate_bias': jnp.zeros((E,), jnp.float32), 'Wg': w(ks[2], (E, I, H), H), 'Wu': w(ks[3], (E, I, H), H), 'Wd': w(ks[4], (E, H, I), I), 'Ws_g': w(ks[5], (SH_I, H), H), 'Ws_u': w(ks[6], (SH_I, H), H), 'Ws_d': w(ks[7], (H, SH_I), SH_I)}
    _L0_ffn_all = _L0_ffn_setup()
    _L0_ffn_in = {k: v for k, v in _L0_ffn_all.items() if k in ('gate_w', 'gate_bias', 'Wg', 'Wu', 'Wd', 'Ws_g', 'Ws_u', 'Ws_d')}
    del _L0_ffn_all
    return {'x': x, 'src': src, 'dst': dst, 'edge_type_5': edge_type_5, 'L0_gnn_edge_type_weights': _L0_gnn_in['edge_type_weights'], 'L0_gnn_wq': _L0_gnn_in['wq'], 'L0_gnn_bq': _L0_gnn_in['bq'], 'L0_gnn_wk': _L0_gnn_in['wk'], 'L0_gnn_bk': _L0_gnn_in['bk'], 'L0_gnn_wv': _L0_gnn_in['wv'], 'L0_gnn_bv': _L0_gnn_in['bv'], 'L0_gnn_wiq': _L0_gnn_in['wiq'], 'L0_gnn_biq': _L0_gnn_in['biq'], 'L0_gnn_wik': _L0_gnn_in['wik'], 'L0_gnn_bik': _L0_gnn_in['bik'], 'L0_gnn_wiv': _L0_gnn_in['wiv'], 'L0_gnn_biv': _L0_gnn_in['biv'], 'L0_gnn_wo': _L0_gnn_in['wo'], 'L0_gnn_bo': _L0_gnn_in['bo'], 'L0_ffn_gate_w': _L0_ffn_in['gate_w'], 'L0_ffn_gate_bias': _L0_ffn_in['gate_bias'], 'L0_ffn_Wg': _L0_ffn_in['Wg'], 'L0_ffn_Wu': _L0_ffn_in['Wu'], 'L0_ffn_Wd': _L0_ffn_in['Wd'], 'L0_ffn_Ws_g': _L0_ffn_in['Ws_g'], 'L0_ffn_Ws_u': _L0_ffn_in['Ws_u'], 'L0_ffn_Ws_d': _L0_ffn_in['Ws_d']}

def reference(x, src, dst, edge_type_5, L0_gnn_edge_type_weights, L0_gnn_wq, L0_gnn_bq, L0_gnn_wk, L0_gnn_bk, L0_gnn_wv, L0_gnn_bv, L0_gnn_wiq, L0_gnn_biq, L0_gnn_wik, L0_gnn_bik, L0_gnn_wiv, L0_gnn_biv, L0_gnn_wo, L0_gnn_bo, L0_ffn_gate_w, L0_ffn_gate_bias, L0_ffn_Wg, L0_ffn_Wu, L0_ffn_Wd, L0_ffn_Ws_g, L0_ffn_Ws_u, L0_ffn_Ws_d):
    import jax
    import jax.numpy as jnp

    def _L0_gnn_ref(x, edge_index, edge_type, edge_type_weights, wq, bq, wk, bk, wv, bv, wiq, biq, wik, bik, wiv, biv, wo, bo):
        import jax, jax.numpy as jnp
        import numpy as np
        N = 384
        E = 12288
        IN_F = 1024
        OUT_F = 1024
        H = 16
        D = OUT_F // H
        NUM_ETYPES = 4

        def _build_mask(edge_index, edge_type, edge_type_weights, dtype):
            src, dst = (edge_index[0], edge_index[1])
            w = jax.nn.softplus(edge_type_weights)
            mask = jnp.full((N, N), -jnp.inf, dtype=dtype)
            mask = mask.at[src, dst].set(w[edge_type - 1])
            diag = jnp.diagonal(mask)
            idx = jnp.arange(N)
            mask = mask.at[idx, idx].set(jnp.where(jnp.isneginf(diag), w[3], diag))
            return mask
        q = x @ wq.T + bq
        k = x @ wk.T + bk
        v = x @ wv.T + bv
        q2 = (q @ wiq.T + biq).reshape(N, H, D).transpose(1, 0, 2)
        k2 = (k @ wik.T + bik).reshape(N, H, D).transpose(1, 0, 2)
        v2 = (v @ wiv.T + biv).reshape(N, H, D).transpose(1, 0, 2)
        mask = _build_mask(edge_index, edge_type, edge_type_weights, x.dtype)
        scale = 1.0 / np.sqrt(D).astype(np.float32)
        scores = jnp.einsum('hnd,hmd->hnm', q2, k2) * scale + mask[None]
        attn = jax.nn.softmax(scores, axis=-1)
        out = jnp.einsum('hnm,hmd->hnd', attn, v2)
        out = out.transpose(1, 0, 2).reshape(N, OUT_F)
        return out @ wo.T + bo

    def _L0_ffn_ref(hidden_states, gate_w, gate_bias, Wg, Wu, Wd, Ws_g, Ws_u, Ws_d):
        import jax, jax.numpy as jnp
        import numpy as np
        E = 16
        K = 4
        NG = 4
        TG = 2
        SCALE = 2.5
        NORM_TOPK = True
        H = 1024
        I = 512
        SH_I = I * 2
        B, S = (2, 256)
        x = hidden_states
        b, s, h = x.shape
        n = b * s
        xf = x.reshape(n, h)
        logits = xf @ gate_w.T
        scores = jax.nn.sigmoid(logits)
        sfc = scores + gate_bias
        epg = E // NG
        grp = sfc.reshape(n, NG, epg)
        g_scores = jax.lax.top_k(grp, 2)[0].sum(-1)
        _, gidx = jax.lax.top_k(g_scores, TG)
        gmask = jax.nn.one_hot(gidx, NG, dtype=sfc.dtype).sum(1)
        emask = jnp.repeat(gmask, epg, axis=1)
        masked = jnp.where(emask > 0, sfc, -jnp.inf)
        _, topk_idx = jax.lax.top_k(masked, K)
        topk_w = jnp.take_along_axis(scores, topk_idx, axis=1)
        if K > 1 and NORM_TOPK:
            topk_w = topk_w / (topk_w.sum(-1, keepdims=True) + 1e-20)
        topk_w = topk_w * SCALE
        cw = (jax.nn.one_hot(topk_idx, E, dtype=topk_w.dtype) * topk_w[..., None]).sum(1)
        hg = jnp.einsum('nh,eih->nei', xf, Wg)
        hu = jnp.einsum('nh,eih->nei', xf, Wu)
        act = jax.nn.silu(hg) * hu
        y = jnp.einsum('nei,ne,ehi->nh', act, cw, Wd)
        shared = jax.nn.silu(xf @ Ws_g.T) * (xf @ Ws_u.T) @ Ws_d.T
        y = y + shared
        return (x + y.reshape(b, s, h)).astype(hidden_states.dtype)
    edge_index = jnp.stack([src, dst])
    x = x + _L0_gnn_ref(_layernorm(x, axis=-1), edge_index, edge_type_5, L0_gnn_edge_type_weights, L0_gnn_wq, L0_gnn_bq, L0_gnn_wk, L0_gnn_bk, L0_gnn_wv, L0_gnn_bv, L0_gnn_wiq, L0_gnn_biq, L0_gnn_wik, L0_gnn_bik, L0_gnn_wiv, L0_gnn_biv, L0_gnn_wo, L0_gnn_bo)
    x = x + _L0_ffn_ref(_layernorm(x, axis=-1)[None], L0_ffn_gate_w, L0_ffn_gate_bias, L0_ffn_Wg, L0_ffn_Wu, L0_ffn_Wd, L0_ffn_Ws_g, L0_ffn_Ws_u, L0_ffn_Ws_d)[0]
    return x

_drawn_inputs = setup_inputs


def setup_inputs(seed=0):
    import zlib

    import numpy as np

    out = dict(_drawn_inputs(seed))
    spreads = {'L0_ffn_gate_bias': (0.0, 0.1)}
    factors = {'L0_gnn_bq': 34.981,
     'L0_gnn_bk': 64.0,
     'L0_gnn_bv': 5.563,
     'L0_gnn_biq': 23.892,
     'L0_gnn_bik': 64.0,
     'L0_gnn_edge_type_weights': 2.781}
    for name, (base, spread) in spreads.items():
        noise = np.random.default_rng([zlib.crc32(name.encode()), seed]).standard_normal(out[name].shape)
        drawn = base * np.exp(spread * noise) if base else spread * noise
        out[name] = jnp.asarray(drawn.astype(out[name].dtype))
    for name, factor in factors.items():
        out[name] = (out[name] * factor).astype(out[name].dtype)
    return out
```

```python
from contextlib import ExitStack

import concourse.bass as bass
from concourse import mybir

ALU = mybir.AluOpType
ACT = mybir.ActivationFunctionType
AX_X = mybir.AxisListType.X
F32 = mybir.dt.float32
R32 = mybir.dt.float32r
F16 = mybir.dt.float16
BF16 = mybir.dt.bfloat16
I32 = mybir.dt.int32

P = 128
NODES = 384
T = NODES // P
F = 1024
C = F // P
HEADS = 16
HD = F // HEADS
EXPERTS = 16
TOP = 4
GROUPS = 4
EPG = EXPERTS // GROUPS
INNER = 512
IC = INNER // P
EDGES = 6144
EC = EDGES // P
EG = 12
SCALE = 1.0 / HD ** 0.5
LN_EPS = 1e-5
ROUTE_SCALE = 2.5
ABSENT = -3.0e37
MAX_BLOCKS = NODES * TOP // P + EXPERTS
IDX_COLS = MAX_BLOCKS + 1

P_V, P_IV, P_Q, P_K, P_IQK, P_O = 0, 8, 16, 24, 32, 48
P_GU, P_EXP = 56, 72
PER_EXPERT = C + IC
P_DOWN = P_EXP + EXPERTS * PER_EXPERT
PIECES = P_DOWN + C
RAWS = 4
SLOTS = 16

BUF_A, BUF_B, BUF_C, BUF_D = 0, 3, 6, 9


def piece_slot(p):
    if p < P_O:
        return 12 + p % 4
    if p < P_GU:
        return (12, 13, 14, 15, 3, 4, 5, 9)[p - P_O]
    if p < P_EXP:
        return (10, 11, 12, 13, 14, 15, 3, 4, 5, 1, 2, 3, 4, 5, 1, 2)[p - P_GU]
    return (p + 1) % SLOTS


def used_at(q):
    if q < P_IV:
        return "proj_done", q + 1
    if q < P_Q:
        return ("piece_used", q - P_IV + 1) if q < P_Q - 1 else ("v2_done", 2 * T)
    if q < P_O:
        return "proj_done", q - P_Q + C + 1
    if q < P_GU:
        return ("piece_used", q - P_O + C) if q < P_GU - 1 else ("wo_done", 2 * T)
    return "gu_s_done", q - P_GU + 1


def slot_free_at(p):
    s = piece_slot(p)
    earlier = [q for q in range(min(p, P_EXP)) if piece_slot(q) == s]
    waits = [used_at(earlier[-1])] if earlier else []
    if P_O <= p:
        if s in (3, 4, 5, 9, 10, 11):
            waits.append(used_at(P_O - 1))
        if s in (0, 1, 2):
            waits.append(used_at(P_GU - 1))
        if s in (6, 7, 8):
            waits.append(used_at(P_EXP - 1))
    return waits


def program(nc, weights, x, biases, bo, gate, gate_bias, etw, edge_cols, edge_rows, out,
            token_table, xn2_dram, y_dram):
    with ExitStack() as ctx:
        def sb(name, shape, dt, at=ctx):
            return at.enter_context(nc.sbuf_tensor(name, shape, dt))

        def sem(name):
            return ctx.enter_context(nc.semaphore(name))

        bank = [ctx.enter_context(nc.psum_tensor(f"bank{i}", [P, 512], F32)) for i in range(8)]

        ring = sb("ring", [P, SLOTS, 2, F], R32)
        raw = sb("raw", [P, RAWS, F], F32)
        res = sb("res", [P, T, F], F32)
        rows = sb("rows", [P, T, F], F32)
        ident = sb("ident", [P, P], F32)
        tri = sb("tri", [P, P], F32)
        ones = sb("ones", [P, P], F32)
        lower = sb("lower", [P, EXPERTS + 1, EXPERTS], F32)
        kcol = sb("kcol", [P, TOP], F32)
        bias = sb("bias", [P, 6, C], F32)
        gate_f = sb("gate_f", [P, C, EXPERTS], F32)
        gate_r = sb("gate_r", [P, 2, C, EXPERTS], R32)
        gbias = sb("gbias", [P, EXPERTS], F32)
        stats = sb("stats", [P, T, 2, 6], F32)
        mv = sb("mv", [P, T, 2], F32)
        sd = sb("sd", [P, T], F32)
        ln_s = sb("ln_s", [P, T, 4], F32)
        eps_c = sb("eps_c", [P, 1], F32)
        esum = sb("esum", [P, 2, T], F32)
        erec = sb("erec", [P, 2, T], F32)
        nmax = sb("nmax", [P, 2, T], F32)
        w8 = sb("w8", [P, 4], F32)
        zone = ExitStack()
        mask = sb("mask", [P, T, NODES], F32, zone)
        early = ExitStack()
        bo_b = sb("bo_b", [P, F], F32, early)
        onehot = sb("onehot", [P, 2, 4, 2, NODES], BF16, early)
        pid_w = sb("pid_w", [2 * EG, EG, P], F16, early)
        erow_i = sb("erow_i", [2 * EG, 512], I32, early)
        erow = sb("erow", [2 * EG, 512], F16, early)
        ecol_i = sb("ecol_i", [P, 3, EC], I32, early)
        ecol = sb("ecol", [P, 3, EC], F32, early)
        pid = sb("pid", [P, EC], F32, early)
        val = sb("val", [P, EC], F32, early)
        pw = sb("pw", [P, EC], I32, early)
        dup = sb("dup", [P, EC], F32, early)
        dup_junk = sb("dup_junk", [P, 4, P], BF16, early)
        iota16 = sb("iota16", [P, NODES], F16, early)
        ident4 = sb("ident4", [P, 2, P], BF16, early)
        w_in = sb("w_in", [P, 4, 4], F32, early)
        mk_i = sb("mk_i", [P, NODES], I32, early)
        mk_t = sb("mk_t", [P, NODES], F32, early)
        early.close()

        attn = ExitStack()
        prob = sb("prob", [P, 2, T, NODES], F32, attn)
        probT = sb("probT", [P, 2, T, NODES], R32, attn)
        qk2 = sb("qk2", [P, 2, 2, 2, NODES], R32, attn)
        attn.close()
        zone.close()

        moe = ctx
        xg_raw = sb("xg_raw", [P, F], F32, moe)
        xgT = sb("xgT", [P, 2, C, P], R32, moe)
        act_s = sb("act_s", [P, 2, 256], F32, moe)
        act_r = sb("act_r", [P, INNER], F32, moe)
        actT = sb("actT", [P, 2, IC, P], R32, moe)
        y_sb = sb("y_sb", [P, F], F32, moe)
        sig = sb("sig", [P, NODES], F32, moe)
        cmp_a, cmp_b = xg_raw, y_sb
        sc = sb("sc", [P, T * EXPERTS], F32, moe)
        sfc = sb("sfc", [P, T * EXPERTS], F32, moe)
        rt = sb("rt", [P, 6, T * EXPERTS], F32, moe)
        gsc = sb("gsc", [P, 3, T * GROUPS], F32, moe)
        den = sb("den", [P, 2, T], F32, moe)
        cw = sb("cw", [P, T, TOP], F32, moe)
        nblk = sb("nblk", [P, 2, EXPERTS], F32, moe)
        first_f = sb("first_f", [P, EXPERTS + 1], F32, moe)
        blk_i = sb("blk_i", [P, 2, EXPERTS + 1], I32, moe)
        row_f = sb("row_f", [P, T * TOP], F32, moe)
        row_i = sb("row_i", [P, T * TOP], I32, moe)
        pos_i = sb("pos_i", [P, 3, T * TOP], I32, moe)
        tok_i = sb("tok_i", [P, T], I32, moe)
        zero_i = sb("zero_i", [P, IDX_COLS], I32, moe)
        idx = sb("idx", [P, IDX_COLS], I32, moe)
        idx_now = sb("idx_now", [P, 1], I32, moe)
        held = sb("held", [P, 1], I32, moe)

        raw_in = [sem(f"raw_in{i}") for i in range(RAWS)]
        hi_done, lo_done = sem("hi_done"), sem("lo_done")
        piece_used, exp_used = sem("piece_used"), sem("exp_used")
        x_in = [sem(f"x_in{t}") for t in range(T)]
        small_in, edge_in = sem("small_in"), sem("edge_in")
        c_set, consts = sem("c_set"), sem("consts")
        v_step = sem("v_step")
        ln_var, ln_sd, xn_done = sem("ln_var"), sem("ln_sd"), sem("xn_done")
        xT_done, xT_hi, xT_lo = sem("xT_done"), sem("xT_hi"), sem("xT_lo")
        gate_hi, gate_lo = sem("gate_hi"), sem("gate_lo")
        sp_ready, sp_exp, sp_ln = sem("sp_ready"), sem("sp_exp"), sem("sp_ln")
        erow_done, pid_done, dup_done = sem("erow_done"), sem("pid_done"), sem("dup_done")
        hot_done, hot_used, mask_sum, mask_done = sem("hot_done"), sem("hot_used"), sem("mask_sum"), sem("mask_done")
        proj_done, proj_hi, proj_lo = sem("proj_done"), sem("proj_hi"), sem("proj_lo")
        v2_done, v2_hi, v2_lo = sem("v2_done"), sem("v2_hi"), sem("v2_lo")
        s_done, sm_done, exp_done, rec_done, p_done = sem("s_done"), sem("sm_done"), sem("exp_done"), sem("rec_done"), sem("p_done")
        pT_done, pT_hi, pT_lo = sem("pT_done"), sem("pT_hi"), sem("pT_lo")
        pv_done, out_hi, out_lo = sem("pv_done"), sem("out_hi"), sem("out_lo")
        res_bo, wo_done = sem("res_bo"), sem("wo_done")
        logits_done, score_done = sem("logits_done"), sem("score_done")
        sel_done, count_done, route_done = sem("sel_done"), sem("count_done"), sem("route_done")
        gu_s_done, sig_s, silu_s = sem("gu_s_done"), sem("sig_s"), sem("silu_s")
        xn2_stored, table_in, idx_in = sem("xn2_stored"), sem("table_in"), sem("idx_in")
        idx_set, held_done, xg_in = sem("idx_set"), sem("held_done"), sem("xg_in")
        xg_done, xg_hi, xg_lo = sem("xg_done"), sem("xg_hi"), sem("xg_lo")
        gu_done, sig_done, mul_done, act_done = sem("gu_done"), sem("sig_done"), sem("mul_done"), sem("act_done")
        aT_done, aT_hi, aT_lo = sem("aT_done"), sem("aT_hi"), sem("aT_lo")
        y_done, y_out_a, y_out_v, y_free = sem("y_done"), sem("y_out_a"), sem("y_out_v"), sem("y_free")
        s_hi, s_lo, down_done = sem("s_hi"), sem("s_lo"), sem("down_done")
        back_in = [sem(f"back_in{k}") for k in range(TOP)]
        y_fill = sem("y_fill")
        sum_done, out_ready, out_stored = sem("sum_done"), sem("out_ready"), sem("out_stored")

        counts = {"proj_done": proj_done, "piece_used": piece_used, "v2_done": v2_done, "wo_done": wo_done,
                  "gu_s_done": gu_s_done}

        def buf(slot):
            return ring[:, slot:slot + 3].rearrange("p s h n -> p (s h n)").rearrange(
                "p (h c n) -> p h c n", h=2, c=C)

        xnT = buf(BUF_A)
        outT = buf(BUF_A)
        vT = buf(BUF_B)
        qT = buf(BUF_B)
        v2 = ring[:, BUF_C:BUF_C + 3].rearrange("p s h n -> p (s h n)").rearrange(
            "p (h t n) -> p h t n", h=2, t=T)
        xn2T = buf(BUF_C)
        kT = buf(BUF_D)
        innerT = buf(1)

        def hi(p):
            return ring[:, piece_slot(p), 0, :]

        def lo(p):
            return ring[:, piece_slot(p), 1, :]

        def f32(ap):
            return ap.bitcast(F32)

        V0, Q0, K0, PAIR0 = 0, 8, 16, 24

        block = ctx.enter_context(nc.Block())

        def each_block(eng, e, body):
            j0 = eng.value_load(blk_i[0:1, 0, bass.ds(e, 1)], min_val=0, max_val=MAX_BLOCKS - 1)
            last = eng.value_load(blk_i[0:1, 1, bass.ds(e, 1)], min_val=0, max_val=MAX_BLOCKS - 1)
            with eng.If(j0 < last):
                with eng.Fori(j0, last) as j:
                    body(j, False)
            body(last, True)

        @block.sync
        def _(sp):
            for t in range(T):
                sp.dma_start(res[:, t, :], x[t * P:(t + 1) * P, :]).then_inc(x_in[t], 16)
            sp.dma_start(ecol_i[:], edge_cols).then_inc(edge_in, 16)
            sp.dma_start(erow_i[:], edge_rows).then_inc(edge_in, 16)
            sp.dma_start(raw[:, 0, :], weights[0]).then_inc(raw_in[0], 16)
            sp.dma_start(bias[:], biases).then_inc(small_in, 16)
            sp.dma_start(w_in[:, 0, :], etw.partition_broadcast(P).rearrange("p a n -> p (a n)")).then_inc(small_in, 16)
            for p in range(1, RAWS):
                sp.dma_start(raw[:, p, :], weights[p]).then_inc(raw_in[p], 16)
            sp.dma_start(gate_f[:], gate).then_inc(small_in, 16)
            sp.dma_start(gbias[:], gate_bias.partition_broadcast(P).rearrange("p a n -> p (a n)")).then_inc(small_in, 16)
            sp.dma_start(bo_b[:], bo.partition_broadcast(P).rearrange("p a n -> p (a n)")).then_inc(small_in, 16)
            with sp.Fori(1, PIECES // RAWS) as g:
                for i in range(RAWS):
                    sp.wait_ge(lo_done, RAWS * g + (i + 1 - RAWS))
                    sp.dma_start(raw[:, i, :], weights[bass.ds(RAWS * g + i, 1)].rearrange("a p n -> (a p) n")).then_inc(raw_in[i], 16)
            for t in range(T):
                sp.wait_ge(out_ready, t + 1)
                sp.dma_start(out[t * P:(t + 1) * P, :], res[:, t, :]).then_inc(out_stored, 16)
            sp.wait_ge(out_stored, 16 * T)

        @block.gpsimd
        def _(pool):
            g = nc.gpsimd
            n_set = [0]

            def put(ins):
                ins.then_inc(c_set, 1)
                n_set[0] += 1

            def affine(ap, pattern, op, fill, base, cm):
                pool.wait_ge(c_set, n_set[0])
                put(g.affine_select(out=ap, in_=ap, pattern=pattern, compare_op=op, fill=fill, base=base,
                                    channel_multiplier=cm))

            put(g.memset(eps_c[:], LN_EPS))
            put(g.memset(ident[:], 0.0))
            put(g.memset(tri[:], 1.0))
            put(g.memset(ones[:], 1.0))
            put(g.memset(lower[:], 1.0))
            put(g.memset(pid_w[:], 0.0))
            affine(ident[:], [[1, P]], ALU.not_equal, 1.0, 0, -1)
            affine(tri[:], [[1, P]], ALU.is_gt, 0.0, 0, -1)
            affine(pid_w[:], [[-2, EG], [0, P]], ALU.not_equal, float(NODES), 0, 1)
            affine(pid_w[:], [[-2, EG], [0, P]], ALU.not_equal, 1.0, -1, 1)
            put(g.iota(iota16[:], [[1, NODES]], base=0, channel_multiplier=0, allow_small_or_imprecise_dtypes=True))
            put(g.iota(pw[:], [[1, EC]], base=8, channel_multiplier=0))
            put(g.iota(kcol[:], [[1, TOP]], base=0, channel_multiplier=0, allow_small_or_imprecise_dtypes=True))
            affine(lower[:], [[1, EXPERTS + 1], [-1, EXPERTS]], ALU.is_gt, 0.0, 0, 0)
            pool.wait_ge(c_set, n_set[0])
            g.memset(dup_junk[:, 0, 0:1], 0.0).then_inc(consts, 1)

            pool.wait_ge(small_in, 80)
            for t in range(T):
                pool.wait_ge(xn_done, t + 1)
                g.tensor_tensor(res[:, t, :], res[:, t, :], bo_b[:], ALU.add).then_inc(res_bo, 1)

            def hold_wait():
                g.tensor_tensor(held[:], idx_now[:], idx_now[:], ALU.add).then_inc(held_done, 1)

            pool.wait_ge(out_lo, HEADS)
            g.iota(tok_i[:], [[P, T]], base=0, channel_multiplier=1).then_inc(c_set, 1)
            g.memset(zero_i[:], 0).then_inc(c_set, 1)
            n_set[0] += 2
            pool.wait_ge(c_set, n_set[0])
            pool.dma_start(token_table.rearrange("(p c) a -> p (c a)", p=P), zero_i[:]).then_inc(y_free, 16)
            for t in range(T):
                pool.wait_ge(xn_done, T + t + 1)
                pool.dma_start(xn2_dram[t * P:(t + 1) * P, :], rows[:, t, :]).then_inc(xn2_stored, 16)
            pool.wait_ge(route_done, 1)
            pool.wait_ge(y_free, 16)
            for n in range(T * TOP):
                pool.indirect_dma_start(token_table, bass.IndirectOffsetOnAxis(pos_i[:, 2, n:n + 1], 0),
                                        tok_i[:, n // TOP:n // TOP + 1], None).then_inc(table_in, 16)
            pool.wait_ge(table_in, 16 * T * TOP)
            pool.dma_start(idx[:], token_table.rearrange("(p c) a -> p (c a)", p=P)).then_inc(idx_in, 16)
            pool.wait_ge(idx_in, 16)
            pool.wait_ge(xn2_stored, 16 * T)
            g.tensor_copy(idx_now[:], idx[:, 0:1]).then_inc(idx_set, 1)
            pool.wait_ge(idx_set, 1)
            hold_wait()
            pool.indirect_dma_start(xg_raw[:], None, xn2_dram, bass.IndirectOffsetOnAxis(idx_now[:], 0)).then_inc(xg_in, 16)

            blocks = pool.value_load(blk_i[0:1, 0, EXPERTS:EXPERTS + 1], min_val=1, max_val=MAX_BLOCKS - 1)
            with pool.Fori(blocks, MAX_BLOCKS) as j:
                pool.dma_start(y_dram[bass.ds(j, 1)].rearrange("a p n -> (a p) n"), x[0:P, :]).then_inc(y_fill, 16)

            def body(j, last):
                pool.wait_ge(held_done, j + 1)
                pool.wait_ge(xg_done, 2 * j + 2)
                g.tensor_copy(idx_now[:], idx[:, bass.ds(j + 1, 1)]).then_inc(idx_set, 1)
                pool.wait_ge(idx_set, j + 2)
                hold_wait()
                pool.indirect_dma_start(xg_raw[:], None, xn2_dram,
                                        bass.IndirectOffsetOnAxis(idx_now[:], 0)).then_inc(xg_in, 16)
                pool.wait_ge(y_out_a, j + 2)
                pool.wait_ge(y_out_v, j + 2)
                pool.dma_start(y_dram[bass.ds(j, 1)].rearrange("a p n -> (a p) n"), y_sb[:]).then_inc(y_free, 16)

            with pool.Fori(0, EXPERTS) as e:
                each_block(pool, e, body)
            blocks = pool.value_load(blk_i[0:1, 0, EXPERTS:EXPERTS + 1], min_val=1, max_val=MAX_BLOCKS)
            unused = pool.value_load(blk_i[0:1, 1, EXPERTS:EXPERTS + 1], min_val=1, max_val=MAX_BLOCKS)
            pool.wait_ge(y_fill, 16 * unused)
            pool.wait_ge(held_done, blocks + 1)
            pool.wait_ge(y_free, 16 * blocks + 16)
            hold_wait()
            pool.wait_ge(lo_done, PIECES)
            y_rows = y_dram.rearrange("b p n -> (b p) n")
            for t in range(T):
                for k in range(TOP):
                    if t:
                        pool.wait_ge(sum_done, TOP * (t - 1) + k + 1)
                    pool.indirect_dma_start(raw[:, k, :], None, y_rows,
                                            bass.IndirectOffsetOnAxis(row_i[:, TOP * t + k:TOP * t + k + 1], 0)).then_inc(back_in[k], 16)

        @block.scalar
        def _(act):
            a = nc.scalar

            def split(p):
                act.wait_ge(raw_in[p % RAWS], 16 * (p // RAWS + 1))
                for name, n in slot_free_at(p):
                    act.wait_ge(counts[name], n)
                a.activation(hi(p), raw[:, p % RAWS, :], ACT.Copy).then_inc(hi_done, 1)

            def ln_root(n):
                act.wait_ge(ln_var, n + 1)
                a.activation(sd[:, n % T:n % T + 1], mv[:, n % T, 1:2], ACT.Sqrt, bias=eps_c[:, 0:1]).then_inc(ln_sd, 1)

            def xT_split(n, dst):
                t, half = n // 2 % T, n % 2
                act.wait_ge(xT_done, n + 1)
                a.activation(dst[:, 0, 4 * half:4 * half + 4, t * P:(t + 1) * P],
                             bank[6 + half][:].rearrange("p (c n) -> p c n", c=4), ACT.Copy).then_inc(xT_hi, 1)

            def proj_split(n, ps, dst, b):
                act.wait_ge(proj_done, n + 1)
                a.activation(dst, ps[:, 0:NODES], ACT.Identity, bias=b).then_inc(proj_hi, 1)

            act.wait_ge(consts, 1)
            for t in range(T):
                ln_root(t)
            act.wait_ge(edge_in, 32)
            a.activation(erow[:], erow_i[:], ACT.Copy).then_inc(erow_done, 1)
            for n in range(2):
                xT_split(n, xnT)
            split(0)
            for n in range(2, 2 * T):
                xT_split(n, xnT)
            for p in range(1, RAWS):
                split(p)
            act.wait_ge(small_in, 80)
            a.activation(gate_r[:, 0], gate_f[:], ACT.Copy).then_inc(gate_hi, 1)
            for i in range(4 * C):
                if i < C:
                    proj_split(V0 + i, bank[6 + i % 2], vT[:, 0, i, :], bias[:, 2, i:i + 1])
                elif i >= 2 * C:
                    n = i - C
                    dst, b = (qT, 0) if n < K0 else (kT, 1)
                    proj_split(n, bank[6 + n % 2], dst[:, 0, n % C, :], bias[:, b, n % C:n % C + 1])
                split(i + RAWS)
                if i == 2 * C - 1:
                    for b in range(6):
                        act.wait_ge(v2_done, b + 1)
                        a.activation(v2[:, 0, b // 2, 512 * (b % 2):512 * (b % 2) + 512], bank[b][:], ACT.Copy).then_inc(v2_hi, 1)
                if i == 3 * C:
                    act.wait_ge(sp_ready, 1)
                    a.activation(w_in[:, 2, :], w_in[:, 1, :], ACT.Exp).then_inc(sp_exp, 1)
                    act.wait_ge(sp_exp, 1)
                    a.activation(w_in[:, 3, :], w_in[:, 2, :], ACT.Ln, bias=1.0).then_inc(sp_ln, 1)

            act.wait_ge(mask_done, T)
            act.wait_ge(res_bo, T)

            def pair_split(n):
                m = n - PAIR0
                proj_split(n, bank[6], qk2[:, m // 2 % 2, m % 2, 0, :], bias[:, 3 + m % 2, m // 2:m // 2 + 1])

            for n in (PAIR0, PAIR0 + 1):
                pair_split(n)
                split(P_IQK + 4 + n - PAIR0)
            for h in range(HEADS + 1):
                if h:
                    for m in range(T):
                        act.wait_ge(pT_done, 3 * (h - 1) + m + 1)
                        a.activation(probT[:, 0, m, :], bank[3 + m][:, 0:NODES], ACT.Copy).then_inc(pT_hi, 1)
                if h < HEADS:
                    for t in range(T):
                        act.wait_ge(sm_done, 3 * h + t + 1)
                        a.activation(prob[:, h % 2, t, :], prob[:, h % 2, t, :], ACT.Exp, scale=-1.0,
                                     bias=nmax[:, h % 2, t:t + 1], accum_out=esum[:, h % 2, t:t + 1]).then_inc(exp_done, 1)
                if h < HEADS - 2:
                    pair_split(PAIR0 + 2 + h)
                    split(P_IQK + 6 + h)
                elif h < HEADS:
                    split(P_O + 4 + 2 * (h - HEADS + 2))
                    split(P_O + 5 + 2 * (h - HEADS + 2))
                if h:
                    r = 64 * ((h - 1) % 2)
                    c = (h - 1) // 2
                    act.wait_ge(pv_done, h)
                    a.activation(outT[r:r + 64, 0, c, :], bank[7][r:r + 64, 0:NODES], ACT.Identity,
                                 bias=bias[r:r + 64, 5, c:c + 1]).then_inc(out_hi, 1)
            split(P_GU)
            split(P_GU + 1)

            ln_root(T)
            xT_split(2 * T, xn2T)
            xT_split(2 * T + 1, xn2T)
            ln_root(T + 1)
            for p in range(P_GU + 2, P_GU + 6):
                split(p)
            xT_split(2 * T + 2, xn2T)
            xT_split(2 * T + 3, xn2T)
            ln_root(T + 2)
            xT_split(2 * T + 4, xn2T)
            xT_split(2 * T + 5, xn2T)
            split(P_GU + 6)
            split(P_GU + 7)
            act.wait_ge(logits_done, 1)
            a.activation(sc[:], bank[4][:, 0:T * EXPERTS], ACT.Sigmoid).then_inc(score_done, 1)

            nxt = P_GU + 8
            for o in range(C):
                act.wait_ge(gu_s_done, 2 * o + 1)
                if o:
                    act.wait_ge(silu_s, 2 * o)
                a.activation(sig[:], bank[o % 2][:, 0:NODES], ACT.Sigmoid).then_inc(sig_s, 1)
                for _ in range((1, 1, 1, 2, 2, 3, 3, 3)[o]):
                    split(nxt)
                    nxt += 1

            def x_split(j):
                for half in range(2):
                    act.wait_ge(xg_done, 2 * j + half + 1)
                    a.activation(xgT[:, 0, 4 * half:4 * half + 4, :],
                                 bank[4 + half][:].rearrange("p (c n) -> p c n", c=4), ACT.Copy).then_inc(xg_hi, 1)

            def split_at(p16, slot_of):
                r = slot_of % RAWS
                act.wait_ge(raw_in[r], p16)
                a.activation(hi(slot_of), raw[:, r, :], ACT.Copy).then_inc(hi_done, 1)

            x_split(0)
            act.wait_ge(route_done, 1)
            act.wait_ge(gu_s_done, 2 * C)
            act.sem_inc(y_out_a, 1)

            with act.Fori(0, EXPERTS // 4) as g4:
                for u in range(4):
                    q0 = P_EXP + PER_EXPERT * u

                    def loaded(p):
                        return 192 * g4 + 16 * (p // RAWS + 1)

                    for i in range(C, PER_EXPERT):
                        split_at(loaded(q0 + i), q0 + i)

                    def next_piece(i):
                        if i >= SLOTS - PER_EXPERT:
                            act.wait_ge(exp_used, 16 * g4 + (4 * u + i - 3))
                        split_at(loaded(q0 + PER_EXPERT + i), q0 + PER_EXPERT + i)

                    def body(j, last):
                        def sigmoid(half):
                            act.wait_ge(gu_done, 2 * j + half + 1)
                            a.activation(act_s[:, half, :], bank[half][:, 0:256], ACT.Sigmoid).then_inc(sig_done, 1)

                        def aT_split(half):
                            act.wait_ge(aT_done, 2 * j + half + 1)
                            a.activation(actT[:, 0, 2 * half:2 * half + 2, :],
                                         bank[2 + half][:, 0:256].rearrange("p (c n) -> p c n", c=2), ACT.Copy).then_inc(aT_hi, 1)

                        sigmoid(0)
                        if last:
                            next_piece(0)
                            next_piece(1)
                        aT_split(0)
                        if last:
                            next_piece(2)
                            next_piece(3)
                        sigmoid(1)
                        x_split(j + 1)
                        aT_split(1)
                        if last:
                            for i in range(4, 8):
                                next_piece(i)
                        act.wait_ge(y_done, 2 * j + 2)
                        act.wait_ge(y_free, 16 * j + 16)
                        a.activation(y_sb[:, 512:1024], bank[7][:], ACT.Copy).then_inc(y_out_a, 1)

                    each_block(act, 4 * g4 + u, body)

            for c in range(C):
                a.activation(innerT[:, 0, c, :], rows[:].rearrange("p t f -> p (t f)")[:, c * NODES:(c + 1) * NODES],
                             ACT.Copy).then_inc(s_hi, 1)

        @block.vector
        def _(dve):
            v = nc.vector
            n_step = [0]

            def step(ins):
                ins.then_inc(v_step, 1)
                n_step[0] += 1
                dve.wait_ge(v_step, n_step[0])

            def rest(dst, src, high):
                return v.tensor_tensor(dst, src, f32(high), ALU.subtract)

            def split(p):
                dve.wait_ge(hi_done, p + 1)
                rest(lo(p), raw[:, p % RAWS, :], hi(p)).then_inc(lo_done, 1)

            def norm_rows(n):
                t = n % T
                xt = res[:, t, :]
                for half in range(2):
                    ins = v.bn_stats(stats[:, t, half, :], xt[:, 512 * half:512 * half + 512])
                step(ins)
                v.bn_aggr(mv[:, t, :], stats[:, t]).then_inc(ln_var, 1)
                dve.wait_ge(ln_var, n + 1)
                dve.wait_ge(ln_sd, n + 1)
                r, b, c, y = (ln_s[:, t, i:i + 1] for i in range(4))
                step(v.reciprocal(r, sd[:, t:t + 1]))
                step(v.tensor_scalar(b, mv[:, t, 1:2], LN_EPS, r, ALU.add, ALU.mult))
                step(v.tensor_scalar(c, b, r, -0.5, ALU.mult, ALU.mult))
                step(v.tensor_scalar(y, c, 1.5, r, ALU.add, ALU.mult))
                v.tensor_scalar(rows[:, t, :], xt, mv[:, t, 0:1], y, ALU.subtract, ALU.mult).then_inc(xn_done, 1)

            def xT_split(n, dst):
                t, half = n // 2 % T, n % 2
                dve.wait_ge(xT_hi, n + 1)
                at = dst[:, :, 4 * half:4 * half + 4, t * P:(t + 1) * P]
                rest(at[:, 1], bank[6 + half][:].rearrange("p (c n) -> p c n", c=4), at[:, 0]).then_inc(xT_lo, 1)

            def proj_split(n, ps, dst, b):
                dve.wait_ge(proj_hi, n + 1)
                v.scalar_tensor_tensor(out=dst[:, 1], in0=ps[:, 0:NODES], scalar=b, in1=f32(dst[:, 0]),
                                       op0=ALU.add, op1=ALU.subtract).then_inc(proj_lo, 1)

            dve.wait_ge(consts, 1)
            for t in range(T):
                dve.wait_ge(x_in[t], 16)
                norm_rows(t)
            dve.wait_ge(edge_in, 32)
            step(v.tensor_copy(ecol[:], ecol_i[:]))
            v.scalar_tensor_tensor(out=pid[:], in0=ecol[:, 0, :], scalar=float(NODES), in1=ecol[:, 1, :],
                                   op0=ALU.mult, op1=ALU.add)
            for n in range(2):
                xT_split(n, xnT)
            split(0)
            for n in range(2, 2 * T):
                xT_split(n, xnT)
            for p in range(1, RAWS):
                split(p)
            step(v.tensor_scalar(val[:], ecol[:, 2, :], 0.0, 4.0, ALU.is_equal, ALU.mult))
            step(v.tensor_tensor(val[:], val[:], ecol[:, 2, :], ALU.add))
            step(v.tensor_scalar(pw[:], pw[:], 25, None, ALU.logical_shift_left))
            step(v.tensor_tensor(val[:], val[:], pw[:].bitcast(F32), ALU.mult))
            v.tensor_scalar(ident4[:, 0, :], ident[:], 1.0, None, ALU.mult)
            v.tensor_scalar(ident4[:, 1, :], ident[:], 4.0 * 2.0 ** (28 - 127), None, ALU.mult)
            dve.wait_ge(gate_hi, 1)
            rest(gate_r[:, 1], gate_f[:], gate_r[:, 0]).then_inc(gate_lo, 1)

            def repeats(group):
                dve.wait_ge(pid_done, group + 1)
                if group:
                    dve.wait_ge(dup_done, group)
                for i in range(4):
                    c = 4 * group + i
                    ins = v.scalar_tensor_tensor(out=dup_junk[:, i, :], in0=bank[group % 6][:, P * i:P * i + P],
                                                 scalar=pid[:, c:c + 1], in1=tri[:], op0=ALU.is_equal,
                                                 op1=ALU.mult, accum_out=dup[:, c:c + 1])
                ins.then_inc(dup_done, 1)

            def onehots(s):
                if s >= 2:
                    dve.wait_ge(hot_used, s - 1)
                for i in range(4):
                    c = 4 * s + i
                    v.tensor_scalar(onehot[:, s % 2, i, 0, :], iota16[:], ecol[:, 0, c:c + 1], None, ALU.is_equal)
                    ins = v.tensor_scalar(onehot[:, s % 2, i, 1, :], iota16[:], ecol[:, 1, c:c + 1],
                                          val[:, c:c + 1], ALU.is_equal, ALU.mult)
                ins.then_inc(hot_done, 1)

            def mask_rows(t):
                dve.wait_ge(mask_sum, 1)
                top = bank[t][:, 0:NODES]
                step(v.tensor_scalar(mk_i[:], top.bitcast(I32), 22, 7, ALU.logical_shift_right, ALU.bitwise_and))
                step(v.tensor_scalar(mask[:, t, :], top, 0.0, ABSENT, ALU.is_equal, ALU.mult))
                for code, n in ((0, 0), (2, 1), (3, 2), (4, 3)):
                    step(v.tensor_scalar(mk_t[:], mk_i[:], float(code), w8[:, n:n + 1], ALU.is_equal, ALU.mult))
                    ins = v.tensor_tensor(mask[:, t, :], mask[:, t, :], mk_t[:], ALU.add)
                    if code < 4:
                        step(ins)
                ins.then_inc(mask_done, 1)

            for i in range(4 * C):
                if i < C:
                    proj_split(V0 + i, bank[6 + i % 2], vT[:, :, i, :], bias[:, 2, i:i + 1])
                elif i >= 2 * C:
                    n = i - C
                    dst, b = (qT, 0) if n < K0 else (kT, 1)
                    proj_split(n, bank[6 + n % 2], dst[:, :, n % C, :], bias[:, b, n % C:n % C + 1])
                split(i + RAWS)
                if i < EG // 2:
                    repeats(2 * i)
                    repeats(2 * i + 1)
                if i == EG // 2:
                    dve.wait_ge(dup_done, EG)
                    step(v.tensor_scalar(dup[:], dup[:], 0.0, None, ALU.is_equal))
                    step(v.tensor_tensor(val[:], val[:], dup[:], ALU.mult))
                    step(v.tensor_scalar(w_in[:, 1, :], w_in[:, 0, :], -1.0, None, ALU.mult))
                    v.tensor_tensor(w_in[:, 1, :], w_in[:, 0, :], w_in[:, 1, :], ALU.min).then_inc(sp_ready, 1)
                if i == 2 * C - 1:
                    for b in range(6):
                        dve.wait_ge(v2_hi, b + 1)
                        at = v2[:, :, b // 2, 512 * (b % 2):512 * (b % 2) + 512]
                        rest(at[:, 1], bank[b][:], at[:, 0]).then_inc(v2_lo, 1)
                if 2 * C <= i < 2 * C + EG:
                    onehots(i - 2 * C)
                if i == 2 * C + EG:
                    dve.wait_ge(sp_ln, 1)
                    step(v.scalar_tensor_tensor(out=w8[:], in0=w_in[:, 0, :], scalar=0.0, in1=w_in[:, 3, :],
                                                op0=ALU.max, op1=ALU.add))
                    step(v.tensor_scalar(w8[:], w8[:], 1.0 / SCALE, None, ALU.mult))
                if i == 4 * C - 2:
                    mask_rows(0)
                if i == 4 * C - 1:
                    mask_rows(1)
                    mask_rows(2)

            dve.wait_ge(res_bo, T)

            def pair_split(n):
                m = n - PAIR0
                proj_split(n, bank[6], qk2[:, m // 2 % 2, m % 2], bias[:, 3 + m % 2, m // 2:m // 2 + 1])

            for n in (PAIR0, PAIR0 + 1):
                pair_split(n)
                split(P_IQK + 4 + n - PAIR0)
            for h in range(HEADS + 1):
                if h:
                    for m in range(T):
                        dve.wait_ge(pT_hi, 3 * (h - 1) + m + 1)
                        rest(probT[:, 1, m, :], bank[3 + m][:, 0:NODES], probT[:, 0, m, :]).then_inc(pT_lo, 1)
                if h < HEADS:
                    for t in range(T):
                        dve.wait_ge(s_done, 3 * h + t + 1)
                        v.tensor_tensor_reduce(out=prob[:, h % 2, t, :], in0=bank[t][:, 0:NODES], in1=mask[:, t, :],
                                               scale=-SCALE, scalar=-2.0 * ABSENT, op0=ALU.add, op1=ALU.min,
                                               accum_out=nmax[:, h % 2, t:t + 1]).then_inc(sm_done, 1)
                if h < HEADS:
                    dve.wait_ge(exp_done, 3 * h + 3)
                    v.reciprocal(erec[:, h % 2, :], esum[:, h % 2, :]).then_inc(rec_done, 1)
                    dve.wait_ge(rec_done, h + 1)
                    for t in range(T):
                        v.tensor_scalar(prob[:, h % 2, t, :], prob[:, h % 2, t, :], erec[:, h % 2, t:t + 1], None,
                                        ALU.mult).then_inc(p_done, 1)
                if h < HEADS - 2:
                    pair_split(PAIR0 + 2 + h)
                    split(P_IQK + 6 + h)
                elif h < HEADS:
                    split(P_O + 4 + 2 * (h - HEADS + 2))
                    split(P_O + 5 + 2 * (h - HEADS + 2))
                if h:
                    r = 64 * ((h - 1) % 2)
                    c = (h - 1) // 2
                    dve.wait_ge(out_hi, h)
                    v.scalar_tensor_tensor(out=outT[r:r + 64, 1, c, :], in0=bank[7][r:r + 64, 0:NODES],
                                           scalar=bias[r:r + 64, 5, c:c + 1], in1=f32(outT[r:r + 64, 0, c, :]),
                                           op0=ALU.add, op1=ALU.subtract).then_inc(out_lo, 1)
            split(P_GU)
            split(P_GU + 1)

            def second_norm(t):
                for half in range(2):
                    dve.wait_ge(wo_done, 2 * t + half + 1)
                    at = res[:, t, 512 * half:512 * half + 512]
                    ins = v.tensor_tensor(at, bank[2 * t + half][:], at, ALU.add)
                step(ins)
                norm_rows(T + t)

            def add_rows(t):
                dve.wait_ge(xn_done, T + t + 1)
                v.tensor_tensor(res[:, t, :], res[:, t, :], rows[:, t, :], ALU.add)

            second_norm(0)
            add_rows(0)
            xT_split(2 * T, xn2T)
            xT_split(2 * T + 1, xn2T)
            second_norm(1)
            add_rows(1)
            for p in range(P_GU + 2, P_GU + 6):
                split(p)
            xT_split(2 * T + 2, xn2T)
            xT_split(2 * T + 3, xn2T)
            second_norm(2)
            add_rows(2)
            xT_split(2 * T + 4, xn2T)
            xT_split(2 * T + 5, xn2T)
            split(P_GU + 6)
            split(P_GU + 7)

            def ranks(n_of, width, src, rank):
                full = [P, n_of, width, width]
                ca = cmp_a[:, 0:n_of * width * width].rearrange("p (n i j) -> p n i j", i=width, j=width)
                cb = cmp_b[:, 0:n_of * width * width].rearrange("p (n i j) -> p n i j", i=width, j=width)
                of_j = src.rearrange("p (n j) -> p n j", j=width).unsqueeze(2).to_broadcast(full)
                of_i = src.rearrange("p (n j) -> p n j", j=width).unsqueeze(3).to_broadcast(full)
                v.tensor_tensor(ca, of_j, of_i, ALU.is_gt)
                step(v.tensor_tensor(cb, of_j, of_i, ALU.is_equal))
                step(v.tensor_tensor(cb, cb, lower[:, 0:width, 0:width].unsqueeze(1).to_broadcast(full), ALU.mult))
                step(v.tensor_tensor(ca, ca, cb, ALU.add))
                step(v.tensor_reduce(rank, ca, AX_X, ALU.add))

            NE = T * EXPERTS
            dve.wait_ge(score_done, 1)
            step(v.tensor_tensor(sfc[:].rearrange("p (t e) -> p t e", t=T), sc[:].rearrange("p (t e) -> p t e", t=T),
                                 gbias[:].unsqueeze(1).to_broadcast([P, T, EXPERTS]), ALU.add))
            rank, keep, weight, place = rt[:, 0], rt[:, 1], rt[:, 2], rt[:, 3]
            ranks(T * GROUPS, EPG, sfc[:], rank.rearrange("p (n i) -> p n i", i=EPG))
            step(v.scalar_tensor_tensor(out=keep, in0=rank, scalar=2.0, in1=sfc[:], op0=ALU.is_lt, op1=ALU.mult))
            step(v.tensor_reduce(gsc[:, 0], keep.rearrange("p (n i) -> p n i", i=EPG), AX_X, ALU.add))
            ranks(T, GROUPS, gsc[:, 0], gsc[:, 1].rearrange("p (n i) -> p n i", i=GROUPS))
            step(v.tensor_scalar(gsc[:, 2], gsc[:, 1], 2.0, None, ALU.is_lt))
            in_group = gsc[:, 2].unsqueeze(2).to_broadcast([P, T * GROUPS, EPG])
            k3 = keep.rearrange("p (n i) -> p n i", i=EPG)
            step(v.tensor_tensor(k3, sfc[:].rearrange("p (n i) -> p n i", i=EPG), in_group, ALU.mult))
            step(v.tensor_scalar(gsc[:, 2], gsc[:, 2], 1.0e30, -1.0e30, ALU.mult, ALU.add))
            step(v.tensor_tensor(k3, k3, in_group, ALU.add))
            ranks(T, EXPERTS, keep, rank.rearrange("p (n i) -> p n i", i=EXPERTS))
            v.tensor_scalar(keep, rank, float(TOP), None, ALU.is_lt).then_inc(sel_done, 1)
            dve.wait_ge(sel_done, 1)
            step(v.tensor_tensor(weight, sc[:], keep, ALU.mult))
            step(v.tensor_reduce(den[:, 0], weight.rearrange("p (t e) -> p t e", t=T), AX_X, ALU.add))
            step(v.tensor_scalar(den[:, 1], den[:, 0], 1e-20, None, ALU.add))
            step(v.reciprocal(den[:, 0], den[:, 1]))
            w3 = weight.rearrange("p (t e) -> p t e", t=T)
            step(v.tensor_tensor(w3, w3, den[:, 0].unsqueeze(2).to_broadcast([P, T, EXPERTS]), ALU.mult))
            full = [P, T, TOP, EXPERTS]
            kth = cmp_a[:, 0:T * TOP * EXPERTS].rearrange("p (t k e) -> p t k e", t=T, k=TOP)
            prod = cmp_b[:, 0:T * TOP * EXPERTS].rearrange("p (t k e) -> p t k e", t=T, k=TOP)
            step(v.tensor_tensor(kth, rank.rearrange("p (t e) -> p t e", t=T).unsqueeze(2).to_broadcast(full),
                                 kcol[:].unsqueeze(1).unsqueeze(3).to_broadcast(full), ALU.is_equal))
            step(v.tensor_tensor(prod, kth, w3.unsqueeze(2).to_broadcast(full), ALU.mult))
            step(v.tensor_reduce(cw[:], prod, AX_X, ALU.add))
            step(v.tensor_scalar(cw[:], cw[:], ROUTE_SCALE, None, ALU.mult))

            def rows_of_experts():
                dve.wait_ge(count_done, 1)
                count = bank[5][:, NE:NE + EXPERTS]
                step(v.tensor_scalar(nblk[:, 0], count, float(P), 1.0, ALU.is_gt, ALU.add))
                step(v.scalar_tensor_tensor(out=nblk[:, 1], in0=count, scalar=float(2 * P), in1=nblk[:, 0],
                                            op0=ALU.is_gt, op1=ALU.add))
                full = [P, EXPERTS + 1, EXPERTS]
                pre = cmp_b[:, 0:(EXPERTS + 1) * EXPERTS].rearrange("p (i j) -> p i j", j=EXPERTS)
                step(v.tensor_tensor(pre, lower[:], nblk[:, 1].unsqueeze(1).to_broadcast(full), ALU.mult))
                step(v.tensor_reduce(first_f[:], pre, AX_X, ALU.add))
                v.tensor_copy(blk_i[:, 0], first_f[:])
                v.tensor_scalar(blk_i[:, 1, EXPERTS:EXPERTS + 1], first_f[:, EXPERTS:EXPERTS + 1], -1.0,
                                float(MAX_BLOCKS), ALU.mult, ALU.add)
                v.tensor_scalar(blk_i[:, 1, 0:EXPERTS], first_f[:, 1:EXPERTS + 1], 1.0, None, ALU.subtract)
                p3 = place.rearrange("p (t e) -> p t e", t=T)
                step(v.scalar_tensor_tensor(out=p3, in0=first_f[:, 0:EXPERTS].unsqueeze(1).to_broadcast([P, T, EXPERTS]),
                                            scalar=float(P), in1=bank[5][:, 0:NE].rearrange("p (t e) -> p t e", t=T),
                                            op0=ALU.mult, op1=ALU.add))
                step(v.tensor_tensor(prod, kth, p3.unsqueeze(2).to_broadcast([P, T, TOP, EXPERTS]), ALU.mult))
                step(v.tensor_reduce(row_f[:].rearrange("p (t k) -> p t k", t=T), prod, AX_X, ALU.add))
                step(v.tensor_copy(row_i[:], row_f[:]))
                v.tensor_scalar(pos_i[:, 0], row_i[:], P - 1, None, ALU.bitwise_and)
                step(v.tensor_scalar(pos_i[:, 1], row_i[:], 7, None, ALU.logical_shift_right))
                v.scalar_tensor_tensor(out=pos_i[:, 2], in0=pos_i[:, 0], scalar=float(IDX_COLS), in1=pos_i[:, 1],
                                       op0=ALU.mult, op1=ALU.add).then_inc(route_done, 1)

            inner = rows[:].rearrange("p t f -> p (t f)")
            nxt = P_GU + 8
            for o in range(C):
                if o == 2:
                    rows_of_experts()
                dve.wait_ge(sig_s, o + 1)
                v.tensor_tensor(sig[:], bank[o % 2][:, 0:NODES], sig[:], ALU.mult).then_inc(silu_s, 1)
                dve.wait_ge(silu_s, 2 * o + 1)
                dve.wait_ge(gu_s_done, 2 * o + 2)
                if o == 0:
                    dve.wait_ge(xn2_stored, 16 * T)
                v.tensor_tensor(inner[:, o * NODES:(o + 1) * NODES], bank[2 + o % 2][:, 0:NODES], sig[:],
                                ALU.mult).then_inc(silu_s, 1)
                for _ in range((1, 1, 1, 2, 2, 3, 3, 3)[o]):
                    split(nxt)
                    nxt += 1

            def x_split(j):
                for half in range(2):
                    dve.wait_ge(xg_hi, 2 * j + half + 1)
                    at = xgT[:, :, 4 * half:4 * half + 4, :]
                    rest(at[:, 1], bank[4 + half][:].rearrange("p (c n) -> p c n", c=4), at[:, 0]).then_inc(xg_lo, 1)

            def split_at(p, slot_of):
                dve.wait_ge(hi_done, p + 1)
                rest(lo(slot_of), raw[:, slot_of % RAWS, :], hi(slot_of)).then_inc(lo_done, 1)

            x_split(0)
            dve.sem_inc(y_out_v, 1)

            with dve.Fori(0, EXPERTS // 4) as g4:
                for u in range(4):
                    p0 = 48 * g4 + (P_EXP + PER_EXPERT * u)
                    q0 = P_EXP + PER_EXPERT * u
                    for i in range(C, PER_EXPERT):
                        split_at(p0 + i, q0 + i)

                    def next_piece(i):
                        split_at(p0 + (PER_EXPERT + i), q0 + PER_EXPERT + i)

                    def body(j, last):
                        def gated(half):
                            dve.wait_ge(sig_done, 2 * j + half + 1)
                            v.tensor_tensor(act_s[:, half, :], bank[half][:, 0:256], act_s[:, half, :],
                                            ALU.mult).then_inc(mul_done, 1)
                            dve.wait_ge(mul_done, 2 * j + half + 1)
                            v.tensor_tensor(act_r[:, 256 * half:256 * half + 256], bank[half][:, 256:512],
                                            act_s[:, half, :], ALU.mult).then_inc(act_done, 1)

                        def aT_split(half):
                            dve.wait_ge(aT_hi, 2 * j + half + 1)
                            at = actT[:, :, 2 * half:2 * half + 2, :]
                            rest(at[:, 1], bank[2 + half][:, 0:256].rearrange("p (c n) -> p c n", c=2),
                                 at[:, 0]).then_inc(aT_lo, 1)

                        gated(0)
                        if last:
                            next_piece(0)
                            next_piece(1)
                        aT_split(0)
                        if last:
                            next_piece(2)
                            next_piece(3)
                        gated(1)
                        x_split(j + 1)
                        aT_split(1)
                        if last:
                            for i in range(4, 8):
                                next_piece(i)
                        dve.wait_ge(y_done, 2 * j + 1)
                        dve.wait_ge(y_free, 16 * j + 16)
                        v.tensor_copy(y_sb[:, 0:512], bank[6][:]).then_inc(y_out_v, 1)

                    each_block(dve, 4 * g4 + u, body)

            for c in range(C):
                dve.wait_ge(s_hi, c + 1)
                rest(innerT[:, 1, c, :], inner[:, c * NODES:(c + 1) * NODES], innerT[:, 0, c, :]).then_inc(s_lo, 1)

            for t in range(T):
                for k in range(TOP):
                    n = TOP * t + k
                    dve.wait_ge(back_in[k], 16 * (t + 1))
                    v.scalar_tensor_tensor(out=res[:, t, :], in0=raw[:, k, :], scalar=cw[:, t, k:k + 1],
                                           in1=res[:, t, :], op0=ALU.mult, op1=ALU.add).then_inc(sum_done, 1)
                    dve.wait_ge(sum_done, n + 1)
                for half in range(2):
                    dve.wait_ge(down_done, 2 * t + half + 1)
                    at = res[:, t, 512 * half:512 * half + 512]
                    ins = v.tensor_tensor(at, bank[2 * t + half][:], at, ALU.add)
                ins.then_inc(out_ready, 1)

        @block.tensor
        def _(pe):
            mm = nc.tensor.matmul

            def mm3(ps, l_hi, l_lo, r_hi, r_lo, start, stop):
                mm(ps, l_hi, r_hi, start=start, stop=False)
                mm(ps, l_hi, r_lo, start=False, stop=False)
                return mm(ps, l_lo, r_hi, start=False, stop=stop)

            def xT(n, half):
                for c in range(4):
                    ins = nc.tensor.transpose(bank[6 + half][:, c * P:(c + 1) * P],
                                              rows[:, n % T, (4 * half + c) * P:(4 * half + c + 1) * P], ident[:])
                ins.then_inc(xT_done, 1)

            def pid_rows(group):
                if group >= 6:
                    pe.wait_ge(dup_done, group - 5)
                mm(bank[group % 6][:], pid_w[:, group, :], erow[:], start=True, stop=True).then_inc(pid_done, 1)

            def project(p, ps, src):
                pe.wait_ge(lo_done, p + 1)
                for c in range(C):
                    w = slice(c * P, (c + 1) * P)
                    ins = mm3(ps[:, 0:NODES], hi(p)[:, w], lo(p)[:, w], src[:, 0, c, :], src[:, 1, c, :],
                              c == 0, c == C - 1)
                return ins

            def mask_sums(s):
                pe.wait_ge(hot_done, s + 1)
                for i in range(4):
                    for t in range(T):
                        ins = mm(bank[t][:, 0:NODES], onehot[:, s % 2, i, 0, t * P:(t + 1) * P],
                                 onehot[:, s % 2, i, 1, :], start=(s == 0 and i == 0), stop=False,
                                 skip_group_check=True)
                ins.then_inc(hot_used, 1)

            pe.wait_ge(consts, 1)
            pe.wait_ge(erow_done, 1)
            for group in range(6):
                pid_rows(group)
            for t in range(T):
                pe.wait_ge(xn_done, t + 1)
                for half in range(2):
                    if t:
                        pe.wait_ge(xT_lo, 2 * t + half - 1)
                    xT(t, half)
            pe.wait_ge(xT_lo, 2 * T)
            for i in range(C):
                if 2 <= i < 5:
                    pid_rows(2 * i + 2)
                    pid_rows(2 * i + 3)
                if i >= 2:
                    pe.wait_ge(proj_lo, i - 1)
                project(P_V + i, bank[6 + i % 2], xnT).then_inc(proj_done, 1)
            pe.wait_ge(dup_done, EG)
            for c in range(C):
                pe.wait_ge(proj_lo, c + 1)
                pe.wait_ge(lo_done, P_IV + c + 1)
                for t in range(T):
                    for half in range(2):
                        w = slice(512 * half, 512 * half + 512)
                        n = slice(t * P, (t + 1) * P)
                        ins = mm3(bank[2 * t + half][:], vT[:, 0, c, n], vT[:, 1, c, n], hi(P_IV + c)[:, w],
                                  lo(P_IV + c)[:, w], c == 0, c == C - 1)
                        if c == C - 1:
                            ins.then_inc(v2_done, 1)
                if c < C - 1:
                    ins.then_inc(piece_used, 1)
            for i in range(2 * C):
                if 2 <= i < EG + 2:
                    if i == 2:
                        pe.wait_ge(v2_lo, 6)
                    mask_sums(i - 2)
                if i == EG + 2:
                    for t in range(T):
                        ins = mm(bank[t][:, t * P:(t + 1) * P], ident4[:, 0, :], ident4[:, 1, :], start=False,
                                 stop=True, skip_group_check=True)
                    ins.then_inc(mask_sum, 1)
                n = Q0 + i
                pe.wait_ge(proj_lo, n - 1)
                project(P_Q + i, bank[6 + n % 2], xnT).then_inc(proj_done, 1)

            def pair_project(m):
                n = PAIR0 + m
                pe.wait_ge(proj_lo, n)
                project(P_IQK + m, bank[6], (qT, kT)[m % 2]).then_inc(proj_done, 1)

            pair_project(0)
            pair_project(1)
            for h in range(HEADS + 1):
                if h:
                    pe.wait_ge(p_done, 3 * h)
                    for m in range(T):
                        for t in range(T):
                            ins = nc.tensor.transpose(bank[3 + m][:, t * P:(t + 1) * P],
                                                      prob[:, (h - 1) % 2, t, m * P:(m + 1) * P], ident[:])
                        ins.then_inc(pT_done, 1)
                if h < HEADS:
                    pe.wait_ge(proj_lo, PAIR0 + 2 * (h // 2) + 2)
                    r = slice(64 * (h % 2), 64 * (h % 2) + 64)
                    q, k = qk2[r, h // 2 % 2, 0], qk2[r, h // 2 % 2, 1]
                    for t in range(T):
                        n = slice(t * P, (t + 1) * P)
                        mm3(bank[t][:, 0:NODES], q[:, 0, n], q[:, 1, n], k[:, 0, :], k[:, 1, :], True,
                            True).then_inc(s_done, 1)
                if h < HEADS - 2:
                    pair_project(h + 2)
                if h:
                    c = slice((h - 1) // 2 * P, (h - 1) // 2 * P + P)
                    if h > 1:
                        pe.wait_ge(out_lo, h - 1)
                    for m in range(T):
                        pe.wait_ge(pT_lo, 3 * (h - 1) + m + 1)
                        ins = mm3(bank[7][:, 0:NODES], v2[:, 0, m, c], v2[:, 1, m, c], probT[:, 0, m, :],
                                  probT[:, 1, m, :], m == 0, m == T - 1)
                    ins.then_inc(pv_done, 1)

            def xT2(t):
                pe.wait_ge(xn_done, T + t + 1)
                for half in range(2):
                    if t:
                        pe.wait_ge(xT_lo, 2 * T + 2 * t + half - 1)
                    xT(t, half)

            pe.wait_ge(out_lo, HEADS)
            for t in range(T):
                for c in range(C):
                    if t == 0:
                        pe.wait_ge(lo_done, P_O + c + 1)
                    n = slice(t * P, (t + 1) * P)
                    for half in range(2):
                        w = slice(512 * half, 512 * half + 512)
                        ins = mm3(bank[2 * t + half][:], outT[:, 0, c, n], outT[:, 1, c, n], hi(P_O + c)[:, w],
                                  lo(P_O + c)[:, w], c == 0, c == C - 1)
                        if c == C - 1:
                            ins.then_inc(wo_done, 1)
                    if t == T - 1 and c < C - 1:
                        ins.then_inc(piece_used, 1)
                if t:
                    xT2(t - 1)
            xT2(T - 1)
            pe.wait_ge(xT_lo, 4 * T)
            pe.wait_ge(gate_lo, 1)
            for t in range(T):
                n = slice(t * P, (t + 1) * P)
                for c in range(C):
                    ins = mm3(bank[4][:, t * EXPERTS:(t + 1) * EXPERTS], xn2T[:, 0, c, n], xn2T[:, 1, c, n],
                              gate_r[:, 0, c, :], gate_r[:, 1, c, :], c == 0, c == C - 1)
            ins.then_inc(logits_done, 1)
            for o in range(C):
                if o == 2:
                    pe.wait_ge(sel_done, 1)
                    NE = T * EXPERTS
                    for t in range(T):
                        for s in range(t + 1):
                            mm(bank[5][:, t * EXPERTS:(t + 1) * EXPERTS], (tri if s == t else ones)[:],
                               rt[:, 1, s * EXPERTS:(s + 1) * EXPERTS], start=(s == 0), stop=(s == t))
                    for s in range(T):
                        ins = mm(bank[5][:, NE:NE + EXPERTS], ones[:], rt[:, 1, s * EXPERTS:(s + 1) * EXPERTS],
                                 start=(s == 0), stop=(s == T - 1))
                    ins.then_inc(count_done, 1)
                if o >= 2:
                    pe.wait_ge(silu_s, 2 * o - 2)
                for which in range(2):
                    p = P_GU + 2 * o + which
                    project(p, bank[2 * which + o % 2], xn2T).then_inc(gu_s_done, 1)

            def x_turn(j):
                pe.wait_ge(xg_in, 16 * j + 16)
                for half in range(2):
                    for c in range(4):
                        ins = nc.tensor.transpose(bank[4 + half][:, c * P:(c + 1) * P],
                                                  xg_raw[:, (4 * half + c) * P:(4 * half + c + 1) * P], ident[:])
                    ins.then_inc(xg_done, 1)

            pe.wait_ge(route_done, 1)
            x_turn(0)
            with pe.Fori(0, EXPERTS // 4) as g4:
                for u in range(4):
                    p0 = 48 * g4 + (P_EXP + PER_EXPERT * u)
                    q0 = P_EXP + PER_EXPERT * u

                    def body(j, last):
                        def turn(half):
                            pe.wait_ge(act_done, 2 * j + half + 1)
                            for c in range(2):
                                ins = nc.tensor.transpose(bank[2 + half][:, c * P:(c + 1) * P],
                                                          act_r[:, (2 * half + c) * P:(2 * half + c + 1) * P], ident[:])
                            ins.then_inc(aT_done, 1)

                        def gate_up(half, chunks):
                            w = slice(512 * half, 512 * half + 512)
                            for c in chunks:
                                if half == 0:
                                    pe.wait_ge(lo_done, p0 + (c + 1))
                                ins = mm3(bank[half][:], xgT[:, 0, c, :], xgT[:, 1, c, :], hi(q0 + c)[:, w],
                                          lo(q0 + c)[:, w], c == 0, c == C - 1)
                                if c == C - 1:
                                    ins.then_inc(gu_done, 1)
                                elif half and last and c < SLOTS - PER_EXPERT:
                                    ins.then_inc(exp_used, 1)

                        def down(half):
                            pe.wait_ge(aT_lo, 2 * j + half + 1)
                            for i in (2 * half, 2 * half + 1):
                                pe.wait_ge(lo_done, p0 + (C + i + 1))
                                for o in range(2):
                                    w = slice(512 * o, 512 * o + 512)
                                    ins = mm3(bank[6 + o][:], actT[:, 0, i, :], actT[:, 1, i, :], hi(q0 + C + i)[:, w],
                                              lo(q0 + C + i)[:, w], i == 0, i == IC - 1)
                                    if i == IC - 1:
                                        ins.then_inc(y_done, 1)

                        pe.wait_ge(xg_lo, 2 * j + 2)
                        gate_up(0, range(C))
                        gate_up(1, range(5))
                        turn(0)
                        gate_up(1, range(5, C))
                        x_turn(j + 1)
                        pe.wait_ge(y_out_a, j + 1)
                        pe.wait_ge(y_out_v, j + 1)
                        down(0)
                        turn(1)
                        down(1)

                    each_block(pe, 4 * g4 + u, body)

            blocks = pe.value_load(blk_i[0:1, 0, EXPERTS:EXPERTS + 1], min_val=1, max_val=MAX_BLOCKS)
            pe.wait_ge(xg_lo, 2 * blocks + 2)
            for t in range(T):
                for c in range(C):
                    if t == 0:
                        pe.wait_ge(lo_done, P_DOWN + c + 1)
                        pe.wait_ge(s_lo, c + 1)
                    n = slice(t * P, (t + 1) * P)
                    for half in range(2):
                        w = slice(512 * half, 512 * half + 512)
                        ins = mm3(bank[2 * t + half][:], innerT[:, 0, c, n], innerT[:, 1, c, n],
                                  hi(P_DOWN + c)[:, w], lo(P_DOWN + c)[:, w], c == 0, c == C - 1)
                        if c == C - 1:
                            ins.then_inc(down_done, 1)


def kernel(x, src, dst, edge_type_5, **w):
    import numpy as np
    import concourse.bacc as bacc
    from concourse.bass_utils import run_bass_kernel_spmd

    w = {k: np.asarray(v) for k, v in w.items()}

    def by_out(m):
        return m.reshape(C, P, C, P).transpose(0, 3, 2, 1).reshape(C, P, F)

    def by_in(m):
        return m.T.reshape(C, P, F)

    def mixed(a, b):
        return np.stack([a, b], 1).reshape(2 * C, P, F)

    wg = w["L0_ffn_Wg"].transpose(0, 2, 1).reshape(EXPERTS, C, P, 2, 1, 256)
    wu = w["L0_ffn_Wu"].transpose(0, 2, 1).reshape(EXPERTS, C, P, 2, 1, 256)
    gu = np.concatenate([wg, wu], 4).reshape(EXPERTS, C, P, F)
    wd = w["L0_ffn_Wd"].transpose(0, 2, 1).reshape(EXPERTS, IC, P, F)
    weights = np.concatenate([
        by_out(w["L0_gnn_wv"]), by_in(w["L0_gnn_wiv"]), by_out(w["L0_gnn_wq"]), by_out(w["L0_gnn_wk"]),
        mixed(by_out(w["L0_gnn_wiq"]), by_out(w["L0_gnn_wik"])), by_in(w["L0_gnn_wo"]),
        mixed(by_out(w["L0_ffn_Ws_g"]), by_out(w["L0_ffn_Ws_u"])),
        np.concatenate([gu, wd], 1).reshape(EXPERTS * PER_EXPERT, P, F), by_in(w["L0_ffn_Ws_d"])])
    biases = np.stack([w["L0_gnn_" + n].reshape(C, P).T for n in ("bq", "bk", "bv", "biq", "bik", "biv")], 1)
    src, dst, kind = (np.asarray(e) for e in (src, dst, edge_type_5))
    arrays = {
        "weights": weights,
        "x": np.asarray(x),
        "biases": biases,
        "bo": w["L0_gnn_bo"].reshape(1, F),
        "gate": w["L0_ffn_gate_w"].reshape(EXPERTS, C, P).transpose(2, 1, 0),
        "gate_bias": w["L0_ffn_gate_bias"].reshape(1, EXPERTS),
        "etw": w["L0_gnn_edge_type_weights"].reshape(1, 4),
        "edge_cols": np.stack([e.reshape(EC, P).T for e in (src, dst, kind)], 1),
        "edge_rows": np.stack([src.reshape(EG, 512), dst.reshape(EG, 512)], 1).reshape(2 * EG, 512),
    }
    arrays = {k: np.ascontiguousarray(v) for k, v in arrays.items()}
    nc = bacc.Bacc("TRN2", target_bir_lowering=False, num_devices=1)
    args = [nc.dram_tensor(k, v.shape, mybir.dt.from_np(v.dtype), kind="ExternalInput").ap() for k, v in arrays.items()]
    args.append(nc.dram_tensor("out", (NODES, F), F32, kind="ExternalOutput").ap())
    args.append(nc.dram_tensor("token_table", (P * IDX_COLS, 1), I32, kind="Internal").ap())
    args.append(nc.dram_tensor("xn2_dram", (NODES, F), F32, kind="Internal").ap())
    args.append(nc.dram_tensor("y_dram", (MAX_BLOCKS, P, F), F32, kind="Internal").ap())
    program(nc, *args)
    r = run_bass_kernel_spmd(nc, [arrays], core_ids=[0])
    return r.results[0]["out"]
```

```python
from contextlib import ExitStack

import concourse.bass as bass
from concourse import mybir

ALU = mybir.AluOpType
ACT = mybir.ActivationFunctionType
AX_X = mybir.AxisListType.X
F32 = mybir.dt.float32
R32 = mybir.dt.float32r
F16 = mybir.dt.float16
BF16 = mybir.dt.bfloat16
I32 = mybir.dt.int32

P = 128
NODES = 384
T = NODES // P
F = 1024
C = F // P
HEADS = 16
HD = F // HEADS
EXPERTS = 16
TOP = 4
GROUPS = 4
EPG = EXPERTS // GROUPS
INNER = 512
IC = INNER // P
EDGES = 6144
EC = EDGES // P
EG = 12
SCALE = 1.0 / HD ** 0.5
LN_EPS = 1e-5
ROUTE_SCALE = 2.5
ABSENT = -3.0e37
MAX_BLOCKS = NODES * TOP // P + EXPERTS
IDX_COLS = MAX_BLOCKS + 1
MASK_CODES = ((0, 0), (2, 1), (3, 2), (4, 3))

P_V, P_IV, P_Q, P_K, P_IQK, P_O = 0, 8, 16, 24, 32, 48
P_GU, P_EXP = 56, 72
PER_EXPERT = C + IC
P_DOWN = P_EXP + EXPERTS * PER_EXPERT
PIECES = P_DOWN + C
RAWS = 4
SLOTS = 16
GU_SLOTS = SLOTS - 3
GU_AHEAD = 8
GU_SPLITS = (2, 3, 3, 3, 3, 3, 2, 2)

BUF_A, BUF_B, BUF_C, BUF_D = 0, 3, 6, 9


def piece_slot(p):
    if p < P_O:
        return 12 + p % 4
    if p < P_GU:
        return (12, 13, 14, 15, 9, 10, 11, 3)[p - P_O]
    if p < P_EXP:
        return (4, 5, 3, 9, 10, 11, 12, 13, 14, 15, 0, 1, 2, 3, 4, 5)[p - P_GU]
    return (p + 1) % SLOTS


def used_at(q):
    if q < P_IV:
        return "proj_done", q + 1
    if q < P_Q:
        return ("piece_used", q - P_IV + 1) if q < P_Q - 1 else ("v2_done", 2 * T)
    if q < P_O:
        return "proj_done", q - P_Q + C + 1
    if q < P_GU:
        return ("piece_used", q - P_O + C) if q < P_GU - 1 else ("wo_done", 2 * T)
    return "gu_s_done", q - P_GU + 1


def slot_free_at(p):
    s = piece_slot(p)
    earlier = [q for q in range(min(p, P_EXP)) if piece_slot(q) == s]
    waits = [used_at(earlier[-1])] if earlier else []
    if P_O <= p:
        if s in (3, 4, 5, 9, 10, 11):
            waits.append(used_at(P_O - 1))
        if s in (0, 1, 2):
            waits.append(used_at(P_GU - 1))
        if s in (6, 7, 8):
            waits.append(used_at(P_EXP - 1))
    return waits


def program(nc, weights, x, biases, bo, gate, gate_bias, etw, edge_cols, edge_rows, out,
            token_table, xn2_dram, y_dram):
    with ExitStack() as ctx:
        def sb(name, shape, dt, at=ctx):
            return at.enter_context(nc.sbuf_tensor(name, shape, dt))

        def sem(name):
            return ctx.enter_context(nc.semaphore(name))

        bank = [ctx.enter_context(nc.psum_tensor(f"bank{i}", [P, 512], F32)) for i in range(8)]

        ring = sb("ring", [P, SLOTS, 2, F], R32)
        raw = sb("raw", [P, RAWS, F], F32)
        res = sb("res", [P, T, F], F32)
        rows = sb("rows", [P, T, F], F32)
        ident = sb("ident", [P, P], F32)
        tri = sb("tri", [P, P], F32)
        ones = sb("ones", [P, P], F32)
        lower = sb("lower", [P, EXPERTS + 1, EXPERTS], F32)
        kcol = sb("kcol", [P, TOP], F32)
        bias = sb("bias", [P, 6, C], F32)
        gate_f = sb("gate_f", [P, C, EXPERTS], F32)
        gate_r = sb("gate_r", [P, 2, C, EXPERTS], R32)
        gbias = sb("gbias", [P, EXPERTS], F32)
        stats = sb("stats", [P, T, 2, 6], F32)
        mv = sb("mv", [P, T, 2], F32)
        sd = sb("sd", [P, T], F32)
        ln_s = sb("ln_s", [P, 4, T], F32)
        eps_c = sb("eps_c", [P, 1], F32)
        esum = sb("esum", [P, 2, T], F32)
        erec = sb("erec", [P, 2, T], F32)
        nmax = sb("nmax", [P, 2, T], F32)
        w8 = sb("w8", [P, 4], F32)
        zone = ExitStack()
        mask = sb("mask", [P, T, NODES], F32, zone)
        early = ExitStack()
        bo_b = sb("bo_b", [P, F], F32, early)
        onehot = sb("onehot", [P, 2, 4, 2, NODES], BF16, early)
        pid_w = sb("pid_w", [2 * EG, EG, P], F16, early)
        erow_i = sb("erow_i", [2 * EG, 512], I32, early)
        erow = sb("erow", [2 * EG, 512], F16, early)
        ecol_i = sb("ecol_i", [P, 3, EC], I32, early)
        ecol = sb("ecol", [P, 3, EC], F32, early)
        pid = sb("pid", [P, EC], F32, early)
        val = sb("val", [P, EC], F32, early)
        pw = sb("pw", [P, EC], I32, early)
        dup = sb("dup", [P, EC], F32, early)
        dup_junk = sb("dup_junk", [P, 4, P], BF16, early)
        iota16 = sb("iota16", [P, NODES], F16, early)
        ident4 = sb("ident4", [P, 2, P], BF16, early)
        w_in = sb("w_in", [P, 4, 4], F32, early)
        early.close()

        attn = ExitStack()
        prob = sb("prob", [P, 2, T, NODES], F32, attn)
        probT = sb("probT", [P, 2, T, NODES], R32, attn)
        qk2 = sb("qk2", [P, 2, 2, 2, NODES], R32, attn)
        attn.close()
        zone.close()

        moe = ctx
        xg_raw = sb("xg_raw", [P, F], F32, moe)
        xgT = sb("xgT", [P, 2, C, P], R32, moe)
        act_s = sb("act_s", [P, 2, 256], F32, moe)
        act_r = sb("act_r", [P, INNER], F32, moe)
        actT = sb("actT", [P, 2, IC, P], R32, moe)
        y_sb = sb("y_sb", [P, F], F32, moe)
        sig = sb("sig", [P, NODES], F32, moe)
        cmp_a, cmp_b = xg_raw, y_sb
        scoreT = sb("scoreT", [EXPERTS, NODES], F32, moe)
        sc = sb("sc", [P, T * EXPERTS], F32, moe)
        sfc = sb("sfc", [P, T * EXPERTS], F32, moe)
        rt = sb("rt", [P, 6, T * EXPERTS], F32, moe)
        gsc = sb("gsc", [P, 3, T * GROUPS], F32, moe)
        den = sb("den", [P, 2, T], F32, moe)
        cw = sb("cw", [P, T, TOP], F32, moe)
        nblk = sb("nblk", [P, 2, EXPERTS], F32, moe)
        first_f = sb("first_f", [P, EXPERTS + 1], F32, moe)
        blk_i = sb("blk_i", [P, 2, EXPERTS + 1], I32, moe)
        row_f = sb("row_f", [P, T * TOP], F32, moe)
        row_i = sb("row_i", [P, T * TOP], I32, moe)
        pos_i = sb("pos_i", [P, 3, T * TOP], I32, moe)
        tok_i = sb("tok_i", [P, T], I32, moe)
        zero_i = sb("zero_i", [P, IDX_COLS], I32, moe)
        idx = sb("idx", [P, IDX_COLS], I32, moe)
        idx_now = sb("idx_now", [P, 1], I32, moe)
        held = sb("held", [P, 1], I32, moe)

        raw_in = [sem(f"raw_in{i}") for i in range(RAWS)]
        hi_done, lo_done = sem("hi_done"), sem("lo_done")
        piece_used, exp_used = sem("piece_used"), sem("exp_used")
        x_in = [sem(f"x_in{t}") for t in range(T)]
        small_in, edge_in = sem("small_in"), sem("edge_in")
        c_set, consts = sem("c_set"), sem("consts")
        v_step = sem("v_step")
        ln_var, ln_sd, xn_done = sem("ln_var"), sem("ln_sd"), sem("xn_done")
        xT_done, xT_hi, xT_lo = sem("xT_done"), sem("xT_hi"), sem("xT_lo")
        gate_hi, gate_lo = sem("gate_hi"), sem("gate_lo")
        sp_ready, sp_exp, sp_ln = sem("sp_ready"), sem("sp_exp"), sem("sp_ln")
        erow_done, pid_done, dup_done = sem("erow_done"), sem("pid_done"), sem("dup_done")
        hot_done, hot_used, mask_sum, mask_done = sem("hot_done"), sem("hot_used"), sem("mask_sum"), sem("mask_done")
        code_done = sem("code_done")
        proj_done, proj_hi, proj_lo = sem("proj_done"), sem("proj_hi"), sem("proj_lo")
        v2_done, v2_hi, v2_lo = sem("v2_done"), sem("v2_hi"), sem("v2_lo")
        s_done, sm_done, exp_done, rec_done, p_done = sem("s_done"), sem("sm_done"), sem("exp_done"), sem("rec_done"), sem("p_done")
        pT_done, pT_hi, pT_lo = sem("pT_done"), sem("pT_hi"), sem("pT_lo")
        pv_done, out_hi, out_lo = sem("pv_done"), sem("out_hi"), sem("out_lo")
        res_bo, wo_done = sem("res_bo"), sem("wo_done")
        logits_done, score_done, score_turned = sem("logits_done"), sem("score_done"), sem("score_turned")
        sel_done, count_done, route_done = sem("sel_done"), sem("count_done"), sem("route_done")
        gu_s_done, sig_s, silu_s = sem("gu_s_done"), sem("sig_s"), sem("silu_s")
        xn2_stored, table_in, idx_in = sem("xn2_stored"), sem("table_in"), sem("idx_in")
        idx_set, held_done, xg_in = sem("idx_set"), sem("held_done"), sem("xg_in")
        xg_done, xg_hi, xg_lo = sem("xg_done"), sem("xg_hi"), sem("xg_lo")
        gu_done, sig_done, mul_done, act_done = sem("gu_done"), sem("sig_done"), sem("mul_done"), sem("act_done")
        aT_done, aT_hi, aT_lo = sem("aT_done"), sem("aT_hi"), sem("aT_lo")
        y_done, y_out_a, y_out_v, y_free = sem("y_done"), sem("y_out_a"), sem("y_out_v"), sem("y_free")
        s_hi, s_lo, down_done = sem("s_hi"), sem("s_lo"), sem("down_done")
        back_in = [sem(f"back_in{k}") for k in range(TOP)]
        y_fill = sem("y_fill")
        sum_done, out_ready, out_stored = sem("sum_done"), sem("out_ready"), sem("out_stored")

        counts = {"proj_done": proj_done, "piece_used": piece_used, "v2_done": v2_done, "wo_done": wo_done,
                  "gu_s_done": gu_s_done}

        def buf(slot):
            return ring[:, slot:slot + 3].rearrange("p s h n -> p (s h n)").rearrange(
                "p (h c n) -> p h c n", h=2, c=C)

        xnT = buf(BUF_A)
        outT = buf(BUF_A)
        vT = buf(BUF_B)
        qT = buf(BUF_B)
        mk_i = [rows[:, t, 0:NODES].bitcast(I32) for t in range(T)]
        mk_t = [rows[:, t, NODES:2 * NODES] for t in range(T)]
        v2 = ring[:, BUF_C:BUF_C + 3].rearrange("p s h n -> p (s h n)").rearrange(
            "p (h t n) -> p h t n", h=2, t=T)
        xn2T = buf(BUF_C)
        kT = buf(BUF_D)
        innerT = buf(1)

        def hi(p):
            return ring[:, piece_slot(p), 0, :]

        def lo(p):
            return ring[:, piece_slot(p), 1, :]

        def f32(ap):
            return ap.bitcast(F32)

        V0, Q0, K0, PAIR0 = 0, 8, 16, 24

        def wo_bank(t, half):
            return 2 * t + half if t or half else 6

        block = ctx.enter_context(nc.Block())

        def each_block(eng, e, body):
            j0 = eng.value_load(blk_i[0:1, 0, bass.ds(e, 1)], min_val=0, max_val=MAX_BLOCKS - 1)
            last = eng.value_load(blk_i[0:1, 1, bass.ds(e, 1)], min_val=0, max_val=MAX_BLOCKS - 1)
            with eng.If(j0 < last):
                with eng.Fori(j0, last) as j:
                    body(j, False)
            body(last, True)

        @block.sync
        def _(sp):
            for t in range(T):
                sp.dma_start(res[:, t, :], x[t * P:(t + 1) * P, :]).then_inc(x_in[t], 16)
            sp.dma_start(ecol_i[:], edge_cols).then_inc(edge_in, 16)
            sp.dma_start(erow_i[:], edge_rows).then_inc(edge_in, 16)
            sp.dma_start(raw[:, 0, :], weights[0]).then_inc(raw_in[0], 16)
            sp.dma_start(bias[:], biases).then_inc(small_in, 16)
            sp.dma_start(w_in[:, 0, :], etw.partition_broadcast(P).rearrange("p a n -> p (a n)")).then_inc(small_in, 16)
            for p in range(1, RAWS):
                sp.dma_start(raw[:, p, :], weights[p]).then_inc(raw_in[p], 16)
            sp.dma_start(gate_f[:], gate).then_inc(small_in, 16)
            sp.dma_start(gbias[:], gate_bias.partition_broadcast(P).rearrange("p a n -> p (a n)")).then_inc(small_in, 16)
            sp.dma_start(bo_b[:], bo.partition_broadcast(P).rearrange("p a n -> p (a n)")).then_inc(small_in, 16)
            with sp.Fori(1, PIECES // RAWS) as g:
                for i in range(RAWS):
                    sp.wait_ge(lo_done, RAWS * g + (i + 1 - RAWS))
                    sp.dma_start(raw[:, i, :], weights[bass.ds(RAWS * g + i, 1)].rearrange("a p n -> (a p) n")).then_inc(raw_in[i], 16)
            for t in range(T):
                sp.wait_ge(out_ready, t + 1)
                sp.dma_start(out[t * P:(t + 1) * P, :], res[:, t, :]).then_inc(out_stored, 16)
            sp.wait_ge(out_stored, 16 * T)

        @block.gpsimd
        def _(pool):
            g = nc.gpsimd
            n_set = [0]

            def put(ins):
                ins.then_inc(c_set, 1)
                n_set[0] += 1

            def affine(ap, pattern, op, fill, base, cm):
                pool.wait_ge(c_set, n_set[0])
                put(g.affine_select(out=ap, in_=ap, pattern=pattern, compare_op=op, fill=fill, base=base,
                                    channel_multiplier=cm))

            put(g.memset(eps_c[:], LN_EPS))
            put(g.memset(ident[:], 0.0))
            put(g.memset(tri[:], 1.0))
            put(g.memset(ones[:], 1.0))
            put(g.memset(lower[:], 1.0))
            put(g.memset(pid_w[:], 0.0))
            affine(ident[:], [[1, P]], ALU.not_equal, 1.0, 0, -1)
            affine(tri[:], [[1, P]], ALU.is_gt, 0.0, 0, -1)
            affine(pid_w[:], [[-2, EG], [0, P]], ALU.not_equal, float(NODES), 0, 1)
            affine(pid_w[:], [[-2, EG], [0, P]], ALU.not_equal, 1.0, -1, 1)
            put(g.iota(iota16[:], [[1, NODES]], base=0, channel_multiplier=0, allow_small_or_imprecise_dtypes=True))
            put(g.iota(pw[:], [[1, EC]], base=8, channel_multiplier=0))
            put(g.iota(kcol[:], [[1, TOP]], base=0, channel_multiplier=0, allow_small_or_imprecise_dtypes=True))
            affine(lower[:], [[1, EXPERTS + 1], [-1, EXPERTS]], ALU.is_gt, 0.0, 0, 0)
            pool.wait_ge(c_set, n_set[0])
            g.memset(dup_junk[:, 0, 0:1], 0.0).then_inc(consts, 1)

            pool.wait_ge(small_in, 80)
            for t in range(T):
                pool.wait_ge(xn_done, t + 1)
                g.tensor_tensor(res[:, t, :], res[:, t, :], bo_b[:], ALU.add).then_inc(res_bo, 1)

            def hold_wait():
                g.tensor_tensor(held[:], idx_now[:], idx_now[:], ALU.add).then_inc(held_done, 1)

            for t in range(1, T):
                pool.wait_ge(code_done, t + 1)
                for code, n in MASK_CODES:
                    put(g.tensor_scalar(mk_t[t], mk_i[t], float(code), w8[:, n:n + 1], ALU.is_equal, ALU.mult))
                    pool.wait_ge(c_set, n_set[0])
                    ins = g.tensor_tensor(mask[:, t, :], mask[:, t, :], mk_t[t], ALU.add)
                    if code == MASK_CODES[-1][0]:
                        ins.then_inc(mask_done, 1)
                    else:
                        put(ins)
                        pool.wait_ge(c_set, n_set[0])

            pool.wait_ge(out_lo, HEADS)
            g.iota(tok_i[:], [[P, T]], base=0, channel_multiplier=1).then_inc(c_set, 1)
            g.memset(zero_i[:], 0).then_inc(c_set, 1)
            n_set[0] += 2
            pool.wait_ge(c_set, n_set[0])
            pool.dma_start(token_table.rearrange("(p c) a -> p (c a)", p=P), zero_i[:]).then_inc(y_free, 16)
            for t in range(T):
                pool.wait_ge(xn_done, T + t + 1)
                pool.dma_start(xn2_dram[t * P:(t + 1) * P, :], rows[:, t, :]).then_inc(xn2_stored, 16)
            pool.wait_ge(route_done, 1)
            pool.wait_ge(y_free, 16)
            for n in range(T * TOP):
                pool.indirect_dma_start(token_table, bass.IndirectOffsetOnAxis(pos_i[:, 2, n:n + 1], 0),
                                        tok_i[:, n // TOP:n // TOP + 1], None).then_inc(table_in, 16)
            pool.wait_ge(table_in, 16 * T * TOP)
            pool.dma_start(idx[:], token_table.rearrange("(p c) a -> p (c a)", p=P)).then_inc(idx_in, 16)
            pool.wait_ge(idx_in, 16)
            pool.wait_ge(xn2_stored, 16 * T)
            g.tensor_copy(idx_now[:], idx[:, 0:1]).then_inc(idx_set, 1)
            pool.wait_ge(idx_set, 1)
            hold_wait()
            pool.indirect_dma_start(xg_raw[:], None, xn2_dram, bass.IndirectOffsetOnAxis(idx_now[:], 0)).then_inc(xg_in, 16)

            blocks = pool.value_load(blk_i[0:1, 0, EXPERTS:EXPERTS + 1], min_val=1, max_val=MAX_BLOCKS - 1)
            with pool.Fori(blocks, MAX_BLOCKS) as j:
                pool.dma_start(y_dram[bass.ds(j, 1)].rearrange("a p n -> (a p) n"), x[0:P, :]).then_inc(y_fill, 16)

            def body(j, last):
                pool.wait_ge(held_done, j + 1)
                pool.wait_ge(xg_done, 2 * j + 2)
                g.tensor_copy(idx_now[:], idx[:, bass.ds(j + 1, 1)]).then_inc(idx_set, 1)
                pool.wait_ge(idx_set, j + 2)
                hold_wait()
                pool.indirect_dma_start(xg_raw[:], None, xn2_dram,
                                        bass.IndirectOffsetOnAxis(idx_now[:], 0)).then_inc(xg_in, 16)
                pool.wait_ge(y_out_a, j + 2)
                pool.wait_ge(y_out_v, j + 2)
                pool.dma_start(y_dram[bass.ds(j, 1)].rearrange("a p n -> (a p) n"), y_sb[:]).then_inc(y_free, 16)

            with pool.Fori(0, EXPERTS) as e:
                each_block(pool, e, body)
            blocks = pool.value_load(blk_i[0:1, 0, EXPERTS:EXPERTS + 1], min_val=1, max_val=MAX_BLOCKS)
            unused = pool.value_load(blk_i[0:1, 1, EXPERTS:EXPERTS + 1], min_val=1, max_val=MAX_BLOCKS)
            pool.wait_ge(y_fill, 16 * unused)
            pool.wait_ge(held_done, blocks + 1)
            pool.wait_ge(y_free, 16 * blocks + 16)
            hold_wait()
            pool.wait_ge(lo_done, PIECES)
            y_rows = y_dram.rearrange("b p n -> (b p) n")
            for t in range(T):
                for k in range(TOP):
                    if t:
                        pool.wait_ge(sum_done, TOP * (t - 1) + k + 1)
                    pool.indirect_dma_start(raw[:, k, :], None, y_rows,
                                            bass.IndirectOffsetOnAxis(row_i[:, TOP * t + k:TOP * t + k + 1], 0)).then_inc(back_in[k], 16)

        @block.scalar
        def _(act):
            a = nc.scalar

            def split(p):
                act.wait_ge(raw_in[p % RAWS], 16 * (p // RAWS + 1))
                for name, n in slot_free_at(p):
                    act.wait_ge(counts[name], n)
                a.activation(hi(p), raw[:, p % RAWS, :], ACT.Copy).then_inc(hi_done, 1)

            def ln_root(n):
                act.wait_ge(ln_var, n + 1)
                a.activation(sd[:, n % T:n % T + 1], mv[:, n % T, 1:2], ACT.Sqrt, bias=eps_c[:, 0:1]).then_inc(ln_sd, 1)

            def xT_split(n, dst):
                t, half = n // 2 % T, n % 2
                act.wait_ge(xT_done, n + 1)
                a.activation(dst[:, 0, 4 * half:4 * half + 4, t * P:(t + 1) * P],
                             bank[6 + half][:].rearrange("p (c n) -> p c n", c=4), ACT.Copy).then_inc(xT_hi, 1)

            def proj_split(n, ps, dst, b):
                act.wait_ge(proj_done, n + 1)
                a.activation(dst, ps[:, 0:NODES], ACT.Identity, bias=b).then_inc(proj_hi, 1)

            act.wait_ge(ln_var, T)
            act.wait_ge(c_set, 1)
            a.activation(sd[:], mv[:, :, 1], ACT.Sqrt, bias=eps_c[:, 0:1]).then_inc(ln_sd, 1)
            act.wait_ge(edge_in, 32)
            a.activation(erow[:], erow_i[:], ACT.Copy).then_inc(erow_done, 1)
            for n in range(2):
                xT_split(n, xnT)
            split(0)
            for n in range(2, 2 * T):
                xT_split(n, xnT)
            for p in range(1, RAWS):
                split(p)
            act.wait_ge(small_in, 80)
            a.activation(gate_r[:, 0], gate_f[:], ACT.Copy).then_inc(gate_hi, 1)
            for i in range(4 * C):
                if i < C:
                    proj_split(V0 + i, bank[6 + i % 2], vT[:, 0, i, :], bias[:, 2, i:i + 1])
                elif i >= 2 * C:
                    n = i - C
                    dst, b = (qT, 0) if n < K0 else (kT, 1)
                    proj_split(n, bank[6 + n % 2], dst[:, 0, n % C, :], bias[:, b, n % C:n % C + 1])
                split(i + RAWS)
                if i == 2 * C - 1:
                    for b in range(6):
                        act.wait_ge(v2_done, b + 1)
                        a.activation(v2[:, 0, b // 2, 512 * (b % 2):512 * (b % 2) + 512], bank[b][:], ACT.Copy).then_inc(v2_hi, 1)
                if i == 3 * C:
                    act.wait_ge(sp_ready, 1)
                    a.activation(w_in[:, 2, :], w_in[:, 1, :], ACT.Exp).then_inc(sp_exp, 1)
                    act.wait_ge(sp_exp, 1)
                    a.activation(w_in[:, 3, :], w_in[:, 2, :], ACT.Ln, bias=1.0).then_inc(sp_ln, 1)

            act.wait_ge(mask_sum, 1)
            act.wait_ge(res_bo, T)

            def pair_split(n):
                m = n - PAIR0
                proj_split(n, bank[6], qk2[:, m // 2 % 2, m % 2, 0, :], bias[:, 3 + m % 2, m // 2:m // 2 + 1])

            for n in (PAIR0, PAIR0 + 1):
                pair_split(n)
                split(P_IQK + 4 + n - PAIR0)
            for h in range(HEADS + 1):
                if h:
                    for m in range(T):
                        act.wait_ge(pT_done, 3 * (h - 1) + m + 1)
                        a.activation(probT[:, 0, m, :], bank[3 + m][:, 0:NODES], ACT.Copy).then_inc(pT_hi, 1)
                if h < HEADS:
                    for t in range(T):
                        act.wait_ge(sm_done, 3 * h + t + 1)
                        a.activation(prob[:, h % 2, t, :], prob[:, h % 2, t, :], ACT.Exp, scale=-1.0,
                                     bias=nmax[:, h % 2, t:t + 1], accum_out=esum[:, h % 2, t:t + 1]).then_inc(exp_done, 1)
                if h < HEADS - 2:
                    pair_split(PAIR0 + 2 + h)
                    split(P_IQK + 6 + h)
                elif h < HEADS:
                    split(P_O + 4 + 2 * (h - HEADS + 2))
                    split(P_O + 5 + 2 * (h - HEADS + 2))
                if h:
                    r = 64 * ((h - 1) % 2)
                    c = (h - 1) // 2
                    act.wait_ge(pv_done, h)
                    a.activation(outT[r:r + 64, 0, c, :], bank[7][r:r + 64, 0:NODES], ACT.Identity,
                                 bias=bias[r:r + 64, 5, c:c + 1]).then_inc(out_hi, 1)
            split(P_GU)
            split(P_GU + 1)

            ln_root(T)
            xT_split(2 * T, xn2T)
            xT_split(2 * T + 1, xn2T)
            ln_root(T + 1)
            xT_split(2 * T + 2, xn2T)
            xT_split(2 * T + 3, xn2T)
            ln_root(T + 2)
            xT_split(2 * T + 4, xn2T)
            xT_split(2 * T + 5, xn2T)
            for p in range(P_GU + 2, P_GU + GU_AHEAD):
                split(p)
            act.wait_ge(logits_done, 1)
            a.activation(scoreT[:], bank[5][0:EXPERTS, 0:NODES], ACT.Sigmoid).then_inc(score_done, 1)

            def x_split(j):
                for half in range(2):
                    act.wait_ge(xg_done, 2 * j + half + 1)
                    a.activation(xgT[:, 0, 4 * half:4 * half + 4, :],
                                 bank[4 + half][:].rearrange("p (c n) -> p c n", c=4), ACT.Copy).then_inc(xg_hi, 1)

            nxt = P_GU + GU_AHEAD
            for o in range(C):
                if o == C - 1:
                    x_split(0)
                act.wait_ge(gu_s_done, 2 * o + 1)
                if o:
                    act.wait_ge(silu_s, 2 * o)
                a.activation(sig[:], bank[o % 2][:, 0:NODES], ACT.Sigmoid).then_inc(sig_s, 1)
                for _ in range(GU_SPLITS[o]):
                    split(nxt)
                    nxt += 1

            def split_at(p16, slot_of):
                r = slot_of % RAWS
                act.wait_ge(raw_in[r], p16)
                a.activation(hi(slot_of), raw[:, r, :], ACT.Copy).then_inc(hi_done, 1)

            act.wait_ge(route_done, 1)
            act.sem_inc(y_out_a, 1)
            act.wait_ge(gu_s_done, 2 * C)
            for p in range(P_EXP + GU_SLOTS, P_EXP + SLOTS):
                split(p)

            with act.Fori(0, EXPERTS // 4) as g4:
                for u in range(4):
                    q0 = P_EXP + PER_EXPERT * u

                    def loaded(p):
                        return 192 * g4 + 16 * (p // RAWS + 1)

                    def refill(i):
                        for k in i:
                            if k % 4 < 3:
                                act.wait_ge(exp_used, 36 * g4 + (9 * u + k - k // 4 + 1))
                            split_at(loaded(q0 + SLOTS + k), q0 + SLOTS + k)

                    def refill_next(i):
                        if u < 3:
                            refill(i)
                        else:
                            with act.If(g4 < EXPERTS // 4 - 1):
                                refill(i)

                    def body(j, last):
                        def sigmoid(half):
                            act.wait_ge(gu_done, 2 * j + half + 1)
                            a.activation(act_s[:, half, :], bank[half][:, 0:256], ACT.Sigmoid).then_inc(sig_done, 1)

                        def aT_split(half):
                            act.wait_ge(aT_done, 2 * j + half + 1)
                            a.activation(actT[:, 0, 2 * half:2 * half + 2, :],
                                         bank[2 + half][:, 0:256].rearrange("p (c n) -> p c n", c=2), ACT.Copy).then_inc(aT_hi, 1)

                        if last:
                            refill(range(0, 3))
                        sigmoid(0)
                        if last:
                            refill(range(3, 4))
                            refill_next(range(4, 5))
                        aT_split(0)
                        if last:
                            refill_next(range(5, 7))
                        sigmoid(1)
                        if last:
                            refill_next(range(7, 8))
                        x_split(j + 1)
                        aT_split(1)
                        if last:
                            refill_next(range(8, 11))
                        act.wait_ge(y_done, 2 * j + 2)
                        act.wait_ge(y_free, 16 * j + 16)
                        a.activation(y_sb[:, 512:1024], bank[7][:], ACT.Copy).then_inc(y_out_a, 1)
                        if last:
                            refill_next(range(11, 12))

                    each_block(act, 4 * g4 + u, body)

            for c in range(C):
                a.activation(innerT[:, 0, c, :], rows[:].rearrange("p t f -> p (t f)")[:, c * NODES:(c + 1) * NODES],
                             ACT.Copy).then_inc(s_hi, 1)

        @block.vector
        def _(dve):
            v = nc.vector
            n_step = [0]

            def step(ins):
                ins.then_inc(v_step, 1)
                n_step[0] += 1
                dve.wait_ge(v_step, n_step[0])

            def rest(dst, src, high):
                return v.tensor_tensor(dst, src, f32(high), ALU.subtract)

            def split(p):
                dve.wait_ge(hi_done, p + 1)
                rest(lo(p), raw[:, p % RAWS, :], hi(p)).then_inc(lo_done, 1)

            def newton(var, sd, s):
                r, b, c, y = (s[:, i] for i in range(4))
                step(v.reciprocal(r, sd))
                step(v.scalar_tensor_tensor(out=b, in0=var, scalar=LN_EPS, in1=r, op0=ALU.add, op1=ALU.mult))
                step(v.tensor_tensor(c, b, r, ALU.mult))
                step(v.tensor_scalar(c, c, -0.5, 1.5, ALU.mult, ALU.add))
                step(v.tensor_tensor(y, c, r, ALU.mult))

            def norm_rows(n):
                t = n % T
                xt = res[:, t, :]
                for half in range(2):
                    ins = v.bn_stats(stats[:, t, half, :], xt[:, 512 * half:512 * half + 512])
                step(ins)
                v.bn_aggr(mv[:, t, :], stats[:, t]).then_inc(ln_var, 1)
                dve.wait_ge(ln_var, n + 1)
                dve.wait_ge(ln_sd, n - T + 2)
                newton(mv[:, t, 1:2], sd[:, t:t + 1], ln_s[:, :, t:t + 1])
                v.tensor_scalar(rows[:, t, :], xt, mv[:, t, 0:1], ln_s[:, 3, t:t + 1], ALU.subtract,
                                ALU.mult).then_inc(xn_done, 1)

            def xT_split(n, dst):
                t, half = n // 2 % T, n % 2
                dve.wait_ge(xT_hi, n + 1)
                at = dst[:, :, 4 * half:4 * half + 4, t * P:(t + 1) * P]
                rest(at[:, 1], bank[6 + half][:].rearrange("p (c n) -> p c n", c=4), at[:, 0]).then_inc(xT_lo, 1)

            def proj_split(n, ps, dst, b):
                dve.wait_ge(proj_hi, n + 1)
                v.scalar_tensor_tensor(out=dst[:, 1], in0=ps[:, 0:NODES], scalar=b, in1=f32(dst[:, 0]),
                                       op0=ALU.add, op1=ALU.subtract).then_inc(proj_lo, 1)

            for t in range(T):
                dve.wait_ge(x_in[t], 16)
                for half in range(2):
                    ins = v.bn_stats(stats[:, t, half, :], res[:, t, 512 * half:512 * half + 512])
                step(ins)
                v.bn_aggr(mv[:, t, :], stats[:, t]).then_inc(ln_var, 1)
            dve.wait_ge(ln_var, T)
            dve.wait_ge(ln_sd, 1)
            newton(mv[:, :, 1], sd[:], ln_s[:])
            for t in range(T):
                v.tensor_scalar(rows[:, t, :], res[:, t, :], mv[:, t, 0:1], ln_s[:, 3, t:t + 1], ALU.subtract,
                                ALU.mult).then_inc(xn_done, 1)
            dve.wait_ge(consts, 1)
            dve.wait_ge(edge_in, 32)
            step(v.tensor_copy(ecol[:], ecol_i[:]))
            v.scalar_tensor_tensor(out=pid[:], in0=ecol[:, 0, :], scalar=float(NODES), in1=ecol[:, 1, :],
                                   op0=ALU.mult, op1=ALU.add)
            for n in range(2):
                xT_split(n, xnT)
            split(0)
            for n in range(2, 2 * T):
                xT_split(n, xnT)
            for p in range(1, RAWS):
                split(p)
            step(v.tensor_scalar(val[:], ecol[:, 2, :], 0.0, 4.0, ALU.is_equal, ALU.mult))
            step(v.tensor_tensor(val[:], val[:], ecol[:, 2, :], ALU.add))
            step(v.tensor_scalar(pw[:], pw[:], 25, None, ALU.logical_shift_left))
            step(v.tensor_tensor(val[:], val[:], pw[:].bitcast(F32), ALU.mult))
            v.tensor_scalar(ident4[:, 0, :], ident[:], 1.0, None, ALU.mult)
            v.tensor_scalar(ident4[:, 1, :], ident[:], 4.0 * 2.0 ** (28 - 127), None, ALU.mult)
            dve.wait_ge(gate_hi, 1)
            rest(gate_r[:, 1], gate_f[:], gate_r[:, 0]).then_inc(gate_lo, 1)

            def repeats(group):
                dve.wait_ge(pid_done, group + 1)
                if group:
                    dve.wait_ge(dup_done, group)
                for i in range(4):
                    c = 4 * group + i
                    ins = v.scalar_tensor_tensor(out=dup_junk[:, i, :], in0=bank[group % 6][:, P * i:P * i + P],
                                                 scalar=pid[:, c:c + 1], in1=tri[:], op0=ALU.is_equal,
                                                 op1=ALU.mult, accum_out=dup[:, c:c + 1])
                ins.then_inc(dup_done, 1)

            def onehots(s):
                if s >= 2:
                    dve.wait_ge(hot_used, s - 1)
                for i in range(4):
                    c = 4 * s + i
                    v.tensor_scalar(onehot[:, s % 2, i, 0, :], iota16[:], ecol[:, 0, c:c + 1], None, ALU.is_equal)
                    ins = v.tensor_scalar(onehot[:, s % 2, i, 1, :], iota16[:], ecol[:, 1, c:c + 1],
                                          val[:, c:c + 1], ALU.is_equal, ALU.mult)
                ins.then_inc(hot_done, 1)

            def mask_codes():
                dve.wait_ge(mask_sum, 1)
                for t in range(T):
                    top = bank[t][:, 0:NODES]
                    v.tensor_scalar(mk_i[t], top.bitcast(I32), 22, 7, ALU.logical_shift_right, ALU.bitwise_and)
                    v.tensor_scalar(mask[:, t, :], top, 0.0, ABSENT, ALU.is_equal, ALU.mult).then_inc(code_done, 1)

            for i in range(4 * C):
                if i < C:
                    proj_split(V0 + i, bank[6 + i % 2], vT[:, :, i, :], bias[:, 2, i:i + 1])
                elif i >= 2 * C:
                    n = i - C
                    dst, b = (qT, 0) if n < K0 else (kT, 1)
                    proj_split(n, bank[6 + n % 2], dst[:, :, n % C, :], bias[:, b, n % C:n % C + 1])
                split(i + RAWS)
                if i < EG // 2:
                    repeats(2 * i)
                    repeats(2 * i + 1)
                if i == EG // 2:
                    dve.wait_ge(dup_done, EG)
                    step(v.tensor_scalar(dup[:], dup[:], 0.0, None, ALU.is_equal))
                    step(v.tensor_tensor(val[:], val[:], dup[:], ALU.mult))
                    step(v.tensor_scalar(w_in[:, 1, :], w_in[:, 0, :], -1.0, None, ALU.mult))
                    v.tensor_tensor(w_in[:, 1, :], w_in[:, 0, :], w_in[:, 1, :], ALU.min).then_inc(sp_ready, 1)
                if i == 2 * C - 1:
                    for b in range(6):
                        dve.wait_ge(v2_hi, b + 1)
                        at = v2[:, :, b // 2, 512 * (b % 2):512 * (b % 2) + 512]
                        rest(at[:, 1], bank[b][:], at[:, 0]).then_inc(v2_lo, 1)
                if 2 * C <= i < 2 * C + EG:
                    onehots(i - 2 * C)
                if i == 2 * C + EG:
                    dve.wait_ge(sp_ln, 1)
                    step(v.scalar_tensor_tensor(out=w8[:], in0=w_in[:, 0, :], scalar=0.0, in1=w_in[:, 3, :],
                                                op0=ALU.max, op1=ALU.add))
                    step(v.tensor_scalar(w8[:], w8[:], 1.0 / SCALE, None, ALU.mult))
                if i == 4 * C - 2:
                    mask_codes()
                if i == 4 * C - 1:
                    dve.wait_ge(code_done, 1)
                    for code, n in MASK_CODES:
                        step(v.tensor_scalar(mk_t[0], mk_i[0], float(code), w8[:, n:n + 1], ALU.is_equal, ALU.mult))
                        step(v.tensor_tensor(mask[:, 0, :], mask[:, 0, :], mk_t[0], ALU.add))

            dve.wait_ge(res_bo, T)

            def pair_split(n):
                m = n - PAIR0
                proj_split(n, bank[6], qk2[:, m // 2 % 2, m % 2], bias[:, 3 + m % 2, m // 2:m // 2 + 1])

            for n in (PAIR0, PAIR0 + 1):
                pair_split(n)
                split(P_IQK + 4 + n - PAIR0)
            for h in range(HEADS + 1):
                if h:
                    for m in range(T):
                        dve.wait_ge(pT_hi, 3 * (h - 1) + m + 1)
                        rest(probT[:, 1, m, :], bank[3 + m][:, 0:NODES], probT[:, 0, m, :]).then_inc(pT_lo, 1)
                if h < HEADS:
                    for t in range(T):
                        dve.wait_ge(s_done, 3 * h + t + 1)
                        if h == 0 and t:
                            dve.wait_ge(mask_done, t)
                        v.tensor_tensor_reduce(out=prob[:, h % 2, t, :], in0=bank[t][:, 0:NODES], in1=mask[:, t, :],
                                               scale=-SCALE, scalar=-2.0 * ABSENT, op0=ALU.add, op1=ALU.min,
                                               accum_out=nmax[:, h % 2, t:t + 1]).then_inc(sm_done, 1)
                if h < HEADS:
                    dve.wait_ge(exp_done, 3 * h + 3)
                    v.reciprocal(erec[:, h % 2, :], esum[:, h % 2, :]).then_inc(rec_done, 1)
                    dve.wait_ge(rec_done, h + 1)
                    for t in range(T):
                        v.tensor_scalar(prob[:, h % 2, t, :], prob[:, h % 2, t, :], erec[:, h % 2, t:t + 1], None,
                                        ALU.mult).then_inc(p_done, 1)
                if h < HEADS - 2:
                    pair_split(PAIR0 + 2 + h)
                    split(P_IQK + 6 + h)
                elif h < HEADS:
                    split(P_O + 4 + 2 * (h - HEADS + 2))
                    split(P_O + 5 + 2 * (h - HEADS + 2))
                if h:
                    r = 64 * ((h - 1) % 2)
                    c = (h - 1) // 2
                    dve.wait_ge(out_hi, h)
                    v.scalar_tensor_tensor(out=outT[r:r + 64, 1, c, :], in0=bank[7][r:r + 64, 0:NODES],
                                           scalar=bias[r:r + 64, 5, c:c + 1], in1=f32(outT[r:r + 64, 0, c, :]),
                                           op0=ALU.add, op1=ALU.subtract).then_inc(out_lo, 1)
            split(P_GU)
            split(P_GU + 1)

            def second_norm(t):
                for half in range(2):
                    dve.wait_ge(wo_done, 2 * t + half + 1)
                    at = res[:, t, 512 * half:512 * half + 512]
                    ins = v.tensor_tensor(at, bank[wo_bank(t, half)][:], at, ALU.add)
                step(ins)
                norm_rows(T + t)

            def add_rows(t):
                dve.wait_ge(xn_done, T + t + 1)
                v.tensor_tensor(res[:, t, :], res[:, t, :], rows[:, t, :], ALU.add)

            second_norm(0)
            add_rows(0)
            xT_split(2 * T, xn2T)
            xT_split(2 * T + 1, xn2T)
            second_norm(1)
            add_rows(1)
            xT_split(2 * T + 2, xn2T)
            xT_split(2 * T + 3, xn2T)
            second_norm(2)
            xT_split(2 * T + 4, xn2T)
            xT_split(2 * T + 5, xn2T)
            add_rows(2)
            for p in range(P_GU + 2, P_GU + GU_AHEAD):
                split(p)

            inner = rows[:].rearrange("p t f -> p (t f)")

            def silu(o):
                dve.wait_ge(sig_s, o + 1)
                v.tensor_tensor(sig[:], bank[o % 2][:, 0:NODES], sig[:], ALU.mult).then_inc(silu_s, 1)
                dve.wait_ge(silu_s, 2 * o + 1)
                dve.wait_ge(gu_s_done, 2 * o + 2)
                if o == 0:
                    dve.wait_ge(xn2_stored, 16 * T)
                v.tensor_tensor(inner[:, o * NODES:(o + 1) * NODES], bank[2 + o % 2][:, 0:NODES], sig[:],
                                ALU.mult).then_inc(silu_s, 1)

            def ranks(n_of, width, src, rank):
                full = [P, n_of, width, width]
                ca = cmp_a[:, 0:n_of * width * width].rearrange("p (n i j) -> p n i j", i=width, j=width)
                cb = cmp_b[:, 0:n_of * width * width].rearrange("p (n i j) -> p n i j", i=width, j=width)
                of_j = src.rearrange("p (n j) -> p n j", j=width).unsqueeze(2).to_broadcast(full)
                of_i = src.rearrange("p (n j) -> p n j", j=width).unsqueeze(3).to_broadcast(full)
                v.tensor_tensor(ca, of_j, of_i, ALU.is_gt)
                step(v.tensor_tensor(cb, of_j, of_i, ALU.is_equal))
                step(v.tensor_tensor(cb, cb, lower[:, 0:width, 0:width].unsqueeze(1).to_broadcast(full), ALU.mult))
                step(v.tensor_tensor(ca, ca, cb, ALU.add))
                step(v.tensor_reduce(rank, ca, AX_X, ALU.add))

            NE = T * EXPERTS
            dve.wait_ge(score_turned, 1)
            step(v.tensor_copy(sc[:], bank[4][:, 0:T * EXPERTS]))
            step(v.tensor_tensor(sfc[:].rearrange("p (t e) -> p t e", t=T), sc[:].rearrange("p (t e) -> p t e", t=T),
                                 gbias[:].unsqueeze(1).to_broadcast([P, T, EXPERTS]), ALU.add))
            rank, keep, weight, place = rt[:, 0], rt[:, 1], rt[:, 2], rt[:, 3]
            ranks(T * GROUPS, EPG, sfc[:], rank.rearrange("p (n i) -> p n i", i=EPG))
            step(v.scalar_tensor_tensor(out=keep, in0=rank, scalar=2.0, in1=sfc[:], op0=ALU.is_lt, op1=ALU.mult))
            step(v.tensor_reduce(gsc[:, 0], keep.rearrange("p (n i) -> p n i", i=EPG), AX_X, ALU.add))
            ranks(T, GROUPS, gsc[:, 0], gsc[:, 1].rearrange("p (n i) -> p n i", i=GROUPS))
            step(v.tensor_scalar(gsc[:, 2], gsc[:, 1], 2.0, None, ALU.is_lt))
            in_group = gsc[:, 2].unsqueeze(2).to_broadcast([P, T * GROUPS, EPG])
            k3 = keep.rearrange("p (n i) -> p n i", i=EPG)
            step(v.tensor_tensor(k3, sfc[:].rearrange("p (n i) -> p n i", i=EPG), in_group, ALU.mult))
            step(v.tensor_scalar(gsc[:, 2], gsc[:, 2], 1.0e30, -1.0e30, ALU.mult, ALU.add))
            step(v.tensor_tensor(k3, k3, in_group, ALU.add))
            silu(0)
            ranks(T, EXPERTS, keep, rank.rearrange("p (n i) -> p n i", i=EXPERTS))
            v.tensor_scalar(keep, rank, float(TOP), None, ALU.is_lt).then_inc(sel_done, 1)
            dve.wait_ge(sel_done, 1)
            step(v.tensor_tensor(weight, sc[:], keep, ALU.mult))
            step(v.tensor_reduce(den[:, 0], weight.rearrange("p (t e) -> p t e", t=T), AX_X, ALU.add))
            step(v.tensor_scalar(den[:, 1], den[:, 0], 1e-20, None, ALU.add))
            step(v.reciprocal(den[:, 0], den[:, 1]))
            silu(1)
            w3 = weight.rearrange("p (t e) -> p t e", t=T)
            step(v.tensor_tensor(w3, w3, den[:, 0].unsqueeze(2).to_broadcast([P, T, EXPERTS]), ALU.mult))
            full = [P, T, TOP, EXPERTS]
            kth = cmp_a[:, 0:T * TOP * EXPERTS].rearrange("p (t k e) -> p t k e", t=T, k=TOP)
            prod = cmp_b[:, 0:T * TOP * EXPERTS].rearrange("p (t k e) -> p t k e", t=T, k=TOP)
            step(v.tensor_tensor(kth, rank.rearrange("p (t e) -> p t e", t=T).unsqueeze(2).to_broadcast(full),
                                 kcol[:].unsqueeze(1).unsqueeze(3).to_broadcast(full), ALU.is_equal))
            step(v.tensor_tensor(prod, kth, w3.unsqueeze(2).to_broadcast(full), ALU.mult))
            step(v.tensor_reduce(cw[:], prod, AX_X, ALU.add))
            step(v.tensor_scalar(cw[:], cw[:], ROUTE_SCALE, None, ALU.mult))

            def rows_of_experts():
                dve.wait_ge(count_done, 1)
                count = bank[5][:, NE:NE + EXPERTS]
                step(v.tensor_scalar(nblk[:, 0], count, float(P), 1.0, ALU.is_gt, ALU.add))
                step(v.scalar_tensor_tensor(out=nblk[:, 1], in0=count, scalar=float(2 * P), in1=nblk[:, 0],
                                            op0=ALU.is_gt, op1=ALU.add))
                full = [P, EXPERTS + 1, EXPERTS]
                pre = cmp_b[:, 0:(EXPERTS + 1) * EXPERTS].rearrange("p (i j) -> p i j", j=EXPERTS)
                step(v.tensor_tensor(pre, lower[:], nblk[:, 1].unsqueeze(1).to_broadcast(full), ALU.mult))
                step(v.tensor_reduce(first_f[:], pre, AX_X, ALU.add))
                v.tensor_copy(blk_i[:, 0], first_f[:])
                v.tensor_scalar(blk_i[:, 1, EXPERTS:EXPERTS + 1], first_f[:, EXPERTS:EXPERTS + 1], -1.0,
                                float(MAX_BLOCKS), ALU.mult, ALU.add)
                v.tensor_scalar(blk_i[:, 1, 0:EXPERTS], first_f[:, 1:EXPERTS + 1], 1.0, None, ALU.subtract)
                p3 = place.rearrange("p (t e) -> p t e", t=T)
                step(v.scalar_tensor_tensor(out=p3, in0=first_f[:, 0:EXPERTS].unsqueeze(1).to_broadcast([P, T, EXPERTS]),
                                            scalar=float(P), in1=bank[5][:, 0:NE].rearrange("p (t e) -> p t e", t=T),
                                            op0=ALU.mult, op1=ALU.add))
                step(v.tensor_tensor(prod, kth, p3.unsqueeze(2).to_broadcast([P, T, TOP, EXPERTS]), ALU.mult))
                step(v.tensor_reduce(row_f[:].rearrange("p (t k) -> p t k", t=T), prod, AX_X, ALU.add))
                step(v.tensor_copy(row_i[:], row_f[:]))
                v.tensor_scalar(pos_i[:, 0], row_i[:], P - 1, None, ALU.bitwise_and)
                step(v.tensor_scalar(pos_i[:, 1], row_i[:], 7, None, ALU.logical_shift_right))
                v.scalar_tensor_tensor(out=pos_i[:, 2], in0=pos_i[:, 0], scalar=float(IDX_COLS), in1=pos_i[:, 1],
                                       op0=ALU.mult, op1=ALU.add).then_inc(route_done, 1)

            def x_split(j):
                for half in range(2):
                    dve.wait_ge(xg_hi, 2 * j + half + 1)
                    at = xgT[:, :, 4 * half:4 * half + 4, :]
                    rest(at[:, 1], bank[4 + half][:].rearrange("p (c n) -> p c n", c=4), at[:, 0]).then_inc(xg_lo, 1)

            nxt = P_GU + GU_AHEAD
            for o in range(C):
                if o == 2:
                    rows_of_experts()
                if o == C - 1:
                    x_split(0)
                if o >= 2:
                    silu(o)
                for _ in range(GU_SPLITS[o]):
                    split(nxt)
                    nxt += 1

            def split_at(p, slot_of):
                dve.wait_ge(hi_done, p + 1)
                rest(lo(slot_of), raw[:, slot_of % RAWS, :], hi(slot_of)).then_inc(lo_done, 1)

            dve.sem_inc(y_out_v, 1)
            for p in range(P_EXP + GU_SLOTS, P_EXP + SLOTS):
                split(p)

            with dve.Fori(0, EXPERTS // 4) as g4:
                for u in range(4):
                    p0 = 48 * g4 + (P_EXP + PER_EXPERT * u)
                    q0 = P_EXP + PER_EXPERT * u

                    def refill(i):
                        for k in i:
                            split_at(p0 + (SLOTS + k), q0 + SLOTS + k)

                    def refill_next(i):
                        if u < 3:
                            refill(i)
                        else:
                            with dve.If(g4 < EXPERTS // 4 - 1):
                                refill(i)

                    def body(j, last):
                        def gated(half):
                            dve.wait_ge(sig_done, 2 * j + half + 1)
                            v.tensor_tensor(act_s[:, half, :], bank[half][:, 0:256], act_s[:, half, :],
                                            ALU.mult).then_inc(mul_done, 1)
                            dve.wait_ge(mul_done, 2 * j + half + 1)
                            v.tensor_tensor(act_r[:, 256 * half:256 * half + 256], bank[half][:, 256:512],
                                            act_s[:, half, :], ALU.mult).then_inc(act_done, 1)

                        def aT_split(half):
                            dve.wait_ge(aT_hi, 2 * j + half + 1)
                            at = actT[:, :, 2 * half:2 * half + 2, :]
                            rest(at[:, 1], bank[2 + half][:, 0:256].rearrange("p (c n) -> p c n", c=2),
                                 at[:, 0]).then_inc(aT_lo, 1)

                        if last:
                            refill(range(0, 3))
                        gated(0)
                        if last:
                            refill(range(3, 4))
                            refill_next(range(4, 5))
                        aT_split(0)
                        if last:
                            refill_next(range(5, 7))
                        gated(1)
                        if last:
                            refill_next(range(7, 8))
                        x_split(j + 1)
                        aT_split(1)
                        if last:
                            refill_next(range(8, 11))
                        dve.wait_ge(y_done, 2 * j + 1)
                        dve.wait_ge(y_free, 16 * j + 16)
                        v.tensor_copy(y_sb[:, 0:512], bank[6][:]).then_inc(y_out_v, 1)
                        if last:
                            refill_next(range(11, 12))

                    each_block(dve, 4 * g4 + u, body)

            for c in range(C):
                dve.wait_ge(s_hi, c + 1)
                rest(innerT[:, 1, c, :], inner[:, c * NODES:(c + 1) * NODES], innerT[:, 0, c, :]).then_inc(s_lo, 1)

            for t in range(T):
                for k in range(TOP):
                    n = TOP * t + k
                    dve.wait_ge(back_in[k], 16 * (t + 1))
                    v.scalar_tensor_tensor(out=res[:, t, :], in0=raw[:, k, :], scalar=cw[:, t, k:k + 1],
                                           in1=res[:, t, :], op0=ALU.mult, op1=ALU.add).then_inc(sum_done, 1)
                    dve.wait_ge(sum_done, n + 1)
                for half in range(2):
                    dve.wait_ge(down_done, 2 * t + half + 1)
                    at = res[:, t, 512 * half:512 * half + 512]
                    ins = v.tensor_tensor(at, bank[2 * t + half][:], at, ALU.add)
                ins.then_inc(out_ready, 1)

        @block.tensor
        def _(pe):
            mm = nc.tensor.matmul

            def mm3(ps, l_hi, l_lo, r_hi, r_lo, start, stop):
                mm(ps, l_hi, r_hi, start=start, stop=False)
                mm(ps, l_hi, r_lo, start=False, stop=False)
                return mm(ps, l_lo, r_hi, start=False, stop=stop)

            def xT(n, half):
                for c in range(4):
                    ins = nc.tensor.transpose(bank[6 + half][:, c * P:(c + 1) * P],
                                              rows[:, n % T, (4 * half + c) * P:(4 * half + c + 1) * P], ident[:])
                ins.then_inc(xT_done, 1)

            def pid_rows(group):
                if group >= 6:
                    pe.wait_ge(dup_done, group - 5)
                mm(bank[group % 6][:], pid_w[:, group, :], erow[:], start=True, stop=True).then_inc(pid_done, 1)

            def project(p, ps, src):
                pe.wait_ge(lo_done, p + 1)
                for c in range(C):
                    w = slice(c * P, (c + 1) * P)
                    ins = mm3(ps[:, 0:NODES], hi(p)[:, w], lo(p)[:, w], src[:, 0, c, :], src[:, 1, c, :],
                              c == 0, c == C - 1)
                return ins

            def mask_sums(s):
                pe.wait_ge(hot_done, s + 1)
                for i in range(4):
                    for t in range(T):
                        ins = mm(bank[t][:, 0:NODES], onehot[:, s % 2, i, 0, t * P:(t + 1) * P],
                                 onehot[:, s % 2, i, 1, :], start=(s == 0 and i == 0), stop=False,
                                 skip_group_check=True)
                ins.then_inc(hot_used, 1)

            pe.wait_ge(consts, 1)
            pe.wait_ge(erow_done, 1)
            for group in range(6):
                pid_rows(group)
            for t in range(T):
                pe.wait_ge(xn_done, t + 1)
                for half in range(2):
                    if t:
                        pe.wait_ge(xT_lo, 2 * t + half - 1)
                    xT(t, half)
            pe.wait_ge(xT_lo, 2 * T)
            for i in range(C):
                if 2 <= i < 5:
                    pid_rows(2 * i + 2)
                    pid_rows(2 * i + 3)
                if i >= 2:
                    pe.wait_ge(proj_lo, i - 1)
                project(P_V + i, bank[6 + i % 2], xnT).then_inc(proj_done, 1)
            pe.wait_ge(dup_done, EG)
            for c in range(C):
                pe.wait_ge(proj_lo, c + 1)
                pe.wait_ge(lo_done, P_IV + c + 1)
                for t in range(T):
                    for half in range(2):
                        w = slice(512 * half, 512 * half + 512)
                        n = slice(t * P, (t + 1) * P)
                        ins = mm3(bank[2 * t + half][:], vT[:, 0, c, n], vT[:, 1, c, n], hi(P_IV + c)[:, w],
                                  lo(P_IV + c)[:, w], c == 0, c == C - 1)
                        if c == C - 1:
                            ins.then_inc(v2_done, 1)
                if c < C - 1:
                    ins.then_inc(piece_used, 1)
            for i in range(2 * C):
                if 2 <= i < EG + 2:
                    if i == 2:
                        pe.wait_ge(v2_lo, 6)
                    mask_sums(i - 2)
                if i == EG + 2:
                    for t in range(T):
                        ins = mm(bank[t][:, t * P:(t + 1) * P], ident4[:, 0, :], ident4[:, 1, :], start=False,
                                 stop=True, skip_group_check=True)
                    ins.then_inc(mask_sum, 1)
                n = Q0 + i
                pe.wait_ge(proj_lo, n - 1)
                project(P_Q + i, bank[6 + n % 2], xnT).then_inc(proj_done, 1)

            def pair_project(m):
                n = PAIR0 + m
                pe.wait_ge(proj_lo, n if m else n - 1)
                project(P_IQK + m, bank[6], (qT, kT)[m % 2]).then_inc(proj_done, 1)

            def wo_part(t, half, chunks):
                n = slice(t * P, (t + 1) * P)
                w = slice(512 * half, 512 * half + 512)
                for c in chunks:
                    if t == half == 0:
                        pe.wait_ge(lo_done, P_O + c + 1)
                    ins = mm3(bank[wo_bank(t, half)][:], outT[:, 0, c, n], outT[:, 1, c, n], hi(P_O + c)[:, w],
                              lo(P_O + c)[:, w], c == 0, c == C - 1)
                    if c == C - 1:
                        ins.then_inc(wo_done, 1)
                    elif t == T - 1 and half:
                        ins.then_inc(piece_used, 1)

            pair_project(0)
            pair_project(1)
            for h in range(HEADS + 1):
                if h:
                    pe.wait_ge(p_done, 3 * h)
                    for m in range(T):
                        for t in range(T):
                            ins = nc.tensor.transpose(bank[3 + m][:, t * P:(t + 1) * P],
                                                      prob[:, (h - 1) % 2, t, m * P:(m + 1) * P], ident[:])
                        ins.then_inc(pT_done, 1)
                if h < HEADS:
                    pe.wait_ge(proj_lo, PAIR0 + 2 * (h // 2) + 2)
                    r = slice(64 * (h % 2), 64 * (h % 2) + 64)
                    q, k = qk2[r, h // 2 % 2, 0], qk2[r, h // 2 % 2, 1]
                    for t in range(T):
                        n = slice(t * P, (t + 1) * P)
                        mm3(bank[t][:, 0:NODES], q[:, 0, n], q[:, 1, n], k[:, 0, :], k[:, 1, :], True,
                            True).then_inc(s_done, 1)
                if h < HEADS - 2:
                    pair_project(h + 2)
                elif h < HEADS:
                    if h == HEADS - 2:
                        pe.wait_ge(proj_lo, PAIR0 + HEADS)
                    wo_part(0, 0, range(0, C - 4) if h == HEADS - 2 else range(C - 4, C - 2))
                if h:
                    c = slice((h - 1) // 2 * P, (h - 1) // 2 * P + P)
                    if h > 1:
                        pe.wait_ge(out_lo, h - 1)
                    for m in range(T):
                        pe.wait_ge(pT_lo, 3 * (h - 1) + m + 1)
                        ins = mm3(bank[7][:, 0:NODES], v2[:, 0, m, c], v2[:, 1, m, c], probT[:, 0, m, :],
                                  probT[:, 1, m, :], m == 0, m == T - 1)
                    ins.then_inc(pv_done, 1)

            def xT2(t):
                pe.wait_ge(xn_done, T + t + 1)
                for half in range(2):
                    if t:
                        pe.wait_ge(xT_lo, 2 * T + 2 * t + half - 1)
                    xT(t, half)

            pe.wait_ge(out_lo, HEADS)
            for t in range(T):
                for half in range(2):
                    if (t, half) == (0, 0):
                        wo_part(0, 0, range(C - 2, C))
                    else:
                        wo_part(t, half, range(C // 2))
                        if t and half:
                            xT2(t - 1)
                        wo_part(t, half, range(C // 2, C))
            xT2(T - 1)
            pe.wait_ge(xT_lo, 4 * T)
            pe.wait_ge(gate_lo, 1)
            for c in range(C):
                ins = mm3(bank[5][0:EXPERTS, 0:NODES], gate_r[:, 0, c, :], gate_r[:, 1, c, :], xn2T[:, 0, c, :],
                          xn2T[:, 1, c, :], c == 0, c == C - 1)
            ins.then_inc(logits_done, 1)
            def x_turn(j):
                pe.wait_ge(xg_in, 16 * j + 16)
                for half in range(2):
                    for c in range(4):
                        ins = nc.tensor.transpose(bank[4 + half][:, c * P:(c + 1) * P],
                                                  xg_raw[:, (4 * half + c) * P:(4 * half + c + 1) * P], ident[:])
                    ins.then_inc(xg_done, 1)

            for o in range(C):
                if o == C - 1:
                    pe.wait_ge(route_done, 1)
                    x_turn(0)
                if o == 2:
                    pe.wait_ge(sel_done, 1)
                    NE = T * EXPERTS
                    for t in range(T):
                        for s in range(t + 1):
                            mm(bank[5][:, t * EXPERTS:(t + 1) * EXPERTS], (tri if s == t else ones)[:],
                               rt[:, 1, s * EXPERTS:(s + 1) * EXPERTS], start=(s == 0), stop=(s == t))
                    for s in range(T):
                        ins = mm(bank[5][:, NE:NE + EXPERTS], ones[:], rt[:, 1, s * EXPERTS:(s + 1) * EXPERTS],
                                 start=(s == 0), stop=(s == T - 1))
                    ins.then_inc(count_done, 1)
                if o >= 2:
                    pe.wait_ge(silu_s, 2 * o - 2)
                for which in range(2):
                    p = P_GU + 2 * o + which
                    project(p, bank[2 * which + o % 2], xn2T).then_inc(gu_s_done, 1)
                    if p == P_GU:
                        pe.wait_ge(score_done, 1)
                        for t in range(T):
                            ins = nc.tensor.transpose(bank[4][:, t * EXPERTS:(t + 1) * EXPERTS],
                                                      scoreT[:, t * P:(t + 1) * P], ident[0:EXPERTS, 0:EXPERTS])
                        ins.then_inc(score_turned, 1)

            pe.wait_ge(silu_s, 2 * C)
            with pe.Fori(0, EXPERTS // 4) as g4:
                for u in range(4):
                    p0 = 48 * g4 + (P_EXP + PER_EXPERT * u)
                    q0 = P_EXP + PER_EXPERT * u

                    def body(j, last):
                        def turn(half):
                            pe.wait_ge(act_done, 2 * j + half + 1)
                            for c in range(2):
                                ins = nc.tensor.transpose(bank[2 + half][:, c * P:(c + 1) * P],
                                                          act_r[:, (2 * half + c) * P:(2 * half + c + 1) * P], ident[:])
                            ins.then_inc(aT_done, 1)

                        def gate_up(half, chunks):
                            for c in chunks:
                                i = 4 * half + c // 2
                                w = slice(512 * (c % 2), 512 * (c % 2) + 512)
                                if c % 2 == 0:
                                    pe.wait_ge(lo_done, p0 + (i + 1))
                                ins = mm3(bank[half][:], xgT[:, 0, c, :], xgT[:, 1, c, :], hi(q0 + i)[:, w],
                                          lo(q0 + i)[:, w], c == 0, c == C - 1)
                                if c == C - 1:
                                    ins.then_inc(gu_done, 1)
                                elif last and c % 2:
                                    ins.then_inc(exp_used, 1)

                        def down(i):
                            pe.wait_ge(lo_done, p0 + (C + i + 1))
                            for o in range(2):
                                w = slice(512 * o, 512 * o + 512)
                                ins = mm3(bank[6 + o][:], actT[:, 0, i, :], actT[:, 1, i, :], hi(q0 + C + i)[:, w],
                                          lo(q0 + C + i)[:, w], i == 0, i == IC - 1)
                                if i == IC - 1:
                                    ins.then_inc(y_done, 1)
                                elif last and o:
                                    ins.then_inc(exp_used, 1)

                        pe.wait_ge(xg_lo, 2 * j + 2)
                        gate_up(0, range(C))
                        gate_up(1, range(4))
                        turn(0)
                        gate_up(1, range(4, C))
                        x_turn(j + 1)
                        pe.wait_ge(y_out_a, j + 1)
                        pe.wait_ge(y_out_v, j + 1)
                        pe.wait_ge(aT_lo, 2 * j + 1)
                        down(0)
                        turn(1)
                        down(1)
                        pe.wait_ge(aT_lo, 2 * j + 2)
                        down(2)
                        down(3)

                    each_block(pe, 4 * g4 + u, body)

            blocks = pe.value_load(blk_i[0:1, 0, EXPERTS:EXPERTS + 1], min_val=1, max_val=MAX_BLOCKS)
            pe.wait_ge(xg_lo, 2 * blocks + 2)
            for t in range(T):
                for c in range(C):
                    if t == 0:
                        pe.wait_ge(lo_done, P_DOWN + c + 1)
                        pe.wait_ge(s_lo, c + 1)
                    n = slice(t * P, (t + 1) * P)
                    for half in range(2):
                        w = slice(512 * half, 512 * half + 512)
                        ins = mm3(bank[2 * t + half][:], innerT[:, 0, c, n], innerT[:, 1, c, n],
                                  hi(P_DOWN + c)[:, w], lo(P_DOWN + c)[:, w], c == 0, c == C - 1)
                        if c == C - 1:
                            ins.then_inc(down_done, 1)


def kernel(x, src, dst, edge_type_5, **w):
    import numpy as np
    import concourse.bacc as bacc
    from concourse.bass_utils import run_bass_kernel_spmd

    w = {k: np.asarray(v) for k, v in w.items()}

    def by_out(m):
        return m.reshape(C, P, C, P).transpose(0, 3, 2, 1).reshape(C, P, F)

    def by_in(m):
        return m.T.reshape(C, P, F)

    def mixed(a, b):
        return np.stack([a, b], 1).reshape(2 * C, P, F)

    wg = w["L0_ffn_Wg"].transpose(0, 2, 1).reshape(EXPERTS, C // 2, 2, P, 2, 1, 256)
    wu = w["L0_ffn_Wu"].transpose(0, 2, 1).reshape(EXPERTS, C // 2, 2, P, 2, 1, 256)
    gu = np.concatenate([wg, wu], 5).transpose(0, 4, 1, 3, 2, 5, 6).reshape(EXPERTS, C, P, F)
    wd = w["L0_ffn_Wd"].transpose(0, 2, 1).reshape(EXPERTS, IC, P, F)
    weights = np.concatenate([
        by_out(w["L0_gnn_wv"]), by_in(w["L0_gnn_wiv"]), by_out(w["L0_gnn_wq"]), by_out(w["L0_gnn_wk"]),
        mixed(by_out(w["L0_gnn_wiq"]), by_out(w["L0_gnn_wik"])), by_in(w["L0_gnn_wo"]),
        mixed(by_out(w["L0_ffn_Ws_g"]), by_out(w["L0_ffn_Ws_u"])),
        np.concatenate([gu, wd], 1).reshape(EXPERTS * PER_EXPERT, P, F), by_in(w["L0_ffn_Ws_d"])])
    biases = np.stack([w["L0_gnn_" + n].reshape(C, P).T for n in ("bq", "bk", "bv", "biq", "bik", "biv")], 1)
    src, dst, kind = (np.asarray(e) for e in (src, dst, edge_type_5))
    arrays = {
        "weights": weights,
        "x": np.asarray(x),
        "biases": biases,
        "bo": w["L0_gnn_bo"].reshape(1, F),
        "gate": w["L0_ffn_gate_w"].reshape(EXPERTS, C, P).transpose(2, 1, 0),
        "gate_bias": w["L0_ffn_gate_bias"].reshape(1, EXPERTS),
        "etw": w["L0_gnn_edge_type_weights"].reshape(1, 4),
        "edge_cols": np.stack([e.reshape(EC, P).T for e in (src, dst, kind)], 1),
        "edge_rows": np.stack([src.reshape(EG, 512), dst.reshape(EG, 512)], 1).reshape(2 * EG, 512),
    }
    arrays = {k: np.ascontiguousarray(v) for k, v in arrays.items()}
    nc = bacc.Bacc("TRN2", target_bir_lowering=False, num_devices=1)
    args = [nc.dram_tensor(k, v.shape, mybir.dt.from_np(v.dtype), kind="ExternalInput").ap() for k, v in arrays.items()]
    args.append(nc.dram_tensor("out", (NODES, F), F32, kind="ExternalOutput").ap())
    args.append(nc.dram_tensor("token_table", (P * IDX_COLS, 1), I32, kind="Internal").ap())
    args.append(nc.dram_tensor("xn2_dram", (NODES, F), F32, kind="Internal").ap())
    args.append(nc.dram_tensor("y_dram", (MAX_BLOCKS, P, F), F32, kind="Internal").ap())
    program(nc, *args)
    r = run_bass_kernel_spmd(nc, [arrays], core_ids=[0])
    return r.results[0]["out"]
```

```python
from contextlib import ExitStack

import concourse.bass as bass
from concourse import mybir

ALU = mybir.AluOpType
ACT = mybir.ActivationFunctionType
AX_X = mybir.AxisListType.X
F32 = mybir.dt.float32
R32 = mybir.dt.float32r
F16 = mybir.dt.float16
BF16 = mybir.dt.bfloat16
I32 = mybir.dt.int32

P = 128
NODES = 384
T = NODES // P
F = 1024
C = F // P
HEADS = 16
HD = F // HEADS
EXPERTS = 16
TOP = 4
GROUPS = 4
EPG = EXPERTS // GROUPS
INNER = 512
IC = INNER // P
EDGES = 6144
EC = EDGES // P
EG = 12
SCALE = 1.0 / HD ** 0.5
LN_EPS = 1e-5
ROUTE_SCALE = 2.5
ABSENT = -3.0e37
MAX_BLOCKS = NODES * TOP // P + EXPERTS - 1
IDX_COLS = MAX_BLOCKS + 2
MASK_CODES = ((0, 0), (2, 1), (3, 2), (4, 3))

P_V, P_IV, P_Q, P_K, P_IQK, P_O = 0, 8, 16, 24, 32, 48
P_GU, P_EXP = 56, 72
PER_EXPERT = C + IC
P_DOWN = P_EXP + EXPERTS * PER_EXPERT
PIECES = P_DOWN + C
SLOTS = 16
RAWS = 4
EXP_RAWS = PER_EXPERT
GU_AHEAD = 8
GU_SPLITS = (2, 3, 3, 1, 2, 2, 2, 2)
POOL_LO = (8, 11)
EARLY_EXP = GU_AHEAD + sum(GU_SPLITS) - 2 * C

BUF_A, BUF_B, BUF_C, BUF_D = 0, 3, 6, 9


def piece_slot(p):
    if p < P_O:
        return 12 + p % 4
    if p < P_GU:
        return (12, 13, 14, 15, 9, 10, 11, 3)[p - P_O]
    if p < P_EXP:
        return (4, 5, 3, 12, 13, 14, 15, 9, 10, 11, 0, 1, 2, 3, 4, 5)[p - P_GU]
    return (9, 10, 11, 0, 1, 2, 3, 4, 5, 6, 7, 8)[(p - P_EXP) % PER_EXPERT]


def dve_before(i):
    return i - sum(k < i for k in POOL_LO)


def raw_index(p):
    if p < P_EXP:
        return p % RAWS, p // RAWS + 1
    r, n = (p - P_EXP) % EXP_RAWS, (p - P_EXP) // EXP_RAWS + 1
    return r, n + (P_EXP // RAWS if r < RAWS else 0)


def used_at(q):
    if q < P_IV:
        return "proj_done", q + 1
    if q < P_Q:
        return ("piece_used", q - P_IV + 1) if q < P_Q - 1 else ("v2_done", 2 * T)
    if q < P_O:
        return "proj_done", q - P_Q + C + 1
    if q < P_GU:
        return ("piece_used", q - P_O + C) if q < P_GU - 1 else ("wo_done", 2 * T)
    return "gu_s_done", q - P_GU + 1


def slot_free_at(p):
    s = piece_slot(p)
    earlier = [q for q in range(min(p, P_EXP)) if piece_slot(q) == s]
    waits = [used_at(earlier[-1])] if earlier else []
    if P_O <= p:
        if s in (3, 4, 5, 9, 10, 11):
            waits.append(used_at(P_O - 1))
        if s in (0, 1, 2):
            waits.append(used_at(P_GU - 1))
        if s in (6, 7, 8):
            waits.append(used_at(P_EXP - 1))
    return waits


def program(nc, weights, x, biases, bo, gate, gate_bias, etw, edge_cols, edge_rows, out,
            token_table, xn2_dram, y_dram):
    with ExitStack() as ctx:
        def sb(name, shape, dt, at=ctx):
            return at.enter_context(nc.sbuf_tensor(name, shape, dt))

        def sem(name):
            return ctx.enter_context(nc.semaphore(name))

        bank = [ctx.enter_context(nc.psum_tensor(f"bank{i}", [P, 512], F32)) for i in range(8)]

        ring = sb("ring", [P, PER_EXPERT, 2, F], R32)
        tail_zone = ExitStack()
        ring_tail = sb("ring_tail", [P, SLOTS - PER_EXPERT, 2, F], R32, tail_zone)
        tail_zone.close()
        raw_more = sb("raw_more", [P, EXP_RAWS - RAWS, F], F32)
        raw = sb("raw", [P, RAWS, F], F32)
        res = sb("res", [P, T, F], F32)
        rows = sb("rows", [P, T, F], F32)
        ident = sb("ident", [P, P], F32)
        tri = sb("tri", [P, P], F32)
        ones = sb("ones", [P, P], F32)
        lower = sb("lower", [P, EXPERTS + 1, EXPERTS], F32)
        kcol = sb("kcol", [P, TOP], F32)
        bias = sb("bias", [P, 6, C], F32)
        gate_f = sb("gate_f", [P, C, EXPERTS], F32)
        gate_r = sb("gate_r", [P, 2, C, EXPERTS], R32)
        gbias = sb("gbias", [P, EXPERTS], F32)
        stats = sb("stats", [P, T, 2, 6], F32)
        mv = sb("mv", [P, T, 2], F32)
        sd = sb("sd", [P, T], F32)
        ln_s = sb("ln_s", [P, 4, T], F32)
        eps_c = sb("eps_c", [P, 1], F32)
        esum = sb("esum", [P, 2, T], F32)
        erec = sb("erec", [P, 2, T], F32)
        nmax = sb("nmax", [P, 2, T], F32)
        w8 = sb("w8", [P, 4], F32)
        zone = ExitStack()
        mask = sb("mask", [P, T, NODES], F32, zone)
        early = ExitStack()
        bo_b = sb("bo_b", [P, F], F32, early)
        onehot = sb("onehot", [P, 2, 4, 2, NODES], BF16, early)
        pid_w = sb("pid_w", [2 * EG, EG, P], F16, early)
        erow_i = sb("erow_i", [2 * EG, 512], I32, early)
        erow = sb("erow", [2 * EG, 512], F16, early)
        ecol_i = sb("ecol_i", [P, 3, EC], I32, early)
        ecol = sb("ecol", [P, 3, EC], F32, early)
        pid = sb("pid", [P, EC], F32, early)
        val = sb("val", [P, EC], F32, early)
        pw = sb("pw", [P, EC], I32, early)
        dup = sb("dup", [P, EC], F32, early)
        dup_junk = sb("dup_junk", [P, 4, P], BF16, early)
        iota16 = sb("iota16", [P, NODES], F16, early)
        ident4 = sb("ident4", [P, 2, P], BF16, early)
        w_in = sb("w_in", [P, 4, 4], F32, early)
        early.close()

        attn = ExitStack()
        prob = sb("prob", [P, 2, T, NODES], F32, attn)
        probT = sb("probT", [P, 2, T, NODES], R32, attn)
        qk2 = sb("qk2", [P, 2, 2, 2, NODES], R32, attn)
        attn.close()
        zone.close()

        moe = ctx
        xg_raw = sb("xg_raw", [P, F], F32, moe)
        xgT = sb("xgT", [P, 2, C, P], R32, moe)
        act_s = sb("act_s", [P, 2, 256], F32, moe)
        act_r = sb("act_r", [P, INNER], F32, moe)
        actT = sb("actT", [P, 2, IC, P], R32, moe)
        y_sb = sb("y_sb", [P, F], F32, moe)
        sig = sb("sig", [P, NODES], F32, moe)
        cmp_a, cmp_b = xg_raw, y_sb
        scoreT = sb("scoreT", [EXPERTS, NODES], F32, moe)
        sc = sb("sc", [P, T * EXPERTS], F32, moe)
        sfc = sb("sfc", [P, T * EXPERTS], F32, moe)
        rt = sb("rt", [P, 6, T * EXPERTS], F32, moe)
        gsc = sb("gsc", [P, 3, T * GROUPS], F32, moe)
        den = sb("den", [P, 2, T], F32, moe)
        cw = sb("cw", [P, T, TOP], F32, moe)
        nblk = sb("nblk", [P, 2, EXPERTS], F32, moe)
        first_f = sb("first_f", [P, EXPERTS + 1], F32, moe)
        blk_i = sb("blk_i", [P, 2, EXPERTS + 1], I32, moe)
        row_f = sb("row_f", [P, T * TOP], F32, moe)
        row_i = sb("row_i", [P, T * TOP], I32, moe)
        pos_i = sb("pos_i", [P, 3, T * TOP], I32, moe)
        tok_i = sb("tok_i", [P, T], I32, moe)
        zero_i = sb("zero_i", [P, IDX_COLS], I32, moe)
        idx = sb("idx", [P, IDX_COLS], I32, moe)
        idx_now = sb("idx_now", [P, 1], I32, moe)
        held = sb("held", [P, 1], I32, moe)

        raw_in = [sem(f"raw_in{i}") for i in range(EXP_RAWS)]
        hi_done, lo_done, lo_pool = sem("hi_done"), sem("lo_done"), sem("lo_pool")
        piece_used, exp_used = sem("piece_used"), sem("exp_used")
        x_in = [sem(f"x_in{t}") for t in range(T)]
        small_in, edge_in = sem("small_in"), sem("edge_in")
        c_set, consts = sem("c_set"), sem("consts")
        v_step = sem("v_step")
        ln_var, ln_sd, xn_done = sem("ln_var"), sem("ln_sd"), sem("xn_done")
        xT_done, xT_hi, xT_lo = sem("xT_done"), sem("xT_hi"), sem("xT_lo")
        gate_hi, gate_lo = sem("gate_hi"), sem("gate_lo")
        sp_ready, sp_exp, sp_ln = sem("sp_ready"), sem("sp_exp"), sem("sp_ln")
        erow_done, pid_done, dup_done = sem("erow_done"), sem("pid_done"), sem("dup_done")
        hot_done, hot_used, mask_sum = sem("hot_done"), sem("hot_used"), sem("mask_sum")
        code_done = sem("code_done")
        proj_done, proj_hi, proj_lo = sem("proj_done"), sem("proj_hi"), sem("proj_lo")
        v2_done, v2_hi, v2_lo = sem("v2_done"), sem("v2_hi"), sem("v2_lo")
        s_done, sm_done, exp_done, rec_done, p_done = sem("s_done"), sem("sm_done"), sem("exp_done"), sem("rec_done"), sem("p_done")
        pT_done, pT_hi, pT_lo = sem("pT_done"), sem("pT_hi"), sem("pT_lo")
        pv_done, out_hi, out_lo = sem("pv_done"), sem("out_hi"), sem("out_lo")
        res_bo, wo_done = sem("res_bo"), sem("wo_done")
        logits_done, score_done, score_turned = sem("logits_done"), sem("score_done"), sem("score_turned")
        sel_done, count_done, route_done = sem("sel_done"), sem("count_done"), sem("route_done")
        gu_s_done, sig_s, silu_s = sem("gu_s_done"), sem("sig_s"), sem("silu_s")
        xn2_stored, table_in, idx_in = sem("xn2_stored"), sem("table_in"), sem("idx_in")
        idx_set, held_done, xg_in = sem("idx_set"), sem("held_done"), sem("xg_in")
        xg_done, xg_hi, xg_lo = sem("xg_done"), sem("xg_hi"), sem("xg_lo")
        gu_done, sig_done, mul_done, act_done = sem("gu_done"), sem("sig_done"), sem("mul_done"), sem("act_done")
        aT_done, aT_hi, aT_lo = sem("aT_done"), sem("aT_hi"), sem("aT_lo")
        y_done, y_out, y_free = sem("y_done"), sem("y_out"), sem("y_free")
        s_hi, s_lo, down_done = sem("s_hi"), sem("s_lo"), sem("down_done")
        back_in = [sem(f"back_in{k}") for k in range(TOP)]
        y_fill = sem("y_fill")
        sum_done, out_ready, out_stored = sem("sum_done"), sem("out_ready"), sem("out_stored")

        counts = {"proj_done": proj_done, "piece_used": piece_used, "v2_done": v2_done, "wo_done": wo_done,
                  "gu_s_done": gu_s_done}

        def buf(slot):
            return ring[:, slot:slot + 3].rearrange("p s h n -> p (s h n)").rearrange(
                "p (h c n) -> p h c n", h=2, c=C)

        xnT = buf(BUF_A)
        outT = buf(BUF_A)
        vT = buf(BUF_B)
        qT = buf(BUF_B)
        mk_i = [rows[:, t, 0:NODES].bitcast(I32) for t in range(T)]
        mk_t = [rows[:, t, NODES:2 * NODES] for t in range(T)]
        v2 = ring[:, BUF_C:BUF_C + 3].rearrange("p s h n -> p (s h n)").rearrange(
            "p (h t n) -> p h t n", h=2, t=T)
        xn2T = buf(BUF_C)
        kT = buf(BUF_D)
        innerT = buf(5)

        def half_slot(p, half):
            s = piece_slot(p)
            return ring[:, s, half, :] if s < PER_EXPERT else ring_tail[:, s - PER_EXPERT, half, :]

        def hi(p):
            return half_slot(p, 0)

        def lo(p):
            return half_slot(p, 1)

        def f32(ap):
            return ap.bitcast(F32)

        def raw_of(r):
            return raw[:, r, :] if r < RAWS else raw_more[:, r - RAWS, :]

        V0, Q0, K0, PAIR0 = 0, 8, 16, 24

        def pair_bank(m):
            return bank[7 if m == 1 else 6]

        def wo_bank(t, half):
            return 2 * t + half if t or half else 6

        block = ctx.enter_context(nc.Block())

        DVE_LO = PER_EXPERT - len(POOL_LO)

        def wait_piece(eng, e, i):
            if i in POOL_LO:
                eng.wait_ge(lo_pool, len(POOL_LO) * e + (POOL_LO.index(i) + 1))
            else:
                eng.wait_ge(lo_done, DVE_LO * e + (P_EXP + PER_EXPERT - DVE_LO + dve_before(i) + 1))

        def each_block(eng, e, body):
            j0 = eng.value_load(blk_i[0:1, 0, bass.ds(e, 1)], min_val=0, max_val=MAX_BLOCKS - 1)
            last = eng.value_load(blk_i[0:1, 1, bass.ds(e, 1)], min_val=0, max_val=MAX_BLOCKS - 1)
            with eng.If(j0 < last):
                with eng.Fori(j0, last) as j:
                    body(j, False)
            body(last, True)

        @block.sync
        def _(sp):
            for t in range(T):
                sp.dma_start(res[:, t, :], x[t * P:(t + 1) * P, :]).then_inc(x_in[t], 16)
            sp.dma_start(ecol_i[:], edge_cols).then_inc(edge_in, 16)
            sp.dma_start(erow_i[:], edge_rows).then_inc(edge_in, 16)
            sp.dma_start(raw[:, 0, :], weights[0]).then_inc(raw_in[0], 16)
            sp.dma_start(bias[:], biases).then_inc(small_in, 16)
            sp.dma_start(w_in[:, 0, :], etw.partition_broadcast(P).rearrange("p a n -> p (a n)")).then_inc(small_in, 16)
            for p in range(1, RAWS):
                sp.dma_start(raw[:, p, :], weights[p]).then_inc(raw_in[p], 16)
            sp.dma_start(gate_f[:], gate).then_inc(small_in, 16)
            sp.dma_start(gbias[:], gate_bias.partition_broadcast(P).rearrange("p a n -> p (a n)")).then_inc(small_in, 16)
            sp.dma_start(bo_b[:], bo.partition_broadcast(P).rearrange("p a n -> p (a n)")).then_inc(small_in, 16)
            with sp.Fori(1, P_EXP // RAWS) as g:
                for i in range(RAWS):
                    sp.wait_ge(lo_done, RAWS * g + (i + 1 - RAWS))
                    sp.dma_start(raw[:, i, :], weights[bass.ds(RAWS * g + i, 1)].rearrange("a p n -> (a p) n")).then_inc(raw_in[i], 16)
            for i in range(EXP_RAWS):
                if i < RAWS:
                    sp.wait_ge(lo_done, P_EXP + i + 1 - RAWS)
                else:
                    last_use = [p for p in range(P_GU, P_EXP) if piece_slot(p) == 12 + (i - RAWS) // 2][-1]
                    sp.wait_ge(gu_s_done, last_use - P_GU + 1)
                sp.dma_start(raw_of(i), weights[P_EXP + i]).then_inc(raw_in[i], 16)
            with sp.Fori(0, EXPERTS - 1) as e:
                for i in range(EXP_RAWS):
                    wait_piece(sp, e, i)
                    sp.dma_start(raw_of(i), weights[bass.ds(PER_EXPERT * e + (P_EXP + PER_EXPERT + i), 1)].rearrange(
                        "a p n -> (a p) n")).then_inc(raw_in[i], 16)
            for i in range(C):
                wait_piece(sp, EXPERTS - 1, i)
                sp.dma_start(raw_of(i), weights[P_DOWN + i]).then_inc(raw_in[i], 16)
            for t in range(T):
                sp.wait_ge(out_ready, t + 1)
                sp.dma_start(out[t * P:(t + 1) * P, :], res[:, t, :]).then_inc(out_stored, 16)
            sp.wait_ge(out_stored, 16 * T)

        @block.gpsimd
        def _(pool):
            g = nc.gpsimd
            n_set = [0]

            def put(ins):
                ins.then_inc(c_set, 1)
                n_set[0] += 1

            def affine(ap, pattern, op, fill, base, cm):
                pool.wait_ge(c_set, n_set[0])
                put(g.affine_select(out=ap, in_=ap, pattern=pattern, compare_op=op, fill=fill, base=base,
                                    channel_multiplier=cm))

            put(g.memset(eps_c[:], LN_EPS))
            put(g.memset(ident[:], 0.0))
            put(g.memset(tri[:], 1.0))
            put(g.memset(ones[:], 1.0))
            put(g.memset(lower[:], 1.0))
            put(g.memset(pid_w[:], 0.0))
            affine(ident[:], [[1, P]], ALU.not_equal, 1.0, 0, -1)
            affine(tri[:], [[1, P]], ALU.is_gt, 0.0, 0, -1)
            affine(pid_w[:], [[-2, EG], [0, P]], ALU.not_equal, float(NODES), 0, 1)
            affine(pid_w[:], [[-2, EG], [0, P]], ALU.not_equal, 1.0, -1, 1)
            put(g.iota(iota16[:], [[1, NODES]], base=0, channel_multiplier=0, allow_small_or_imprecise_dtypes=True))
            put(g.iota(pw[:], [[1, EC]], base=8, channel_multiplier=0))
            put(g.iota(kcol[:], [[1, TOP]], base=0, channel_multiplier=0, allow_small_or_imprecise_dtypes=True))
            affine(lower[:], [[1, EXPERTS + 1], [-1, EXPERTS]], ALU.is_gt, 0.0, 0, 0)
            pool.wait_ge(c_set, n_set[0])
            g.memset(dup_junk[:, 0, 0:1], 0.0).then_inc(consts, 1)

            pool.wait_ge(small_in, 80)
            for t in range(T):
                pool.wait_ge(xn_done, t + 1)
                g.tensor_tensor(res[:, t, :], res[:, t, :], bo_b[:], ALU.add).then_inc(res_bo, 1)

            def hold_wait():
                g.tensor_tensor(held[:], idx_now[:], idx_now[:], ALU.add).then_inc(held_done, 1)

            for j in range(EXPERTS, MAX_BLOCKS):
                pool.dma_start(y_dram[j], x[0:P, :]).then_inc(y_fill, 16)

            pool.wait_ge(lo_done, P_O + 4)
            for p in range(P_O + 4, P_O + C):
                pool.wait_ge(hi_done, p + 1)
                g.tensor_tensor(lo(p), raw_of(raw_index(p)[0]), f32(hi(p)), ALU.subtract).then_inc(lo_done, 1)

            pool.wait_ge(out_lo, HEADS)
            g.iota(tok_i[:], [[P, T]], base=0, channel_multiplier=1).then_inc(c_set, 1)
            g.memset(zero_i[:], 0).then_inc(c_set, 1)
            n_set[0] += 2
            pool.wait_ge(c_set, n_set[0])
            pool.dma_start(token_table.rearrange("(p c) a -> p (c a)", p=P), zero_i[:]).then_inc(y_free, 16)
            for t in range(T):
                pool.wait_ge(xn_done, T + t + 1)
                pool.dma_start(xn2_dram[t * P:(t + 1) * P, :], rows[:, t, :]).then_inc(xn2_stored, 16)
            pool.wait_ge(route_done, 1)
            pool.wait_ge(y_fill, 16 * (MAX_BLOCKS - EXPERTS))
            pool.wait_ge(y_free, 16)
            for n in range(T * TOP):
                pool.indirect_dma_start(token_table, bass.IndirectOffsetOnAxis(pos_i[:, 2, n:n + 1], 0),
                                        tok_i[:, n // TOP:n // TOP + 1], None).then_inc(table_in, 16)
            pool.wait_ge(table_in, 16 * T * TOP)
            pool.dma_start(idx[:], token_table.rearrange("(p c) a -> p (c a)", p=P)).then_inc(idx_in, 16)
            pool.wait_ge(idx_in, 16)
            pool.wait_ge(xn2_stored, 16 * T)
            for j in range(2):
                if j:
                    pool.wait_ge(held_done, 1)
                    pool.wait_ge(xg_done, 2)
                g.tensor_copy(idx_now[:], idx[:, j:j + 1]).then_inc(idx_set, 1)
                pool.wait_ge(idx_set, j + 1)
                hold_wait()
                pool.indirect_dma_start(xg_raw[:], None, xn2_dram, bass.IndirectOffsetOnAxis(idx_now[:], 0)).then_inc(xg_in, 16)

            def split(e, k):
                with pool.If(e < EXPERTS - 1):
                    pool.wait_ge(hi_done, PER_EXPERT * e + (P_EXP + PER_EXPERT + k + 1))
                    g.tensor_tensor(lo(P_EXP + k), raw_of(k), f32(hi(P_EXP + k)), ALU.subtract).then_inc(lo_pool, 1)

            def body(e, j, last):
                pool.wait_ge(held_done, j + 2)
                pool.wait_ge(xg_done, 2 * j + 4)
                g.tensor_copy(idx_now[:], idx[:, bass.ds(j + 2, 1)]).then_inc(idx_set, 1)
                pool.wait_ge(idx_set, j + 3)
                hold_wait()
                pool.indirect_dma_start(xg_raw[:], None, xn2_dram,
                                        bass.IndirectOffsetOnAxis(idx_now[:], 0)).then_inc(xg_in, 16)
                if last:
                    split(e, POOL_LO[0])
                pool.wait_ge(y_out, j + 2)
                pool.dma_start(y_dram[bass.ds(j, 1)].rearrange("a p n -> (a p) n"), y_sb[:]).then_inc(y_free, 16)
                if last:
                    split(e, POOL_LO[1])

            pool.sem_inc(lo_pool, len(POOL_LO))
            with pool.Fori(0, EXPERTS) as e:
                each_block(pool, e, lambda j, last: body(e, j, last))
            blocks = pool.value_load(blk_i[0:1, 0, EXPERTS:EXPERTS + 1], min_val=1, max_val=MAX_BLOCKS)
            pool.wait_ge(held_done, blocks + 2)
            pool.wait_ge(y_free, 16 * blocks + 16)
            hold_wait()
            for i in range(TOP):
                wait_piece(pool, EXPERTS, i)
            y_rows = y_dram.rearrange("b p n -> (b p) n")
            for t in range(T):
                for k in range(TOP):
                    if t:
                        pool.wait_ge(sum_done, TOP * (t - 1) + k + 1)
                    pool.indirect_dma_start(raw[:, k, :], None, y_rows,
                                            bass.IndirectOffsetOnAxis(row_i[:, TOP * t + k:TOP * t + k + 1], 0)).then_inc(back_in[k], 16)

        @block.scalar
        def _(act):
            a = nc.scalar

            def split(p):
                r, n = raw_index(p)
                act.wait_ge(raw_in[r], 16 * n)
                for name, n in slot_free_at(p):
                    act.wait_ge(counts[name], n)
                a.activation(hi(p), raw_of(r), ACT.Copy).then_inc(hi_done, 1)

            def ln_root(n):
                act.wait_ge(ln_var, n + 1)
                a.activation(sd[:, n % T:n % T + 1], mv[:, n % T, 1:2], ACT.Sqrt, bias=eps_c[:, 0:1]).then_inc(ln_sd, 1)

            def xT_split(n, dst):
                t, half = n // 2 % T, n % 2
                act.wait_ge(xT_done, n + 1)
                a.activation(dst[:, 0, 4 * half:4 * half + 4, t * P:(t + 1) * P],
                             bank[6 + half][:].rearrange("p (c n) -> p c n", c=4), ACT.Copy).then_inc(xT_hi, 1)

            def proj_split(n, ps, dst, b):
                act.wait_ge(proj_done, n + 1)
                a.activation(dst, ps[:, 0:NODES], ACT.Identity, bias=b).then_inc(proj_hi, 1)

            act.wait_ge(ln_var, T)
            act.wait_ge(c_set, 1)
            a.activation(sd[:], mv[:, :, 1], ACT.Sqrt, bias=eps_c[:, 0:1]).then_inc(ln_sd, 1)
            act.wait_ge(edge_in, 32)
            a.activation(erow[:], erow_i[:], ACT.Copy).then_inc(erow_done, 1)
            for n in range(2):
                xT_split(n, xnT)
            split(0)
            for n in range(2, 2 * T):
                xT_split(n, xnT)
            for p in range(1, RAWS):
                split(p)
            act.wait_ge(small_in, 80)
            a.activation(gate_r[:, 0], gate_f[:], ACT.Copy).then_inc(gate_hi, 1)
            for i in range(4 * C):
                if i < C:
                    proj_split(V0 + i, bank[6 + i % 2], vT[:, 0, i, :], bias[:, 2, i:i + 1])
                elif i >= 2 * C:
                    n = i - C
                    dst, b = (qT, 0) if n < K0 else (kT, 1)
                    proj_split(n, bank[6 + n % 2], dst[:, 0, n % C, :], bias[:, b, n % C:n % C + 1])
                split(i + RAWS)
                if i == 2 * C - 1:
                    for b in range(6):
                        act.wait_ge(v2_done, b + 1)
                        a.activation(v2[:, 0, b // 2, 512 * (b % 2):512 * (b % 2) + 512], bank[b][:], ACT.Copy).then_inc(v2_hi, 1)
                if i == 2 * C + 4:
                    act.wait_ge(sp_ready, 1)
                    a.activation(w_in[:, 2, :], w_in[:, 1, :], ACT.Exp).then_inc(sp_exp, 1)
                    act.wait_ge(sp_exp, 1)
                    a.activation(w_in[:, 3, :], w_in[:, 2, :], ACT.Ln, bias=1.0).then_inc(sp_ln, 1)

            act.wait_ge(mask_sum, 1)
            act.wait_ge(res_bo, T)

            def pair_split(n):
                m = n - PAIR0
                proj_split(n, pair_bank(m), qk2[:, m // 2 % 2, m % 2, 0, :], bias[:, 3 + m % 2, m // 2:m // 2 + 1])

            for n in (PAIR0, PAIR0 + 1):
                pair_split(n)
                split(P_IQK + 4 + n - PAIR0)
            for h in range(HEADS + 1):
                if h:
                    for m in range(T):
                        act.wait_ge(pT_done, 3 * (h - 1) + m + 1)
                        a.activation(probT[:, 0, m, :], bank[3 + m][:, 0:NODES], ACT.Copy).then_inc(pT_hi, 1)
                if h < HEADS:
                    for t in range(T):
                        act.wait_ge(sm_done, 3 * h + t + 1)
                        a.activation(prob[:, h % 2, t, :], prob[:, h % 2, t, :], ACT.Exp, scale=-1.0,
                                     bias=nmax[:, h % 2, t:t + 1], accum_out=esum[:, h % 2, t:t + 1]).then_inc(exp_done, 1)
                if h < HEADS - 2:
                    pair_split(PAIR0 + 2 + h)
                    split(P_IQK + 6 + h)
                elif h < HEADS:
                    split(P_O + 4 + 2 * (h - HEADS + 2))
                    split(P_O + 5 + 2 * (h - HEADS + 2))
                if h:
                    r = 64 * ((h - 1) % 2)
                    c = (h - 1) // 2
                    act.wait_ge(pv_done, h)
                    a.activation(outT[r:r + 64, 0, c, :], bank[7][r:r + 64, 0:NODES], ACT.Identity,
                                 bias=bias[r:r + 64, 5, c:c + 1]).then_inc(out_hi, 1)
            split(P_GU)
            split(P_GU + 1)

            ln_root(T)
            xT_split(2 * T, xn2T)
            xT_split(2 * T + 1, xn2T)
            ln_root(T + 1)
            xT_split(2 * T + 2, xn2T)
            xT_split(2 * T + 3, xn2T)
            ln_root(T + 2)
            xT_split(2 * T + 4, xn2T)
            xT_split(2 * T + 5, xn2T)
            for p in range(P_GU + 2, P_GU + GU_AHEAD):
                split(p)
            act.wait_ge(logits_done, 1)
            a.activation(scoreT[:], bank[5][0:EXPERTS, 0:NODES], ACT.Sigmoid).then_inc(score_done, 1)

            def x_split(j):
                for half in range(2):
                    act.wait_ge(xg_done, 2 * j + half + 1)
                    a.activation(xgT[:, 0, 4 * half:4 * half + 4, :],
                                 bank[4 + half][:].rearrange("p (c n) -> p c n", c=4), ACT.Copy).then_inc(xg_hi, 1)

            nxt = P_GU + GU_AHEAD
            for o in range(C):
                act.wait_ge(gu_s_done, 2 * o + 1)
                if o:
                    act.wait_ge(silu_s, 2 * o)
                a.activation(sig[:], bank[o % 2][:, 0:NODES], ACT.Sigmoid).then_inc(sig_s, 1)
                if o == C - 1:
                    x_split(0)
                for _ in range(GU_SPLITS[o]):
                    split(nxt)
                    nxt += 1

            act.wait_ge(route_done, 1)
            act.sem_inc(y_out, 1)
            act.wait_ge(gu_s_done, 2 * C)
            for p in range(P_EXP + EARLY_EXP, P_EXP + PER_EXPERT):
                split(p)

            with act.Fori(0, EXPERTS) as e:

                def refill(pieces):
                    for k in pieces:
                        if k % 4 < 3:
                            act.wait_ge(exp_used, 9 * e + (k - k // 4 + 1))
                        r, n = raw_index(P_EXP + PER_EXPERT + k)
                        act.wait_ge(raw_in[r], 16 * e + 16 * n)
                        a.activation(hi(P_EXP + k), raw_of(r), ACT.Copy).then_inc(hi_done, 1)

                def refill_expert(pieces):
                    with act.If(e < EXPERTS - 1):
                        refill(pieces)

                def body(j, last):
                    def sigmoid(half):
                        act.wait_ge(gu_done, 2 * j + half + 1)
                        a.activation(act_s[:, half, :], bank[half][:, 0:256], ACT.Sigmoid).then_inc(sig_done, 1)

                    def aT_split(half):
                        act.wait_ge(aT_done, 2 * j + half + 1)
                        a.activation(actT[:, 0, 2 * half:2 * half + 2, :],
                                     bank[2 + half][:, 0:256].rearrange("p (c n) -> p c n", c=2), ACT.Copy).then_inc(aT_hi, 1)

                    if last:
                        refill(range(0, 3))
                    sigmoid(0)
                    if last:
                        refill(range(3, 5))
                    aT_split(0)
                    if last:
                        refill(range(5, 7))
                    sigmoid(1)
                    if last:
                        refill(range(7, 8))
                    aT_split(1)
                    x_split(j + 1)
                    if last:
                        refill_expert(range(8, 11))
                    act.wait_ge(y_done, 2 * j + 2)
                    act.wait_ge(y_free, 16 * j + 16)
                    a.activation(y_sb[:, 0:512], bank[6][:], ACT.Copy)
                    a.activation(y_sb[:, 512:1024], bank[7][:], ACT.Copy).then_inc(y_out, 1)
                    if last:
                        refill_expert(range(11, 12))

                each_block(act, e, body)

            for c in range(C):
                a.activation(innerT[:, 0, c, :], rows[:].rearrange("p t f -> p (t f)")[:, c * NODES:(c + 1) * NODES],
                             ACT.Copy).then_inc(s_hi, 1)

        @block.vector
        def _(dve):
            v = nc.vector
            n_step = [0]

            def step(ins):
                ins.then_inc(v_step, 1)
                n_step[0] += 1
                dve.wait_ge(v_step, n_step[0])

            def rest(dst, src, high):
                return v.tensor_tensor(dst, src, f32(high), ALU.subtract)

            def split(p):
                dve.wait_ge(hi_done, p + 1)
                rest(lo(p), raw_of(raw_index(p)[0]), hi(p)).then_inc(lo_done, 1)

            def newton(var, sd, s):
                r, b, c, y = (s[:, i] for i in range(4))
                step(v.reciprocal(r, sd))
                step(v.scalar_tensor_tensor(out=b, in0=var, scalar=LN_EPS, in1=r, op0=ALU.add, op1=ALU.mult))
                step(v.tensor_tensor(c, b, r, ALU.mult))
                step(v.tensor_scalar(c, c, -0.5, 1.5, ALU.mult, ALU.add))
                step(v.tensor_tensor(y, c, r, ALU.mult))

            def norm_rows(n):
                t = n % T
                xt = res[:, t, :]
                for half in range(2):
                    ins = v.bn_stats(stats[:, t, half, :], xt[:, 512 * half:512 * half + 512])
                step(ins)
                v.bn_aggr(mv[:, t, :], stats[:, t]).then_inc(ln_var, 1)
                dve.wait_ge(ln_var, n + 1)
                dve.wait_ge(ln_sd, n - T + 2)
                newton(mv[:, t, 1:2], sd[:, t:t + 1], ln_s[:, :, t:t + 1])
                v.tensor_scalar(rows[:, t, :], xt, mv[:, t, 0:1], ln_s[:, 3, t:t + 1], ALU.subtract,
                                ALU.mult).then_inc(xn_done, 1)

            def xT_split(n, dst):
                t, half = n // 2 % T, n % 2
                dve.wait_ge(xT_hi, n + 1)
                at = dst[:, :, 4 * half:4 * half + 4, t * P:(t + 1) * P]
                rest(at[:, 1], bank[6 + half][:].rearrange("p (c n) -> p c n", c=4), at[:, 0]).then_inc(xT_lo, 1)

            def proj_split(n, ps, dst, b):
                dve.wait_ge(proj_hi, n + 1)
                v.scalar_tensor_tensor(out=dst[:, 1], in0=ps[:, 0:NODES], scalar=b, in1=f32(dst[:, 0]),
                                       op0=ALU.add, op1=ALU.subtract).then_inc(proj_lo, 1)

            for t in range(T):
                dve.wait_ge(x_in[t], 16)
                for half in range(2):
                    ins = v.bn_stats(stats[:, t, half, :], res[:, t, 512 * half:512 * half + 512])
                step(ins)
                v.bn_aggr(mv[:, t, :], stats[:, t]).then_inc(ln_var, 1)
            dve.wait_ge(ln_var, T)
            dve.wait_ge(ln_sd, 1)
            newton(mv[:, :, 1], sd[:], ln_s[:])
            for t in range(T):
                v.tensor_scalar(rows[:, t, :], res[:, t, :], mv[:, t, 0:1], ln_s[:, 3, t:t + 1], ALU.subtract,
                                ALU.mult).then_inc(xn_done, 1)
            dve.wait_ge(consts, 1)
            dve.wait_ge(edge_in, 32)
            step(v.tensor_copy(ecol[:], ecol_i[:]))
            v.scalar_tensor_tensor(out=pid[:], in0=ecol[:, 0, :], scalar=float(NODES), in1=ecol[:, 1, :],
                                   op0=ALU.mult, op1=ALU.add)
            for n in range(2):
                xT_split(n, xnT)
            split(0)
            for n in range(2, 2 * T):
                xT_split(n, xnT)
            for p in range(1, RAWS):
                split(p)
            step(v.tensor_scalar(val[:], ecol[:, 2, :], 0.0, 4.0, ALU.is_equal, ALU.mult))
            step(v.tensor_tensor(val[:], val[:], ecol[:, 2, :], ALU.add))
            step(v.tensor_scalar(pw[:], pw[:], 25, None, ALU.logical_shift_left))
            step(v.tensor_tensor(val[:], val[:], pw[:].bitcast(F32), ALU.mult))
            v.tensor_scalar(ident4[:, 0, :], ident[:], 1.0, None, ALU.mult)
            v.tensor_scalar(ident4[:, 1, :], ident[:], 4.0 * 2.0 ** (28 - 127), None, ALU.mult)
            dve.wait_ge(gate_hi, 1)
            rest(gate_r[:, 1], gate_f[:], gate_r[:, 0]).then_inc(gate_lo, 1)

            def repeats(group):
                dve.wait_ge(pid_done, group + 1)
                if group:
                    dve.wait_ge(dup_done, group)
                for i in range(4):
                    c = 4 * group + i
                    ins = v.scalar_tensor_tensor(out=dup_junk[:, i, :], in0=bank[group % 6][:, P * i:P * i + P],
                                                 scalar=pid[:, c:c + 1], in1=tri[:], op0=ALU.is_equal,
                                                 op1=ALU.mult, accum_out=dup[:, c:c + 1])
                ins.then_inc(dup_done, 1)

            def onehots(s):
                if s >= 2:
                    dve.wait_ge(hot_used, s - 1)
                for i in range(4):
                    c = 4 * s + i
                    v.tensor_scalar(onehot[:, s % 2, i, 0, :], iota16[:], ecol[:, 0, c:c + 1], None, ALU.is_equal)
                    ins = v.tensor_scalar(onehot[:, s % 2, i, 1, :], iota16[:], ecol[:, 1, c:c + 1],
                                          val[:, c:c + 1], ALU.is_equal, ALU.mult)
                ins.then_inc(hot_done, 1)

            def mask_codes():
                dve.wait_ge(mask_sum, 1)
                for t in range(T):
                    top = bank[t][:, 0:NODES]
                    v.tensor_scalar(mk_i[t], top.bitcast(I32), 22, 7, ALU.logical_shift_right, ALU.bitwise_and)
                    v.tensor_scalar(mask[:, t, :], top, 0.0, ABSENT, ALU.is_equal, ALU.mult).then_inc(code_done, 1)

            def mask_weights(t):
                dve.wait_ge(code_done, t + 1)
                for code, n in MASK_CODES:
                    step(v.tensor_scalar(mk_t[t], mk_i[t], float(code), w8[:, n:n + 1], ALU.is_equal, ALU.mult))
                    step(v.tensor_tensor(mask[:, t, :], mask[:, t, :], mk_t[t], ALU.add))

            for i in range(4 * C):
                if 2 * C + 2 <= i < 2 * C + EG // 2 + 1:
                    onehots(2 * (i - 2 * C) - 2)
                    onehots(2 * (i - 2 * C) - 1)
                if i < C:
                    proj_split(V0 + i, bank[6 + i % 2], vT[:, :, i, :], bias[:, 2, i:i + 1])
                elif i >= 2 * C:
                    n = i - C
                    dst, b = (qT, 0) if n < K0 else (kT, 1)
                    proj_split(n, bank[6 + n % 2], dst[:, :, n % C, :], bias[:, b, n % C:n % C + 1])
                split(i + RAWS)
                if i < EG // 2:
                    repeats(2 * i)
                    repeats(2 * i + 1)
                if i == EG // 2:
                    dve.wait_ge(dup_done, EG)
                    step(v.tensor_scalar(dup[:], dup[:], 0.0, None, ALU.is_equal))
                    step(v.tensor_tensor(val[:], val[:], dup[:], ALU.mult))
                    step(v.tensor_scalar(w_in[:, 1, :], w_in[:, 0, :], -1.0, None, ALU.mult))
                    v.tensor_tensor(w_in[:, 1, :], w_in[:, 0, :], w_in[:, 1, :], ALU.min).then_inc(sp_ready, 1)
                if i == 2 * C - 1:
                    for b in range(6):
                        dve.wait_ge(v2_hi, b + 1)
                        at = v2[:, :, b // 2, 512 * (b % 2):512 * (b % 2) + 512]
                        rest(at[:, 1], bank[b][:], at[:, 0]).then_inc(v2_lo, 1)
                if i in (2 * C - 2, 2 * C - 1):
                    onehots(i - 2 * C + 2)
                if i == 2 * C + EG // 2 + 1:
                    dve.wait_ge(sp_ln, 1)
                    step(v.scalar_tensor_tensor(out=w8[:], in0=w_in[:, 0, :], scalar=0.0, in1=w_in[:, 3, :],
                                                op0=ALU.max, op1=ALU.add))
                    step(v.tensor_scalar(w8[:], w8[:], 1.0 / SCALE, None, ALU.mult))
                if i == 2 * C + EG // 2 + 2:
                    mask_codes()
                if i in (4 * C - 7, 4 * C - 5, 4 * C - 3):
                    mask_weights((i - 4 * C + 7) // 2)

            dve.wait_ge(res_bo, T)

            def pair_split(n):
                m = n - PAIR0
                proj_split(n, pair_bank(m), qk2[:, m // 2 % 2, m % 2], bias[:, 3 + m % 2, m // 2:m // 2 + 1])

            for n in (PAIR0, PAIR0 + 1):
                pair_split(n)
                split(P_IQK + 4 + n - PAIR0)
            for h in range(HEADS + 1):
                if h:
                    for m in range(T):
                        dve.wait_ge(pT_hi, 3 * (h - 1) + m + 1)
                        rest(probT[:, 1, m, :], bank[3 + m][:, 0:NODES], probT[:, 0, m, :]).then_inc(pT_lo, 1)
                if h < HEADS:
                    for t in range(T):
                        dve.wait_ge(s_done, 3 * h + t + 1)
                        v.tensor_tensor_reduce(out=prob[:, h % 2, t, :], in0=bank[t][:, 0:NODES], in1=mask[:, t, :],
                                               scale=-SCALE, scalar=-2.0 * ABSENT, op0=ALU.add, op1=ALU.min,
                                               accum_out=nmax[:, h % 2, t:t + 1]).then_inc(sm_done, 1)
                if h < HEADS:
                    dve.wait_ge(exp_done, 3 * h + 3)
                    v.reciprocal(erec[:, h % 2, :], esum[:, h % 2, :]).then_inc(rec_done, 1)
                    dve.wait_ge(rec_done, h + 1)
                    for t in range(T):
                        v.tensor_scalar(prob[:, h % 2, t, :], prob[:, h % 2, t, :], erec[:, h % 2, t:t + 1], None,
                                        ALU.mult).then_inc(p_done, 1)
                if h < HEADS - 2:
                    pair_split(PAIR0 + 2 + h)
                    split(P_IQK + 6 + h)
                if h:
                    r = 64 * ((h - 1) % 2)
                    c = (h - 1) // 2
                    dve.wait_ge(out_hi, h)
                    v.scalar_tensor_tensor(out=outT[r:r + 64, 1, c, :], in0=bank[7][r:r + 64, 0:NODES],
                                           scalar=bias[r:r + 64, 5, c:c + 1], in1=f32(outT[r:r + 64, 0, c, :]),
                                           op0=ALU.add, op1=ALU.subtract).then_inc(out_lo, 1)
            dve.wait_ge(lo_done, P_O + C)
            split(P_GU)
            split(P_GU + 1)

            def second_norm(t):
                for half in range(2):
                    dve.wait_ge(wo_done, 2 * t + half + 1)
                    at = res[:, t, 512 * half:512 * half + 512]
                    ins = v.tensor_tensor(at, bank[wo_bank(t, half)][:], at, ALU.add)
                step(ins)
                norm_rows(T + t)

            def add_rows(t):
                dve.wait_ge(xn_done, T + t + 1)
                v.tensor_tensor(res[:, t, :], res[:, t, :], rows[:, t, :], ALU.add)

            second_norm(0)
            add_rows(0)
            xT_split(2 * T, xn2T)
            xT_split(2 * T + 1, xn2T)
            second_norm(1)
            add_rows(1)
            xT_split(2 * T + 2, xn2T)
            xT_split(2 * T + 3, xn2T)
            second_norm(2)
            xT_split(2 * T + 4, xn2T)
            xT_split(2 * T + 5, xn2T)
            add_rows(2)
            for p in range(P_GU + 2, P_GU + GU_AHEAD):
                split(p)

            inner = rows[:].rearrange("p t f -> p (t f)")

            def silu(o):
                dve.wait_ge(sig_s, o + 1)
                v.tensor_tensor(sig[:], bank[o % 2][:, 0:NODES], sig[:], ALU.mult).then_inc(silu_s, 1)
                dve.wait_ge(silu_s, 2 * o + 1)
                dve.wait_ge(gu_s_done, 2 * o + 2)
                if o == 0:
                    dve.wait_ge(xn2_stored, 16 * T)
                v.tensor_tensor(inner[:, o * NODES:(o + 1) * NODES], bank[2 + o % 2][:, 0:NODES], sig[:],
                                ALU.mult).then_inc(silu_s, 1)

            def ranks(n_of, width, src, rank):
                full = [P, n_of, width, width]
                ca = cmp_a[:, 0:n_of * width * width].rearrange("p (n i j) -> p n i j", i=width, j=width)
                cb = cmp_b[:, 0:n_of * width * width].rearrange("p (n i j) -> p n i j", i=width, j=width)
                of_j = src.rearrange("p (n j) -> p n j", j=width).unsqueeze(2).to_broadcast(full)
                of_i = src.rearrange("p (n j) -> p n j", j=width).unsqueeze(3).to_broadcast(full)
                v.tensor_tensor(ca, of_j, of_i, ALU.is_gt)
                step(v.tensor_tensor(cb, of_j, of_i, ALU.is_equal))
                step(v.tensor_tensor(cb, cb, lower[:, 0:width, 0:width].unsqueeze(1).to_broadcast(full), ALU.mult))
                step(v.tensor_tensor(ca, ca, cb, ALU.add))
                step(v.tensor_reduce(rank, ca, AX_X, ALU.add))

            NE = T * EXPERTS
            dve.wait_ge(score_turned, 1)
            step(v.tensor_copy(sc[:], bank[4][:, 0:T * EXPERTS]))
            step(v.tensor_tensor(sfc[:].rearrange("p (t e) -> p t e", t=T), sc[:].rearrange("p (t e) -> p t e", t=T),
                                 gbias[:].unsqueeze(1).to_broadcast([P, T, EXPERTS]), ALU.add))
            rank, keep, weight, place = rt[:, 0], rt[:, 1], rt[:, 2], rt[:, 3]
            ranks(T * GROUPS, EPG, sfc[:], rank.rearrange("p (n i) -> p n i", i=EPG))
            step(v.scalar_tensor_tensor(out=keep, in0=rank, scalar=2.0, in1=sfc[:], op0=ALU.is_lt, op1=ALU.mult))
            step(v.tensor_reduce(gsc[:, 0], keep.rearrange("p (n i) -> p n i", i=EPG), AX_X, ALU.add))
            ranks(T, GROUPS, gsc[:, 0], gsc[:, 1].rearrange("p (n i) -> p n i", i=GROUPS))
            step(v.tensor_scalar(gsc[:, 2], gsc[:, 1], 2.0, None, ALU.is_lt))
            in_group = gsc[:, 2].unsqueeze(2).to_broadcast([P, T * GROUPS, EPG])
            k3 = keep.rearrange("p (n i) -> p n i", i=EPG)
            step(v.tensor_tensor(k3, sfc[:].rearrange("p (n i) -> p n i", i=EPG), in_group, ALU.mult))
            step(v.tensor_scalar(gsc[:, 2], gsc[:, 2], 1.0e30, -1.0e30, ALU.mult, ALU.add))
            step(v.tensor_tensor(k3, k3, in_group, ALU.add))
            silu(0)
            ranks(T, EXPERTS, keep, rank.rearrange("p (n i) -> p n i", i=EXPERTS))
            v.tensor_scalar(keep, rank, float(TOP), None, ALU.is_lt).then_inc(sel_done, 1)
            dve.wait_ge(sel_done, 1)
            step(v.tensor_tensor(weight, sc[:], keep, ALU.mult))
            step(v.tensor_reduce(den[:, 0], weight.rearrange("p (t e) -> p t e", t=T), AX_X, ALU.add))
            step(v.tensor_scalar(den[:, 1], den[:, 0], 1e-20, None, ALU.add))
            step(v.reciprocal(den[:, 0], den[:, 1]))
            w3 = weight.rearrange("p (t e) -> p t e", t=T)
            step(v.tensor_tensor(w3, w3, den[:, 0].unsqueeze(2).to_broadcast([P, T, EXPERTS]), ALU.mult))
            full = [P, T, TOP, EXPERTS]
            kth = cmp_a[:, 0:T * TOP * EXPERTS].rearrange("p (t k e) -> p t k e", t=T, k=TOP)
            prod = cmp_b[:, 0:T * TOP * EXPERTS].rearrange("p (t k e) -> p t k e", t=T, k=TOP)
            step(v.tensor_tensor(kth, rank.rearrange("p (t e) -> p t e", t=T).unsqueeze(2).to_broadcast(full),
                                 kcol[:].unsqueeze(1).unsqueeze(3).to_broadcast(full), ALU.is_equal))
            step(v.tensor_tensor(prod, kth, w3.unsqueeze(2).to_broadcast(full), ALU.mult))
            step(v.tensor_reduce(cw[:], prod, AX_X, ALU.add))
            step(v.tensor_scalar(cw[:], cw[:], ROUTE_SCALE, None, ALU.mult))

            def rows_of_experts():
                dve.wait_ge(count_done, 1)
                count = bank[5][:, NE:NE + EXPERTS]
                step(v.tensor_scalar(nblk[:, 0], count, float(P), 1.0, ALU.is_gt, ALU.add))
                step(v.scalar_tensor_tensor(out=nblk[:, 1], in0=count, scalar=float(2 * P), in1=nblk[:, 0],
                                            op0=ALU.is_gt, op1=ALU.add))
                full = [P, EXPERTS + 1, EXPERTS]
                pre = cmp_b[:, 0:(EXPERTS + 1) * EXPERTS].rearrange("p (i j) -> p i j", j=EXPERTS)
                step(v.tensor_tensor(pre, lower[:], nblk[:, 1].unsqueeze(1).to_broadcast(full), ALU.mult))
                step(v.tensor_reduce(first_f[:], pre, AX_X, ALU.add))
                v.tensor_copy(blk_i[:, 0], first_f[:])
                v.tensor_scalar(blk_i[:, 1, 0:EXPERTS], first_f[:, 1:EXPERTS + 1], 1.0, None, ALU.subtract)
                p3 = place.rearrange("p (t e) -> p t e", t=T)
                step(v.scalar_tensor_tensor(out=p3, in0=first_f[:, 0:EXPERTS].unsqueeze(1).to_broadcast([P, T, EXPERTS]),
                                            scalar=float(P), in1=bank[5][:, 0:NE].rearrange("p (t e) -> p t e", t=T),
                                            op0=ALU.mult, op1=ALU.add))
                step(v.tensor_tensor(prod, kth, p3.unsqueeze(2).to_broadcast([P, T, TOP, EXPERTS]), ALU.mult))
                step(v.tensor_reduce(row_f[:].rearrange("p (t k) -> p t k", t=T), prod, AX_X, ALU.add))
                step(v.tensor_copy(row_i[:], row_f[:]))
                v.tensor_scalar(pos_i[:, 0], row_i[:], P - 1, None, ALU.bitwise_and)
                step(v.tensor_scalar(pos_i[:, 1], row_i[:], 7, None, ALU.logical_shift_right))
                v.scalar_tensor_tensor(out=pos_i[:, 2], in0=pos_i[:, 0], scalar=float(IDX_COLS), in1=pos_i[:, 1],
                                       op0=ALU.mult, op1=ALU.add).then_inc(route_done, 1)

            def x_split(j):
                for half in range(2):
                    dve.wait_ge(xg_hi, 2 * j + half + 1)
                    at = xgT[:, :, 4 * half:4 * half + 4, :]
                    rest(at[:, 1], bank[4 + half][:].rearrange("p (c n) -> p c n", c=4), at[:, 0]).then_inc(xg_lo, 1)

            rows_of_experts()
            silu(1)

            nxt = P_GU + GU_AHEAD
            for o in range(C):
                if o == C - 1:
                    x_split(0)
                if o >= 2:
                    silu(o)
                for _ in range(GU_SPLITS[o]):
                    split(nxt)
                    nxt += 1

            for p in range(P_EXP + EARLY_EXP, P_EXP + PER_EXPERT):
                split(p)

            with dve.Fori(0, EXPERTS) as e:
                p0 = PER_EXPERT * e + P_EXP

                def refill(pieces):
                    for k in (k for k in pieces if k not in POOL_LO):
                        dve.wait_ge(hi_done, p0 + (PER_EXPERT + k + 1))
                        rest(lo(P_EXP + k), raw_of(k), hi(P_EXP + k)).then_inc(lo_done, 1)

                def refill_expert(pieces):
                    with dve.If(e < EXPERTS - 1):
                        refill(pieces)

                def body(j, last):
                    def gated(half):
                        dve.wait_ge(sig_done, 2 * j + half + 1)
                        v.tensor_tensor(act_s[:, half, :], bank[half][:, 0:256], act_s[:, half, :],
                                        ALU.mult).then_inc(mul_done, 1)
                        dve.wait_ge(mul_done, 2 * j + half + 1)
                        v.tensor_tensor(act_r[:, 256 * half:256 * half + 256], bank[half][:, 256:512],
                                        act_s[:, half, :], ALU.mult).then_inc(act_done, 1)

                    def aT_split(half):
                        dve.wait_ge(aT_hi, 2 * j + half + 1)
                        at = actT[:, :, 2 * half:2 * half + 2, :]
                        rest(at[:, 1], bank[2 + half][:, 0:256].rearrange("p (c n) -> p c n", c=2),
                             at[:, 0]).then_inc(aT_lo, 1)

                    if last:
                        refill(range(0, 3))
                    gated(0)
                    if last:
                        refill(range(3, 5))
                    aT_split(0)
                    if last:
                        refill(range(5, 7))
                    gated(1)
                    if last:
                        refill(range(7, 8))
                    aT_split(1)
                    x_split(j + 1)
                    if last:
                        refill_expert(range(8, 11))

                each_block(dve, e, body)

            for c in range(C):
                dve.wait_ge(s_hi, c + 1)
                rest(innerT[:, 1, c, :], inner[:, c * NODES:(c + 1) * NODES], innerT[:, 0, c, :]).then_inc(s_lo, 1)

            for t in range(T):
                for k in range(TOP):
                    n = TOP * t + k
                    dve.wait_ge(back_in[k], 16 * (t + 1))
                    v.scalar_tensor_tensor(out=res[:, t, :], in0=raw[:, k, :], scalar=cw[:, t, k:k + 1],
                                           in1=res[:, t, :], op0=ALU.mult, op1=ALU.add).then_inc(sum_done, 1)
                    dve.wait_ge(sum_done, n + 1)
                for half in range(2):
                    dve.wait_ge(down_done, 2 * t + half + 1)
                    at = res[:, t, 512 * half:512 * half + 512]
                    ins = v.tensor_tensor(at, bank[2 * t + half][:], at, ALU.add)
                ins.then_inc(out_ready, 1)

        @block.tensor
        def _(pe):
            mm = nc.tensor.matmul

            def mm3(ps, l_hi, l_lo, r_hi, r_lo, start, stop):
                mm(ps, l_hi, r_hi, start=start, stop=False)
                mm(ps, l_hi, r_lo, start=False, stop=False)
                return mm(ps, l_lo, r_hi, start=False, stop=stop)

            def xT(n, half):
                for c in range(4):
                    ins = nc.tensor.transpose(bank[6 + half][:, c * P:(c + 1) * P],
                                              rows[:, n % T, (4 * half + c) * P:(4 * half + c + 1) * P], ident[:])
                ins.then_inc(xT_done, 1)

            def pid_rows(group):
                if group >= 6:
                    pe.wait_ge(dup_done, group - 5)
                mm(bank[group % 6][:], pid_w[:, group, :], erow[:], start=True, stop=True).then_inc(pid_done, 1)

            def project(p, ps, src):
                pe.wait_ge(lo_done, p + 1)
                for c in range(C):
                    w = slice(c * P, (c + 1) * P)
                    ins = mm3(ps[:, 0:NODES], hi(p)[:, w], lo(p)[:, w], src[:, 0, c, :], src[:, 1, c, :],
                              c == 0, c == C - 1)
                return ins

            def mask_sums(s):
                pe.wait_ge(hot_done, s + 1)
                for i in range(4):
                    for t in range(T):
                        ins = mm(bank[t][:, 0:NODES], onehot[:, s % 2, i, 0, t * P:(t + 1) * P],
                                 onehot[:, s % 2, i, 1, :], start=(s == 0 and i == 0), stop=False,
                                 skip_group_check=True)
                ins.then_inc(hot_used, 1)

            pe.wait_ge(consts, 1)
            pe.wait_ge(erow_done, 1)
            for group in range(6):
                pid_rows(group)
            for t in range(T):
                pe.wait_ge(xn_done, t + 1)
                for half in range(2):
                    if t:
                        pe.wait_ge(xT_lo, 2 * t + half - 1)
                    xT(t, half)
            pe.wait_ge(xT_lo, 2 * T)
            for i in range(C):
                if 2 <= i < 5:
                    pid_rows(2 * i + 2)
                    pid_rows(2 * i + 3)
                if i >= 2:
                    pe.wait_ge(proj_lo, i - 1)
                project(P_V + i, bank[6 + i % 2], xnT).then_inc(proj_done, 1)
            pe.wait_ge(dup_done, EG)
            for c in range(C):
                pe.wait_ge(proj_lo, c + 1)
                pe.wait_ge(lo_done, P_IV + c + 1)
                for t in range(T):
                    for half in range(2):
                        w = slice(512 * half, 512 * half + 512)
                        n = slice(t * P, (t + 1) * P)
                        ins = mm3(bank[2 * t + half][:], vT[:, 0, c, n], vT[:, 1, c, n], hi(P_IV + c)[:, w],
                                  lo(P_IV + c)[:, w], c == 0, c == C - 1)
                        if c == C - 1:
                            ins.then_inc(v2_done, 1)
                if c < C - 1:
                    ins.then_inc(piece_used, 1)
            for i in range(2 * C):
                if i == 2:
                    pe.wait_ge(v2_lo, 6)
                if 2 <= i < EG // 2 + 2:
                    mask_sums(2 * i - 4)
                    mask_sums(2 * i - 3)
                if i == EG // 2 + 2:
                    for t in range(T):
                        ins = mm(bank[t][:, t * P:(t + 1) * P], ident4[:, 0, :], ident4[:, 1, :], start=False,
                                 stop=True, skip_group_check=True)
                    ins.then_inc(mask_sum, 1)
                n = Q0 + i
                pe.wait_ge(proj_lo, n - 1)
                project(P_Q + i, bank[6 + n % 2], xnT).then_inc(proj_done, 1)

            def pair_project(m):
                n = PAIR0 + m
                pe.wait_ge(proj_lo, n if m > 1 else n - 1)
                project(P_IQK + m, pair_bank(m), (qT, kT)[m % 2]).then_inc(proj_done, 1)

            def wo_part(t, half, chunks):
                n = slice(t * P, (t + 1) * P)
                w = slice(512 * half, 512 * half + 512)
                for c in chunks:
                    if t == half == 0:
                        pe.wait_ge(lo_done, P_O + c + 1)
                    ins = mm3(bank[wo_bank(t, half)][:], outT[:, 0, c, n], outT[:, 1, c, n], hi(P_O + c)[:, w],
                              lo(P_O + c)[:, w], c == 0, c == C - 1)
                    if c == C - 1:
                        ins.then_inc(wo_done, 1)
                    elif t == T - 1 and half:
                        ins.then_inc(piece_used, 1)

            pair_project(0)
            pair_project(1)
            for h in range(HEADS + 1):
                if h == HEADS:
                    pe.wait_ge(out_lo, HEADS - 2)
                    wo_part(0, 0, range(C - 2, C - 1))
                    pe.wait_ge(sm_done, 3 * HEADS)
                    wo_part(0, 1, range(C - 1))
                if h:
                    pe.wait_ge(p_done, 3 * h)
                    for m in range(T):
                        for t in range(T):
                            ins = nc.tensor.transpose(bank[3 + m][:, t * P:(t + 1) * P],
                                                      prob[:, (h - 1) % 2, t, m * P:(m + 1) * P], ident[:])
                        ins.then_inc(pT_done, 1)
                if h < HEADS:
                    pe.wait_ge(proj_lo, PAIR0 + 2 * (h // 2) + 2)
                    r = slice(64 * (h % 2), 64 * (h % 2) + 64)
                    q, k = qk2[r, h // 2 % 2, 0], qk2[r, h // 2 % 2, 1]
                    for t in range(T):
                        n = slice(t * P, (t + 1) * P)
                        mm3(bank[t][:, 0:NODES], q[:, 0, n], q[:, 1, n], k[:, 0, :], k[:, 1, :], True,
                            True).then_inc(s_done, 1)
                if h < HEADS - 2:
                    pair_project(h + 2)
                elif h < HEADS:
                    if h == HEADS - 2:
                        pe.wait_ge(proj_lo, PAIR0 + HEADS)
                    wo_part(0, 0, range(0, C - 4) if h == HEADS - 2 else range(C - 4, C - 2))
                if h:
                    c = slice((h - 1) // 2 * P, (h - 1) // 2 * P + P)
                    if h > 1:
                        pe.wait_ge(out_lo, h - 1)
                    for m in range(T):
                        pe.wait_ge(pT_lo, 3 * (h - 1) + m + 1)
                        ins = mm3(bank[7][:, 0:NODES], v2[:, 0, m, c], v2[:, 1, m, c], probT[:, 0, m, :],
                                  probT[:, 1, m, :], m == 0, m == T - 1)
                    ins.then_inc(pv_done, 1)

            def xT2(t):
                pe.wait_ge(xn_done, T + t + 1)
                for half in range(2):
                    if t:
                        pe.wait_ge(xT_lo, 2 * T + 2 * t + half - 1)
                    xT(t, half)

            pe.wait_ge(out_lo, HEADS)
            for t in range(T):
                for half in range(2):
                    if (t, half) == (0, 0):
                        wo_part(0, 0, range(C - 1, C))
                    elif (t, half) == (0, 1):
                        wo_part(0, 1, range(C - 1, C))
                    else:
                        wo_part(t, half, range(C // 2))
                        if t and half:
                            xT2(t - 1)
                        wo_part(t, half, range(C // 2, C))
            xT2(T - 1)
            pe.wait_ge(xT_lo, 4 * T)
            pe.wait_ge(gate_lo, 1)
            for c in range(C):
                ins = mm3(bank[5][0:EXPERTS, 0:NODES], gate_r[:, 0, c, :], gate_r[:, 1, c, :], xn2T[:, 0, c, :],
                          xn2T[:, 1, c, :], c == 0, c == C - 1)
            ins.then_inc(logits_done, 1)
            def x_turn(j):
                pe.wait_ge(xg_in, 16 * j + 16)
                for half in range(2):
                    for c in range(4):
                        ins = nc.tensor.transpose(bank[4 + half][:, c * P:(c + 1) * P],
                                                  xg_raw[:, (4 * half + c) * P:(4 * half + c + 1) * P], ident[:])
                    ins.then_inc(xg_done, 1)

            def places():
                pe.wait_ge(sel_done, 1)
                NE = T * EXPERTS
                for t in range(T):
                    for s in range(t + 1):
                        mm(bank[5][:, t * EXPERTS:(t + 1) * EXPERTS], (tri if s == t else ones)[:],
                           rt[:, 1, s * EXPERTS:(s + 1) * EXPERTS], start=(s == 0), stop=(s == t))
                for s in range(T):
                    ins = mm(bank[5][:, NE:NE + EXPERTS], ones[:], rt[:, 1, s * EXPERTS:(s + 1) * EXPERTS],
                             start=(s == 0), stop=(s == T - 1))
                ins.then_inc(count_done, 1)

            for o in range(C):
                if o >= 2:
                    pe.wait_ge(silu_s, 2 * o - 2)
                for which in range(2):
                    p = P_GU + 2 * o + which
                    project(p, bank[2 * which + o % 2], xn2T).then_inc(gu_s_done, 1)
                    if p == P_GU + 3:
                        places()
                    if p == P_EXP - 2:
                        pe.wait_ge(route_done, 1)
                        x_turn(0)
                    if p == P_GU:
                        pe.wait_ge(score_done, 1)
                        for t in range(T):
                            ins = nc.tensor.transpose(bank[4][:, t * EXPERTS:(t + 1) * EXPERTS],
                                                      scoreT[:, t * P:(t + 1) * P], ident[0:EXPERTS, 0:EXPERTS])
                        ins.then_inc(score_turned, 1)

            pe.wait_ge(silu_s, 2 * C - 2)
            with pe.Fori(0, EXPERTS) as e:
                def body(j, last):
                    def turn(half):
                        pe.wait_ge(act_done, 2 * j + half + 1)
                        for c in range(2):
                            ins = nc.tensor.transpose(bank[2 + half][:, c * P:(c + 1) * P],
                                                      act_r[:, (2 * half + c) * P:(2 * half + c + 1) * P], ident[:])
                        ins.then_inc(aT_done, 1)

                    def gate_up(half, chunks):
                        for c in chunks:
                            i = 4 * half + c // 2
                            w = slice(512 * (c % 2), 512 * (c % 2) + 512)
                            if c % 2 == 0:
                                wait_piece(pe, e, i)
                            ins = mm3(bank[half][:], xgT[:, 0, c, :], xgT[:, 1, c, :], hi(P_EXP + i)[:, w],
                                      lo(P_EXP + i)[:, w], c == 0, c == C - 1)
                            if c == C - 1:
                                ins.then_inc(gu_done, 1)
                            elif last and c % 2:
                                ins.then_inc(exp_used, 1)

                    def down(i):
                        wait_piece(pe, e, C + i)
                        for o in range(2):
                            w = slice(512 * o, 512 * o + 512)
                            ins = mm3(bank[6 + o][:], actT[:, 0, i, :], actT[:, 1, i, :], hi(P_EXP + C + i)[:, w],
                                      lo(P_EXP + C + i)[:, w], i == 0, i == IC - 1)
                            if i == IC - 1:
                                ins.then_inc(y_done, 1)
                            elif last and o:
                                ins.then_inc(exp_used, 1)

                    pe.wait_ge(xg_lo, 2 * j + 2)
                    gate_up(0, range(C))
                    pe.wait_ge(silu_s, 2 * C)
                    gate_up(1, range(6))
                    turn(0)
                    gate_up(1, range(6, C))
                    pe.wait_ge(y_out, j + 1)
                    pe.wait_ge(aT_lo, 2 * j + 1)
                    down(0)
                    down(1)
                    turn(1)
                    x_turn(j + 1)
                    pe.wait_ge(aT_lo, 2 * j + 2)
                    down(2)
                    down(3)

                each_block(pe, e, body)

            blocks = pe.value_load(blk_i[0:1, 0, EXPERTS:EXPERTS + 1], min_val=1, max_val=MAX_BLOCKS)
            pe.wait_ge(xg_lo, 2 * blocks + 2)
            for t in range(T):
                for c in range(C):
                    if t == 0:
                        wait_piece(pe, EXPERTS, c)
                        pe.wait_ge(s_lo, c + 1)
                    n = slice(t * P, (t + 1) * P)
                    for half in range(2):
                        w = slice(512 * half, 512 * half + 512)
                        ins = mm3(bank[2 * t + half][:], innerT[:, 0, c, n], innerT[:, 1, c, n],
                                  hi(P_DOWN + c)[:, w], lo(P_DOWN + c)[:, w], c == 0, c == C - 1)
                        if c == C - 1:
                            ins.then_inc(down_done, 1)


def kernel(x, src, dst, edge_type_5, **w):
    import numpy as np
    import concourse.bacc as bacc
    from concourse.bass_utils import run_bass_kernel_spmd

    w = {k: np.asarray(v) for k, v in w.items()}

    def by_out(m):
        return m.reshape(C, P, C, P).transpose(0, 3, 2, 1).reshape(C, P, F)

    def by_in(m):
        return m.T.reshape(C, P, F)

    def mixed(a, b):
        return np.stack([a, b], 1).reshape(2 * C, P, F)

    wg = w["L0_ffn_Wg"].transpose(0, 2, 1).reshape(EXPERTS, C // 2, 2, P, 2, 1, 256)
    wu = w["L0_ffn_Wu"].transpose(0, 2, 1).reshape(EXPERTS, C // 2, 2, P, 2, 1, 256)
    gu = np.concatenate([wg, wu], 5).transpose(0, 4, 1, 3, 2, 5, 6).reshape(EXPERTS, C, P, F)
    wd = w["L0_ffn_Wd"].transpose(0, 2, 1).reshape(EXPERTS, IC, P, F)
    weights = np.concatenate([
        by_out(w["L0_gnn_wv"]), by_in(w["L0_gnn_wiv"]), by_out(w["L0_gnn_wq"]), by_out(w["L0_gnn_wk"]),
        mixed(by_out(w["L0_gnn_wiq"]), by_out(w["L0_gnn_wik"])), by_in(w["L0_gnn_wo"]),
        mixed(by_out(w["L0_ffn_Ws_g"]), by_out(w["L0_ffn_Ws_u"])),
        np.concatenate([gu, wd], 1).reshape(EXPERTS * PER_EXPERT, P, F), by_in(w["L0_ffn_Ws_d"])])
    biases = np.stack([w["L0_gnn_" + n].reshape(C, P).T for n in ("bq", "bk", "bv", "biq", "bik", "biv")], 1)
    src, dst, kind = (np.asarray(e) for e in (src, dst, edge_type_5))
    arrays = {
        "weights": weights,
        "x": np.asarray(x),
        "biases": biases,
        "bo": w["L0_gnn_bo"].reshape(1, F),
        "gate": w["L0_ffn_gate_w"].reshape(EXPERTS, C, P).transpose(2, 1, 0),
        "gate_bias": w["L0_ffn_gate_bias"].reshape(1, EXPERTS),
        "etw": w["L0_gnn_edge_type_weights"].reshape(1, 4),
        "edge_cols": np.stack([e.reshape(EC, P).T for e in (src, dst, kind)], 1),
        "edge_rows": np.stack([src.reshape(EG, 512), dst.reshape(EG, 512)], 1).reshape(2 * EG, 512),
    }
    arrays = {k: np.ascontiguousarray(v) for k, v in arrays.items()}
    nc = bacc.Bacc("TRN2", target_bir_lowering=False, num_devices=1)
    args = [nc.dram_tensor(k, v.shape, mybir.dt.from_np(v.dtype), kind="ExternalInput").ap() for k, v in arrays.items()]
    args.append(nc.dram_tensor("out", (NODES, F), F32, kind="ExternalOutput").ap())
    args.append(nc.dram_tensor("token_table", (P * IDX_COLS, 1), I32, kind="Internal").ap())
    args.append(nc.dram_tensor("xn2_dram", (NODES, F), F32, kind="Internal").ap())
    args.append(nc.dram_tensor("y_dram", (MAX_BLOCKS, P, F), F32, kind="Internal").ap())
    program(nc, *args)
    r = run_bass_kernel_spmd(nc, [arrays], core_ids=[0])
    return r.results[0]["out"]
```
